# Optimizing a Trainium2 kernel written in Bass

```python
import numpy as np
import jax
import jax.numpy as jnp

def _softmax(x, axis=-1):
    return jax.nn.softmax(x, axis=axis)

def _gelu(x):
    return jax.nn.gelu(x, approximate=True)

def _silu(x):
    return jax.nn.silu(x)

def _sigmoid(x):
    return jax.nn.sigmoid(x)

def _layernorm(x, axis=-1, eps=1e-05):
    m = jnp.mean(x, axis=axis, keepdims=True)
    v = jnp.var(x, axis=axis, keepdims=True)
    return (x - m) / jnp.sqrt(v + eps)

def _scatter_add(tgt, idx, src, axis=0):
    return tgt.at[idx].add(src)

def _segment_sum(src, seg, n):
    return jax.ops.segment_sum(src, seg, n)
kernel_name = 'mk_adj_resnorm_d2_adj_r2_51872e'

def setup_inputs(seed: int=0):
    np.random.seed(seed)
    _w = jnp.asarray

    def _rec_inputs():
        import jax
        import jax.numpy as jnp
        _gk = jax.random.key(seed)
        x = -0.000929 + 1 * jax.random.normal(jax.random.fold_in(_gk, 1), (8, 1024, 64), jnp.float32)
        _a = jax.random.bernoulli(jax.random.fold_in(_gk, 2), 0.00195312, (1024, 1024))
        _a = jnp.logical_or(_a, jnp.swapaxes(_a, -1, -2))
        _a = jnp.logical_or(_a, jnp.eye(1024, dtype=bool))
        _af = _a.astype(jnp.float32)
        adj = _af
        return (x, adj)
    x, adj = _rec_inputs()

    def _L0_gnn_setup():
        import jax, jax.numpy as jnp
        import numpy as np
        NEG = -1000000000.0
        key = jax.random.key(seed)
        ks = jax.random.split(key, 14)
        B, N, E, NF, NH = (8, 1024, 64, 64, 64)
        x = jax.random.normal(ks[0], (B, N, NF), dtype=jnp.float32)
        base = jax.nn.one_hot(jax.random.randint(ks[1], (N,), 0, E), E, dtype=jnp.float32)
        extra = (jax.random.uniform(ks[2], (N, E)) < 0.03).astype(jnp.float32)
        H = jnp.clip(base + extra, 0.0, 1.0)
        adj = (jax.random.uniform(ks[3], (N, N)) < 0.01).astype(jnp.float32)
        adj = jnp.clip(adj + jnp.eye(N, dtype=jnp.float32), 0.0, 1.0)
        s_in = 1.0 / np.sqrt(NF)
        s_h = 1.0 / np.sqrt(NH)
        W = jax.random.normal(ks[4], (NF, NH), dtype=jnp.float32) * s_in
        W_ind = jax.random.normal(ks[5], (NF, NH), dtype=jnp.float32) * s_in
        a_node = jax.random.normal(ks[6], (NH,), dtype=jnp.float32) * s_h
        a_gn = jax.random.normal(ks[7], (NH,), dtype=jnp.float32) * s_h
        a_ge = jax.random.normal(ks[8], (NH,), dtype=jnp.float32) * s_h
        fcW = jax.random.normal(ks[9], (NH, 2 * NH), dtype=jnp.float32) * s_h
        fcb = jnp.zeros((2 * NH,), dtype=jnp.float32)
        av = jax.random.normal(ks[10], (2 * NH,), dtype=jnp.float32) / np.sqrt(2 * NH)
        return {'x': x, 'H': H, 'adj': adj, 'nhid': NH, 'W': W, 'W_ind': W_ind, 'a_node': a_node, 'a_gn': a_gn, 'a_ge': a_ge, 'fcW': fcW, 'fcb': fcb, 'av': av}
    _L0_gnn_all = _L0_gnn_setup()
    _L0_gnn_in = {k: v for k, v in _L0_gnn_all.items() if k in ('H', 'W', 'W_ind', 'a_node', 'a_gn', 'a_ge', 'fcW', 'fcb', 'av')}
    del _L0_gnn_all

    def _L1_gnn_setup():
        import jax, jax.numpy as jnp
        import numpy as np
        NEG_INF = -1e+16

        def gat_layer(x, graph, W, b):
            h = x @ W
            s = jnp.einsum('bnd,bmd->bnm', h, h) * graph
            s = jnp.where(s == 0.0, NEG_INF, s)
            a = jax.nn.softmax(s, axis=2)
            return jnp.einsum('bnm,bmd->bnd', a, h) + b
        key = jax.random.key(seed)
        k1, k2, k3, k4, k5, k6 = jax.random.split(key, 6)
        B, N, C_IN, HID, HEADS, C_OUT = (16, 512, 64, 128, 8, 64)
        flow_x = jax.random.normal(k1, (B, N, C_IN), dtype=jnp.float32)
        graph = jax.random.randint(k2, (N, N), 0, 2).astype(jnp.float32)
        Wh = jax.random.normal(k3, (HEADS, C_IN, HID), dtype=jnp.float32)
        bh = jax.random.normal(k4, (HEADS, HID), dtype=jnp.float32)
        W_out = jax.random.normal(k5, (HID * HEADS, C_OUT), dtype=jnp.float32)
        b_out = jax.random.normal(k6, (C_OUT,), dtype=jnp.float32)
        return {'flow_x': flow_x, 'graph': graph, 'Wh': Wh, 'bh': bh, 'W_out': W_out, 'b_out': b_out}
    _L1_gnn_all = _L1_gnn_setup()
    _L1_gnn_in = {k: v for k, v in _L1_gnn_all.items() if k in ('Wh', 'bh', 'W_out', 'b_out')}
    del _L1_gnn_all
    return {'x': x, 'adj': adj, 'L0_gnn_H': _L0_gnn_in['H'], 'L0_gnn_W': _L0_gnn_in['W'], 'L0_gnn_W_ind': _L0_gnn_in['W_ind'], 'L0_gnn_a_node': _L0_gnn_in['a_node'], 'L0_gnn_a_gn': _L0_gnn_in['a_gn'], 'L0_gnn_a_ge': _L0_gnn_in['a_ge'], 'L0_gnn_fcW': _L0_gnn_in['fcW'], 'L0_gnn_fcb': _L0_gnn_in['fcb'], 'L0_gnn_av': _L0_gnn_in['av'], 'L1_gnn_Wh': _L1_gnn_in['Wh'], 'L1_gnn_bh': _L1_gnn_in['bh'], 'L1_gnn_W_out': _L1_gnn_in['W_out'], 'L1_gnn_b_out': _L1_gnn_in['b_out']}

def reference(x, adj, L0_gnn_H, L0_gnn_W, L0_gnn_W_ind, L0_gnn_a_node, L0_gnn_a_gn, L0_gnn_a_ge, L0_gnn_fcW, L0_gnn_fcb, L0_gnn_av, L1_gnn_Wh, L1_gnn_bh, L1_gnn_W_out, L1_gnn_b_out):
    import jax
    import jax.numpy as jnp

    def _L0_gnn_ref(x, H, adj, nhid, W, W_ind, a_node, a_gn, a_ge, fcW, fcb, av):
        import jax, jax.numpy as jnp
        import numpy as np
        NEG = -1000000000.0
        h = x @ W
        maskEN = H.T
        s = jax.nn.leaky_relu(h @ a_node, 0.2)
        logits = jnp.where(maskEN[None, :, :] > 0, s[:, None, :], NEG)
        alpha = jax.nn.softmax(logits, axis=-1)
        agg = jnp.einsum('ben,bnf->bef', alpha, h)
        beta = jax.nn.sigmoid((h @ a_gn)[:, None, :] + (agg @ a_ge)[:, :, None])
        all_he = beta[..., None] * h[:, None, :, :] + (1.0 - beta[..., None]) * agg[:, :, None, :]
        deg = jnp.maximum(adj.sum(-1), 1.0)[:, None]
        industry = jnp.einsum('nm,bmf->bnf', adj / deg, x @ W_ind)
        all_he = jax.nn.elu(all_he)
        he = jax.nn.elu(agg)

        def attn_scores(f):
            return jnp.tanh(f @ fcW + fcb) @ av
        se = attn_scores(he)
        logits2 = jnp.where(H[None, :, :] > 0, se[:, None, :], NEG)
        coefs1 = jax.nn.softmax(logits2, axis=-1)
        g = jnp.einsum('bne,benf->bnf', coefs1, all_he)
        pair = jnp.stack([industry, g], axis=2)
        coefs2 = jax.nn.softmax(attn_scores(pair), axis=-1)
        out = jnp.einsum('bnk,bnkf->bnf', coefs2, pair)
        return out

    def _L1_gnn_ref(flow_x, graph, Wh, bh, W_out, b_out):
        import jax, jax.numpy as jnp
        import numpy as np
        NEG_INF = -1e+16

        def gat_layer(x, graph, W, b):
            h = x @ W
            s = jnp.einsum('bnd,bmd->bnm', h, h) * graph
            s = jnp.where(s == 0.0, NEG_INF, s)
            a = jax.nn.softmax(s, axis=2)
            return jnp.einsum('bnm,bmd->bnd', a, h) + b
        heads = jax.vmap(lambda W, b: gat_layer(flow_x, graph, W, b))(Wh, bh)
        H, B, N, D = heads.shape
        cat = jnp.moveaxis(heads, 0, 2).reshape(B, N, H * D)
        x = jax.nn.leaky_relu(cat, negative_slope=0.01)
        out = gat_layer(x, graph, W_out, b_out)
        return jax.nn.leaky_relu(out, negative_slope=0.01)
    x = _layernorm(x + _L0_gnn_ref(x, L0_gnn_H, adj, 64, L0_gnn_W, L0_gnn_W_ind, L0_gnn_a_node, L0_gnn_a_gn, L0_gnn_a_ge, L0_gnn_fcW, L0_gnn_fcb, L0_gnn_av), axis=-1)
    x = _layernorm(x + _L1_gnn_ref(x, adj, L1_gnn_Wh, L1_gnn_bh, L1_gnn_W_out, L1_gnn_b_out), axis=-1)
    return x

_drawn_inputs = setup_inputs


def setup_inputs(seed=0):
    import zlib

    import numpy as np

    out = dict(_drawn_inputs(seed))
    spreads = {'L0_gnn_fcb': (0.0, 0.8)}
    factors = {'L0_gnn_a_ge': 3.797, 'L1_gnn_b_out': 7.49}
    for name, (base, spread) in spreads.items():
        noise = np.random.default_rng([zlib.crc32(name.encode()), seed]).standard_normal(out[name].shape)
        drawn = base * np.exp(spread * noise) if base else spread * noise
        out[name] = jnp.asarray(drawn.astype(out[name].dtype))
    for name, factor in factors.items():
        out[name] = (out[name] * factor).astype(out[name].dtype)
    return out
```

```python
from contextlib import ExitStack

import concourse.bass as bass
from concourse import mybir

ALU = mybir.AluOpType
ACT = mybir.ActivationFunctionType
AX = mybir.AxisListType
F32 = mybir.dt.float32
F16 = mybir.dt.float16
BF16 = mybir.dt.bfloat16

P = 128
B, N, F = 8, 1024, 64
E = 64
NT = N // P
HEADS, HID = 8, 128
HALF = 512
K2 = E // 2
OFF_EDGE = 1.0e9
OFF_GRAPH = -float(2 ** 53)
EPS = 1e-5
BIG = 3.0e38

USE_X = 0
USE_Y0 = 2
USES = 44
USE_TAIL = 39
USE_OUT = 42


def use_body(h):
    return 6 + 5 * (h - 1)


TILES = NT * (HEADS + 1)


class Net:
    pass


def setup(nc, g, s):
    with ExitStack() as ctx:
        def sb(name, shape, dt=F32):
            return ctx.enter_context(nc.sbuf_tensor(name, shape, dt))

        def sem(name):
            return ctx.enter_context(nc.semaphore(name))

        ps = ctx.enter_context(nc.psum_tensor("ps_setup", [P, 8, HALF], F32))
        adj = sb("adj_rows", [P, NT, N])
        adjT = sb("adj_cols", [P, NT, N])
        wh = sb("wh_twice", [P, HEADS, HID])
        whT = sb("wh_transposed", [P, HEADS, 2, F])
        hrow = sb("incidence", [P, NT, E])
        cols = sb("attention_columns", [F, 3])
        avc = sb("av_column", [P, 1])
        xb = sb("x_one_batch", [P, NT, F])
        xT = sb("x_transposed", [F, N])
        wind = sb("w_ind", [F, F])
        deg = sb("degree", [P, NT])
        rdeg = sb("degree_reciprocal", [P, NT])
        v = sb("x_w_ind", [P, NT, B, F])

        loaded_w, loaded_x, loaded_adj = sem("loaded_w"), sem("loaded_x"), sem("loaded_adj")
        zeroed, ident_ready = sem("zeroed"), sem("ident_ready")
        whT_psum, whT_ready, gram_psum, gram_hi = sem("whT_psum"), sem("whT_ready"), sem("gram_psum"), sem("gram_hi")
        wa_ready, stacked = sem("wa_ready"), sem("stacked")
        mask_ready, maskT_psum, maskT_ready = sem("mask_ready"), sem("maskT_psum"), sem("maskT_ready")
        deg_step = sem("deg_step")
        adjT_psum, adjT_act, adjT_dve = sem("adjT_psum"), sem("adjT_act"), sem("adjT_dve")
        xb_ready, xT_psum, xT_ready = sem("xb_ready"), sem("xT_psum"), sem("xT_ready")
        v_psum, v_ready, ind_psum, ind_ready = sem("v_psum"), sem("v_ready"), sem("ind_psum"), sem("ind_ready")

        WEIGHTS = 15
        with nc.Block() as block:
            @block.sync
            def _(sp):
                def load(dst, src, slow=False):
                    sp.dma_start(dst, src, allow_slow_non_contiguous=slow).then_inc(loaded_w, 16)
                sp.dma_start(s.X[:, :, :], g.x.rearrange("b (t p) f -> p (b t) f", p=P)).then_inc(loaded_x, 16)
                load(wh[0:F, :, :], g.Wh.rearrange("h f k -> f h k"))
                load(wh[F:P, :, :], g.Wh.rearrange("h f k -> f h k"))
                load(hrow[:, :, :], g.H.rearrange("(t p) e -> p t e", p=P))
                load(s.w2[:, 0:F], g.W)
                load(s.w2[:, F:P], g.W)
                load(wind[:, :], g.W_ind)
                for c, a in enumerate((g.a_node, g.a_gn, g.a_ge)):
                    load(cols[:, c:c + 1], a.rearrange("(f o) -> f o", o=1))
                load(s.fcw[:, :], g.fcW)
                load(s.fcb[:, :], g.fcb.rearrange("(k o) -> k o", o=1))
                load(avc[:, :], g.av.rearrange("(k o) -> k o", o=1))
                load(s.wout[:, :, :], g.W_out.rearrange("(h k) f -> k h f", k=HID))
                load(s.bh[:, :], g.bh.rearrange("h k -> k h"), slow=True)
                load(s.bout[:, :], g.b_out.rearrange("(o f) -> o f", o=1).broadcast_to([P, F]))
                for t in range(NT):
                    sp.dma_start(adj[:, t, :], g.adj[t * P:(t + 1) * P, :]).then_inc(loaded_adj, 16)

            @block.gpsimd
            def _(pool):
                nc.gpsimd.memset(s.ident[:, :], 0.0).then_inc(zeroed, 1)
                pool.wait_ge(zeroed, 1)
                nc.gpsimd.affine_select(out=s.ident[:, :], in_=s.ident[:, :], compare_op=ALU.not_equal, fill=1.0,
                                        base=0, pattern=[[-1, P]], channel_multiplier=1).then_inc(ident_ready, 1)
                nc.gpsimd.memset(s.ones[:, :], 1.0).then_inc(zeroed, 1)
                pool.wait_ge(loaded_x, 16)
                nc.gpsimd.tensor_copy(xb[:, :, :], s.X[:, 0:NT, :]).then_inc(xb_ready, 1)
                with pool.Fori(1, B) as b:
                    pool.wait_ge(xT_psum, b)
                    pool.nop(nofuse=True)
                    nc.gpsimd.tensor_copy(xb[:, :, :], s.X[:, bass.ds(b * NT, NT), :]).then_inc(xb_ready, 1)

            @block.vector
            def _(dve):
                dve.wait_ge(ident_ready, 1)
                nc.vector.tensor_copy(s.ident16[:, :], s.ident[:, :]).then_inc(stacked, 1)
                nc.vector.tensor_tensor(s.twice[:, :], s.ident[:, 0:F], s.ident[:, F:P], ALU.add).then_inc(stacked, 1)
                dve.wait_ge(stacked, 2)
                nc.vector.tensor_copy(
                    s.pick[:, :, :, :],
                    s.twice[:, :].rearrange("p (j k) -> p k j", j=2).unsqueeze(3).broadcast_to([P, K2, 2, F])).then_inc(stacked, 1)
                dve.wait_ge(loaded_w, 16 * WEIGHTS)
                nc.vector.tensor_copy(s.w_hi[:, :, :], wh[:, :, :]).then_inc(wa_ready, 1)
                dve.wait_ge(wa_ready, 1)
                nc.vector.tensor_tensor(s.w_lo[:, :, :], wh[:, :, :], s.w_hi[:, :, :], ALU.subtract).then_inc(stacked, 1)
                nc.vector.tensor_copy(s.anode[:, :], cols[:, 0:1].broadcast_to([F, E])).then_inc(stacked, 1)
                nc.vector.tensor_copy(s.agn[:, :], cols[:, 1:2].broadcast_to([F, P])).then_inc(stacked, 1)
                nc.vector.tensor_copy(s.age[:, :], cols[:, 2:3]).then_inc(stacked, 1)
                nc.vector.tensor_copy(s.av[:, :], avc[:, 0:1].broadcast_to([P, P])).then_inc(stacked, 1)
                nc.vector.tensor_scalar(s.nav[:, :], avc[:, 0:1].broadcast_to([P, F]), -1.0, None, ALU.mult).then_inc(stacked, 1)
                nc.vector.tensor_scalar(s.mask[:, :, :], hrow[:, :, :], 0.0, None, ALU.is_gt).then_inc(mask_ready, 1)
                dve.wait_ge(mask_ready, 1)
                nc.vector.tensor_scalar(s.off[:, :, :], s.mask[:, :, :], 1.0, OFF_EDGE, ALU.subtract, ALU.mult).then_inc(stacked, 1)
                dve.wait_ge(whT_psum, 1)
                nc.vector.tensor_copy(whT[:, :, :, :],
                                      ps[:, 0, :].rearrange("p (h f) -> p h f", h=HEADS).unsqueeze(2).broadcast_to([P, HEADS, 2, F])
                                      ).then_inc(whT_ready, 1)
                dve.wait_ge(maskT_psum, 1)
                nc.vector.tensor_copy(s.maskT[:, :], ps[0:E, 4:6, :].rearrange("p a n -> p (a n)")).then_inc(maskT_ready, 1)
                dve.wait_ge(maskT_ready, 1)
                nc.vector.tensor_scalar(s.offT[:, :], s.maskT[:, :], 1.0, OFF_EDGE, ALU.subtract, ALU.mult).then_inc(stacked, 1)
                dve.wait_ge(gram_psum, 1)
                gp = ps[:, 1:3, :].rearrange("p a n -> p (a n)")
                nc.vector.tensor_copy(s.gram[:, :], gp).then_inc(gram_hi, 1)
                dve.wait_ge(gram_hi, 1)
                nc.vector.tensor_tensor(s.gram[F:P, :], gp[F:P, :], s.gram[F:P, :], ALU.subtract).then_inc(gram_hi, 1)
                for t in range(NT):
                    dve.wait_ge(loaded_adj, 16 * NT)
                    nc.vector.tensor_scalar(s.offgraph[:, t, :], adj[:, t, :], 0.0, OFF_GRAPH, ALU.is_equal, ALU.mult).then_inc(stacked, 1)
                    nc.vector.tensor_reduce(deg[:, t:t + 1], adj[:, t, :], AX.X, ALU.add).then_inc(deg_step, 1)
                dve.wait_ge(deg_step, NT)
                nc.vector.tensor_scalar(deg[:, :], deg[:, :], 1.0, None, ALU.max).then_inc(deg_step, 1)
                dve.wait_ge(deg_step, NT + 1)
                nc.vector.reciprocal(rdeg[:, :], deg[:, :]).then_inc(deg_step, 1)
                for t in range(NT):
                    dve.wait_ge(adjT_psum, 2 * t + 2)
                    nc.vector.tensor_copy(adjT[:, t, HALF:N], ps[:, 2 * (t % 2) + 1, :]).then_inc(adjT_dve, 1)
                with dve.Fori(0, B) as b:
                    dve.wait_ge(v_psum, b + 1)
                    nc.vector.tensor_copy(v[:, :, bass.ds(b, 1), :],
                                          ps[:, 6, :].rearrange("p (t o f) -> p t o f", t=NT, o=1)).then_inc(v_ready, 1)
                dve.wait_ge(deg_step, NT + 2)
                for t in range(NT):
                    dve.wait_ge(ind_psum, t + 1)
                    nc.vector.tensor_scalar(s.industry[:, t, :], ps[:, t % 2, :], rdeg[:, t:t + 1], None, ALU.mult).then_inc(ind_ready, 1)

            @block.scalar
            def _(act):
                for t in range(NT):
                    act.wait_ge(adjT_psum, 2 * t + 1)
                    nc.scalar.copy(adjT[:, t, 0:HALF], ps[:, 2 * (t % 2), :]).then_inc(adjT_act, 1)
                with act.Fori(0, B) as b:
                    act.wait_ge(xT_psum, b + 1)
                    nc.scalar.copy(xT[:, :], ps[0:F, 4:6, :].rearrange("p a n -> p (a n)")).then_inc(xT_ready, 1)

            @block.tensor
            def _(pe):
                pe.wait_ge(ident_ready, 1)
                pe.wait_ge(loaded_w, 16 * WEIGHTS)
                for h in range(HEADS):
                    last = nc.tensor.transpose(ps[:, 0, h * F:(h + 1) * F], wh[0:F, h, :], s.ident[0:F, 0:F])
                last.then_inc(whT_psum, 1)
                pe.wait_ge(mask_ready, 1)
                for t in range(NT):
                    last = nc.tensor.transpose(ps[0:E, 4 + t // 4, (t % 4) * P:(t % 4 + 1) * P], s.mask[:, t, :], s.ident[:, :])
                last.then_inc(maskT_psum, 1)
                pe.wait_ge(whT_ready, 1)
                for h in range(HEADS):
                    w = whT[:, h, :, :].rearrange("p j f -> p (j f)")
                    last = nc.tensor.matmul(ps[:, 1 + h // 4, (h % 4) * P:(h % 4 + 1) * P], w, w, start=True, stop=True)
                last.then_inc(gram_psum, 1)
                pe.wait_ge(gram_hi, 2)
                pe.wait_ge(loaded_adj, 16 * NT)
                for m in range(NT):
                    if m >= 2:
                        pe.wait_ge(adjT_act, m - 1)
                        pe.wait_ge(adjT_dve, m - 1)
                    for half in range(2):
                        for q in range(4):
                            last = nc.tensor.transpose(ps[:, 2 * (m % 2) + half, q * P:(q + 1) * P],
                                                       adj[:, 4 * half + q, m * P:(m + 1) * P], s.ident[:, :])
                        last.then_inc(adjT_psum, 1)
                pe.wait_ge(maskT_ready, 1)
                with pe.Fori(0, B) as b:
                    pe.wait_ge(xb_ready, b + 1)
                    pe.nop(nofuse=True)
                    for t in range(NT):
                        last = nc.tensor.transpose(ps[0:F, 4 + t // 4, (t % 4) * P:(t % 4 + 1) * P], xb[:, t, :], s.ident[:, :])
                    last.then_inc(xT_psum, 1)
                    pe.wait_ge(xT_ready, b + 1)
                    for t in range(NT):
                        last = nc.tensor.matmul(ps[:, 6, t * F:(t + 1) * F], xT[:, t * P:(t + 1) * P], wind[:, :],
                                                start=True, stop=True)
                    last.then_inc(v_psum, 1)
                    pe.wait_ge(v_ready, b + 1)
                pe.wait_ge(adjT_act, NT)
                pe.wait_ge(adjT_dve, NT)
                for t in range(NT):
                    if t >= 2:
                        pe.wait_ge(ind_ready, t - 1)
                    for m in range(NT):
                        last = nc.tensor.matmul(ps[:, t % 2, :], adjT[:, m, t * P:(t + 1) * P],
                                                v[:, m, :, :].rearrange("p b f -> p (b f)"), start=(m == 0), stop=(m == NT - 1))
                    last.then_inc(ind_psum, 1)


def layer0(nc, s):
    with ExitStack() as ctx:
        def sb(name, shape, dt=F32):
            return ctx.enter_context(nc.sbuf_tensor(name, shape, dt))

        def sem(name):
            return ctx.enter_context(nc.semaphore(name))

        ps = ctx.enter_context(nc.psum_tensor("ps_layer0", [P, 8, HALF], F32))

        def banks(a, rows=P):
            return ps[0:rows, a:a + 2, :].rearrange("p a n -> p (a n)")

        xb, ib = sb("l0_x", [P, NT, F]), sb("l0_industry", [P, NT, F])
        xT, h2T, h2 = sb("l0_xT", [F, N]), sb("l0_hT_twice", [P, N]), sb("l0_h_twice", [P, NT, 2 * F])
        z, al, alT = sb("l0_node_score", [E, N]), sb("l0_alpha", [E, N]), sb("l0_alphaT", [P, NT, E])
        nmx, asum, arec = sb("l0_alpha_shift", [E, 1]), sb("l0_alpha_sum", [E, 1]), sb("l0_alpha_rec", [E, 1])
        agg, aggT, aggc, nagg = sb("l0_agg", [E, F]), sb("l0_aggT_twice", [F, 2, E]), sb("l0_agg_cols", [P, K2]), sb("l0_neg_agg_cols", [P, K2])
        qh = sb("l0_edge_gate", [P, 1])
        beta, bst = sb("l0_beta", [P, N]), sb("l0_beta_stack", [P, N], F16)
        r64, e64, ur, heT, thf = (sb("l0_relu", [F, E]), sb("l0_exp", [F, E]), sb("l0_u_plus_relu", [F, E]),
                                  sb("l0_heT", [F, E]), sb("l0_tanh", [P, E]))
        l2, cmx, csum, crec = sb("l0_logits", [P, NT, E]), sb("l0_c_max", [P, NT]), sb("l0_c_sum", [P, NT]), sb("l0_c_rec", [P, NT])
        cd, cT, cst = sb("l0_c_twice", [P, NT, 2, E]), sb("l0_cT", [E, N]), sb("l0_c_stack", [P, N], F16)
        cb, cob, glin = sb("l0_c_beta", [E, N]), sb("l0_c_rest", [E, N]), sb("l0_linear", [F, N])
        vb, rb, eb, ab, wb = (sb("l0_v", [P, 2, N]), sb("l0_r", [P, 2, N]), sb("l0_e", [P, 2, N]),
                              sb("l0_a", [P, 2, N]), sb("l0_w", [P, 2, N]))
        gT, iT, t1, t2, sg = sb("l0_gT", [F, N]), sb("l0_indT", [F, N]), sb("l0_tanh_ind", [P, N]), sb("l0_tanh_g", [P, N]), sb("l0_sigma", [F, N])

        names = ("xb_rdy ib_rdy xT_ps xT_rdy h_ps h2_rdy h2T_rdy s_ps z_rdy p_ps lk1 lk2 sh_rdy al_exp arec_rdy al_rdy alT_ps "
                 "alT_rdy agg_ps agg_rdy aggc_rdy nagg_rdy q_ps q_rdy th_rdy be_rdy bhi_rdy bst_rdy r_rdy e_rdy ur_rdy "
                 "he_rdy fc_ps thf_rdy se_ps l2a l2b l2m l2c l2_exp l2s l2r cd_rdy cT_ps chi_rdy cst_rdy cT_rdy cb_rdy cob_rdy "
                 "cbB_ps glin_rdy gT_rdy iT_ps iT_rdy fi_ps fg_ps t1_rdy t2_rdy d_ps sg0_rdy sg_rdy df_rdy dfs_rdy o_rdy "
                 "oT_ps x_rdy").split()
        S = {n: sem("l0_" + n) for n in names}
        gate_ps, gated, relu_rdy, exp_rdy, added, coef_ps, weighted, summed = (
            sem(n) for n in ("gate_ps", "gated", "relu_rdy", "exp_rdy", "added", "coef_ps", "weighted", "summed"))

        with nc.Block() as block:
            @block.gpsimd
            def _(pool):
                def fetch(b):
                    nc.gpsimd.tensor_copy(xb[:, :, :], s.X[:, bass.ds(b * NT, NT), :]).then_inc(S["xb_rdy"], 1)
                    nc.gpsimd.tensor_copy(ib[:, :, :], s.industry[:, :, bass.ds(b * F, F)]).then_inc(S["ib_rdy"], 1)

                def pairs(b):
                    def add(k, j, warm):
                        pool.wait_ge(exp_rdy, b * K2 + k + 1)
                        if warm:
                            pool.wait_ge(weighted, b * K2 + k - 1)
                        nc.gpsimd.tensor_tensor(ab[:, j, :], rb[:, j, :], eb[:, j, :], ALU.add).then_inc(added, 1)

                    add(0, 0, False)
                    add(1, 1, False)
                    with pool.Fori(1, K2 // 2) as pair:
                        k = 2 * pair
                        add(k, 0, True)
                        add(k + 1, 1, True)

                fetch(0)
                with pool.Fori(0, B - 1) as b:
                    pairs(b)
                    pool.wait_ge(S["x_rdy"], b + 1)
                    pool.nop(nofuse=True)
                    fetch(b + 1)
                pairs(B - 1)

            @block.scalar
            def _(act):
                with act.Fori(0, B) as b:
                    act.wait_ge(S["xT_ps"], b + 1)
                    nc.scalar.copy(xT[:, :], banks(0, F)).then_inc(S["xT_rdy"], 1)
                    act.wait_ge(S["h_ps"], b + 1)
                    nc.scalar.copy(h2T[:, :], banks(2)).then_inc(S["h2T_rdy"], 1)
                    act.wait_ge(S["s_ps"], b + 1)
                    nc.scalar.copy(z[:, :], banks(6, E)).then_inc(S["z_rdy"], 1)
                    act.wait_ge(S["sh_rdy"], b + 1)
                    nc.scalar.activation(al[:, :], al[:, :], ACT.Exp, bias=nmx[:, 0:1], scale=-1.0,
                                         accum_out=asum[:, 0:1]).then_inc(S["al_exp"], 1)
                    act.wait_ge(S["agg_rdy"], b + 1)
                    nc.scalar.activation(r64[:, :], aggT[:, 0, :], ACT.Relu, scale=-1.0).then_inc(S["r_rdy"], 1)
                    act.wait_ge(S["r_rdy"], b + 1)
                    nc.scalar.activation(e64[:, :], r64[:, :], ACT.Exp, scale=-1.0).then_inc(S["e_rdy"], 1)
                    act.wait_ge(S["q_rdy"], b + 1)
                    act.wait_ge(S["p_ps"], b + 1)
                    nc.scalar.activation(beta[:, :], banks(0), ACT.Tanh, bias=qh[:, 0:1], scale=0.5).then_inc(S["th_rdy"], 1)
                    act.wait_ge(S["fc_ps"], b + 1)
                    nc.scalar.activation(thf[:, :], ps[:, 6, 0:E], ACT.Tanh, bias=s.fcb[:, 0:1]).then_inc(S["thf_rdy"], 1)
                    act.wait_ge(S["l2c"], b + 1)
                    nc.scalar.activation(l2[:, :, :], l2[:, :, :], ACT.Exp).then_inc(S["l2_exp"], 1)
                    act.wait_ge(S["cst_rdy"], b + 1)
                    nc.scalar.copy(cT[:, :], banks(2, E)).then_inc(S["cT_rdy"], 1)

                    def relu_exp(k, j, warm):
                        act.wait_ge(gated, b * K2 + k + 1)
                        if warm:
                            act.wait_ge(added, b * K2 + k - 1)
                        act.nop(nofuse=True)
                        nc.scalar.activation(rb[:, j, :], vb[:, j, :], ACT.Relu, bias=nagg[:, bass.ds(k, 1)],
                                             scale=-1.0).then_inc(relu_rdy, 1)
                        act.wait_ge(relu_rdy, b * K2 + k + 1)
                        nc.scalar.activation(eb[:, j, :], rb[:, j, :], ACT.Exp, scale=-1.0).then_inc(exp_rdy, 1)

                    relu_exp(0, 0, False)
                    relu_exp(1, 1, False)
                    with act.Fori(1, K2 // 2) as pair:
                        k = 2 * pair
                        relu_exp(k, 0, True)
                        relu_exp(k + 1, 1, True)
                    act.wait_ge(S["iT_ps"], b + 1)
                    nc.scalar.copy(iT[:, :], banks(0, F)).then_inc(S["iT_rdy"], 1)
                    act.wait_ge(S["fi_ps"], b + 1)
                    nc.scalar.activation(t1[:, :], banks(2), ACT.Tanh, bias=s.fcb[:, 0:1]).then_inc(S["t1_rdy"], 1)
                    act.wait_ge(S["fg_ps"], b + 1)
                    nc.scalar.activation(t2[:, :], banks(4), ACT.Tanh, bias=s.fcb[:, 0:1]).then_inc(S["t2_rdy"], 1)
                    act.wait_ge(S["d_ps"], b + 1)
                    nc.scalar.activation(sg[:, :], banks(6, F), ACT.Tanh, scale=0.5).then_inc(S["sg0_rdy"], 1)

            @block.vector
            def _(dve):
                with dve.Fori(0, B) as b:
                    def step(name):
                        dve.wait_ge(S[name], b + 1)
                    step("h_ps")
                    nc.vector.tensor_copy(h2[:, :, :].rearrange("p t f -> p (t f)"), banks(4)).then_inc(S["h2_rdy"], 1)
                    step("z_rdy")
                    nc.vector.scalar_tensor_tensor(out=al[:, :], in0=z[:, :], scalar=0.2, in1=z[:, :], op0=ALU.mult,
                                                   op1=ALU.max).then_inc(S["lk1"], 1)
                    step("lk1")
                    nc.vector.tensor_tensor(z[:, :], al[:, :], s.maskT[:, :], ALU.mult).then_inc(S["lk2"], 1)
                    step("lk2")
                    dve.nop(nofuse=True)
                    nc.vector.tensor_tensor_reduce(al[:, :], z[:, :], s.offT[:, :], -1.0, BIG, ALU.add, ALU.min,
                                                   nmx[:, 0:1]).then_inc(S["sh_rdy"], 1)
                    step("al_exp")
                    nc.vector.reciprocal(arec[:, :], asum[:, :]).then_inc(S["arec_rdy"], 1)
                    step("arec_rdy")
                    nc.vector.tensor_scalar(al[:, :], al[:, :], arec[:, 0:1], None, ALU.mult).then_inc(S["al_rdy"], 1)
                    step("alT_ps")
                    nc.vector.tensor_copy(alT[:, :, :].rearrange("p t e -> p (t e)"), ps[:, 2, :]).then_inc(S["alT_rdy"], 1)
                    step("agg_ps")
                    nc.vector.tensor_copy(agg[:, :], ps[0:E, 3, 0:F])
                    nc.vector.tensor_copy(aggT[:, :, :], ps[0:F, 4, 0:E].unsqueeze(1).broadcast_to([F, 2, E])).then_inc(S["agg_rdy"], 1)
                    nc.vector.tensor_copy(aggc[0:F, :], ps[0:F, 4, 0:K2])
                    nc.vector.tensor_copy(aggc[F:P, :], ps[F:P, 4, K2:E]).then_inc(S["aggc_rdy"], 1)
                    step("aggc_rdy")
                    nc.vector.tensor_scalar(nagg[:, :], aggc[:, :], -1.0, None, ALU.mult).then_inc(S["nagg_rdy"], 1)
                    step("q_ps")
                    nc.vector.tensor_scalar(qh[:, :], ps[:, 5, 0:1], 0.5, None, ALU.mult).then_inc(S["q_rdy"], 1)
                    step("e_rdy")
                    nc.vector.tensor_tensor(ur[:, :], aggT[:, 0, :], r64[:, :], ALU.add).then_inc(S["ur_rdy"], 1)
                    step("ur_rdy")
                    nc.vector.scalar_tensor_tensor(out=heT[:, :], in0=e64[:, :], scalar=-1.0, in1=ur[:, :], op0=ALU.add,
                                                   op1=ALU.add).then_inc(S["he_rdy"], 1)
                    step("th_rdy")
                    nc.vector.tensor_scalar(beta[:, :], beta[:, :], 0.5, 0.5, ALU.mult, ALU.add).then_inc(S["be_rdy"], 1)
                    step("be_rdy")
                    nc.vector.tensor_copy(bst[:, :], beta[:, :]).then_inc(S["bhi_rdy"], 1)
                    step("bhi_rdy")
                    nc.vector.tensor_tensor(bst[F:P, :], beta[F:P, :], bst[F:P, :], ALU.subtract).then_inc(S["bst_rdy"], 1)
                    step("se_ps")
                    nc.vector.tensor_tensor(l2[:, :, :], ps[:, 7, 0:E].unsqueeze(1).broadcast_to([P, NT, E]), s.mask[:, :, :],
                                            ALU.mult).then_inc(S["l2a"], 1)
                    step("l2a")
                    nc.vector.tensor_tensor(l2[:, :, :], l2[:, :, :], s.off[:, :, :], ALU.add).then_inc(S["l2b"], 1)
                    step("l2b")
                    nc.vector.tensor_reduce(cmx[:, :], l2[:, :, :], AX.X, ALU.max).then_inc(S["l2m"], 1)
                    step("l2m")
                    nc.vector.tensor_tensor(l2[:, :, :], l2[:, :, :], cmx[:, :].unsqueeze(2).broadcast_to([P, NT, E]),
                                            ALU.subtract).then_inc(S["l2c"], 1)
                    step("l2_exp")
                    nc.vector.tensor_reduce(csum[:, :], l2[:, :, :], AX.X, ALU.add).then_inc(S["l2s"], 1)
                    step("l2s")
                    nc.vector.reciprocal(crec[:, :], csum[:, :]).then_inc(S["l2r"], 1)
                    step("l2r")
                    for j in range(2):
                        last = nc.vector.tensor_tensor(cd[:, :, j, :], l2[:, :, :], crec[:, :].unsqueeze(2).broadcast_to([P, NT, E]), ALU.mult)
                    last.then_inc(S["cd_rdy"], 1)
                    step("cT_ps")
                    nc.vector.tensor_copy(cst[:, :], banks(2)).then_inc(S["chi_rdy"], 1)
                    step("chi_rdy")
                    nc.vector.tensor_tensor(cst[F:P, :], banks(2)[F:P, :], cst[F:P, :], ALU.subtract).then_inc(S["cst_rdy"], 1)
                    step("cT_rdy")
                    nc.vector.tensor_tensor(cb[:, :], cT[:, :], beta[0:E, :], ALU.mult).then_inc(S["cb_rdy"], 1)
                    step("cb_rdy")
                    nc.vector.tensor_tensor(cob[:, :], cT[:, :], cb[:, :], ALU.subtract).then_inc(S["cob_rdy"], 1)
                    step("cbB_ps")
                    nc.vector.tensor_tensor(glin[:, :], banks(4, F), h2T[0:F, :], ALU.mult).then_inc(S["glin_rdy"], 1)

                    def gate(k, j, warm):
                        dve.wait_ge(gate_ps, b * K2 + k + 1)
                        if warm:
                            dve.wait_ge(relu_rdy, b * K2 + k - 1)
                        nc.vector.scalar_tensor_tensor(out=vb[:, j, :], in0=h2T[:, :], scalar=aggc[:, bass.ds(k, 1)],
                                                       in1=banks(2 * j), op0=ALU.subtract, op1=ALU.mult).then_inc(gated, 1)

                    def weigh(k, j, warm):
                        dve.wait_ge(coef_ps, b * K2 + k + 1)
                        dve.wait_ge(added, b * K2 + k + 1)
                        if warm:
                            dve.wait_ge(summed, b * K2 + k - 1)
                        nc.vector.tensor_tensor(wb[:, j, :], ab[:, j, :], banks(4), ALU.mult).then_inc(weighted, 1)

                    gate(0, 0, False)
                    gate(1, 1, False)
                    weigh(0, 0, False)
                    gate(2, 0, True)
                    weigh(1, 1, False)
                    gate(3, 1, True)
                    with dve.Fori(2, K2 // 2) as pair:
                        k = 2 * pair
                        for j in range(2):
                            weigh(k + j - 2, j, True)
                            gate(k + j, j, True)
                    weigh(K2 - 2, 0, True)
                    weigh(K2 - 1, 1, True)
                    dve.wait_ge(summed, (b + 1) * K2)
                    nc.vector.scalar_tensor_tensor(out=gT[:, :], in0=banks(6, F), scalar=-1.0, in1=glin[:, :], op0=ALU.add,
                                                   op1=ALU.add).then_inc(S["gT_rdy"], 1)
                    step("gT_rdy")
                    step("iT_rdy")
                    nc.vector.tensor_tensor(z[0:F, :], iT[:, :], gT[:, :], ALU.subtract).then_inc(S["df_rdy"], 1)
                    step("sg0_rdy")
                    nc.vector.tensor_scalar(sg[:, :], sg[:, :], 0.5, 0.5, ALU.mult, ALU.add).then_inc(S["sg_rdy"], 1)
                    step("sg_rdy")
                    step("df_rdy")
                    nc.vector.tensor_tensor(sg[:, :], sg[:, :], z[0:F, :], ALU.mult).then_inc(S["dfs_rdy"], 1)
                    step("dfs_rdy")
                    nc.vector.tensor_tensor(sg[:, :], sg[:, :], gT[:, :], ALU.add).then_inc(S["o_rdy"], 1)
                    step("oT_ps")
                    nc.vector.tensor_tensor(s.X[:, bass.ds(b * NT, NT), :], ps[:, 0, :].rearrange("p (t f) -> p t f", t=NT), xb[:, :, :],
                                            ALU.add).then_inc(S["x_rdy"], 1)

            @block.tensor
            def _(pe):
                with pe.Fori(0, B) as b:
                    def step(name):
                        pe.wait_ge(S[name], b + 1)

                    def wide(bank, lhsT, rhs, name, start=True, stop=True, rows=P):
                        for half in range(2):
                            last = nc.tensor.matmul(ps[0:rows, bank + half, :], lhsT, rhs[:, half * HALF:(half + 1) * HALF],
                                                    start=start, stop=stop)
                        if name is not None:
                            last.then_inc(S[name], 1)

                    step("xb_rdy")
                    pe.nop(nofuse=True)
                    for t in range(NT):
                        last = nc.tensor.transpose(ps[0:F, t // 4, (t % 4) * P:(t % 4 + 1) * P], xb[:, t, :], s.ident[:, :])
                    last.then_inc(S["xT_ps"], 1)
                    step("xT_rdy")
                    wide(2, s.w2[:, :], xT[:, :], None)
                    for t in range(NT):
                        last = nc.tensor.matmul(ps[:, 4 + t // 4, (t % 4) * P:(t % 4 + 1) * P], xT[:, t * P:(t + 1) * P], s.w2[:, :],
                                                start=True, stop=True)
                    last.then_inc(S["h_ps"], 1)
                    step("h2T_rdy")
                    pe.nop(nofuse=True)
                    wide(6, s.anode[:, :], h2T[0:F, :], "s_ps", rows=E)
                    wide(0, s.agn[:, :], h2T[0:F, :], "p_ps")
                    step("al_rdy")
                    pe.nop(nofuse=True)
                    for t in range(NT):
                        last = nc.tensor.transpose(ps[:, 2, t * E:(t + 1) * E], al[:, t * P:(t + 1) * P], s.ident[0:E, 0:E])
                    last.then_inc(S["alT_ps"], 1)
                    step("alT_rdy")
                    step("h2_rdy")
                    for t in range(NT):
                        nc.tensor.matmul(ps[0:E, 3, 0:F], alT[:, t, :], h2[:, t, 0:F], start=(t == 0), stop=(t == NT - 1))
                    for t in range(NT):
                        last = nc.tensor.matmul(ps[:, 4, 0:E], h2[:, t, :], alT[:, t, :], start=(t == 0), stop=(t == NT - 1))
                    last.then_inc(S["agg_ps"], 1)
                    step("agg_rdy")
                    nc.tensor.matmul(ps[:, 5, 0:1], aggT[:, :, :].rearrange("p j e -> p (j e)"), s.age[:, :], start=True, stop=True
                                     ).then_inc(S["q_ps"], 1)
                    step("he_rdy")
                    step("z_rdy")
                    nc.tensor.matmul(ps[:, 6, 0:E], s.fcw[:, :], heT[:, :], start=True, stop=True).then_inc(S["fc_ps"], 1)
                    step("thf_rdy")
                    nc.tensor.matmul(ps[:, 7, 0:E], s.av[:, :], thf[:, :], start=True, stop=True).then_inc(S["se_ps"], 1)
                    step("cd_rdy")
                    for t in range(NT):
                        last = nc.tensor.transpose(ps[:, 2 + t // 4, (t % 4) * P:(t % 4 + 1) * P],
                                                   cd[:, t, :, :].rearrange("p j e -> p (j e)"), s.ident[:, :])
                    last.then_inc(S["cT_ps"], 1)
                    step("cb_rdy")
                    step("nagg_rdy")
                    step("q_rdy")
                    pe.nop(nofuse=True)
                    wide(4, s.ones[0:E, 0:F], cb[:, :], "cbB_ps", rows=F)
                    step("cob_rdy")
                    pe.nop(nofuse=True)
                    wide(6, agg[:, :], cob[:, :], None, stop=False, rows=F)

                    def gates(k, j):
                        for half in range(2):
                            last = nc.tensor.matmul(ps[:, 2 * j + half, :], s.pick[:, bass.ds(k, 1), :, :].rearrange("p o j f -> p (o j f)"),
                                                    bst[:, half * HALF:(half + 1) * HALF], start=True, stop=True)
                        last.then_inc(gate_ps, 1)

                    def coefs(k):
                        for half in range(2):
                            last = nc.tensor.matmul(ps[:, 4 + half, :], s.pick[:, bass.ds(k, 1), :, :].rearrange("p o j f -> p (o j f)"),
                                                    cst[:, half * HALF:(half + 1) * HALF], start=True, stop=True)
                        last.then_inc(coef_ps, 1)

                    def total(k, j, stop=False):
                        pe.wait_ge(weighted, b * K2 + k + 1)
                        for half in range(2):
                            last = nc.tensor.matmul(ps[0:F, 6 + half, :], s.twice[:, :], wb[:, j, half * HALF:(half + 1) * HALF],
                                                    start=False, stop=stop)
                        last.then_inc(summed, 1)

                    step("bst_rdy")
                    gates(0, 0)
                    step("cT_rdy")
                    gates(1, 1)
                    step("glin_rdy")
                    coefs(0)
                    with pe.Fori(0, K2 // 2 - 1) as pair:
                        k = 2 * pair
                        for j in range(2):
                            pe.wait_ge(gated, b * K2 + k + j + 1)
                            gates(k + j + 2, j)
                            pe.wait_ge(weighted, b * K2 + k + j + 1)
                            coefs(k + j + 1)
                            total(k + j, j)
                    total(K2 - 2, 0)
                    coefs(K2 - 1)
                    total(K2 - 1, 1, stop=True)
                    step("ib_rdy")
                    pe.nop(nofuse=True)
                    for t in range(NT):
                        last = nc.tensor.transpose(ps[0:F, t // 4, (t % 4) * P:(t % 4 + 1) * P], ib[:, t, :], s.ident[:, :])
                    last.then_inc(S["iT_ps"], 1)
                    step("iT_rdy")
                    wide(2, s.fcw[:, :], iT[:, :], "fi_ps")
                    step("gT_rdy")
                    wide(4, s.fcw[:, :], gT[:, :], "fg_ps")
                    step("t1_rdy")
                    step("t2_rdy")
                    for half in range(2):
                        cols = slice(half * HALF, (half + 1) * HALF)
                        nc.tensor.matmul(ps[0:F, 6 + half, :], s.av[:, 0:F], t1[:, cols], start=True, stop=False)
                        last = nc.tensor.matmul(ps[0:F, 6 + half, :], s.nav[:, :], t2[:, cols], start=False, stop=True)
                    last.then_inc(S["d_ps"], 1)
                    step("o_rdy")
                    pe.nop(nofuse=True)
                    for t in range(NT):
                        last = nc.tensor.transpose(ps[:, 0, t * F:(t + 1) * F], sg[:, t * P:(t + 1) * P], s.ident[0:F, 0:F])
                    last.then_inc(S["oT_ps"], 1)
                    step("x_rdy")


def norm(nc, s, name, out=None):
    with ExitStack() as ctx:
        def sb(n, shape, dt=F32):
            return ctx.enter_context(nc.sbuf_tensor(f"{name}_{n}", shape, dt))

        def sem(n):
            return ctx.enter_context(nc.semaphore(f"{name}_{n}"))

        T = B * NT
        sq, mean, var, root, rec = sb("squares", [P, T, F]), sb("mean", [P, T]), sb("var", [P, T]), sb("root", [P, T]), sb("rec", [P, T])
        summed, meaned, centred, squared, square_sum, shifted, rooted, inverted, normed, stored = (
            sem(n) for n in ("summed", "meaned", "centred", "squared", "square_sum", "shifted", "rooted", "inverted", "normed", "stored"))

        def over_f(a):
            return a[:, :].unsqueeze(2).broadcast_to([P, T, F])

        with nc.Block() as block:
            @block.vector
            def _(dve):
                nc.vector.tensor_reduce(mean[:, :], s.X[:, :, :], AX.X, ALU.add).then_inc(summed, 1)
                dve.wait_ge(summed, 1)
                nc.vector.tensor_scalar(mean[:, :], mean[:, :], 1.0 / F, None, ALU.mult).then_inc(meaned, 1)
                dve.wait_ge(meaned, 1)
                nc.vector.tensor_tensor(s.X[:, :, :], s.X[:, :, :], over_f(mean), ALU.subtract).then_inc(centred, 1)
                dve.wait_ge(squared, 1)
                nc.vector.tensor_reduce(var[:, :], sq[:, :, :], AX.X, ALU.add).then_inc(square_sum, 1)
                dve.wait_ge(square_sum, 1)
                nc.vector.tensor_scalar(var[:, :], var[:, :], 1.0 / F, EPS, ALU.mult, ALU.add).then_inc(shifted, 1)
                dve.wait_ge(rooted, 1)
                nc.vector.reciprocal(rec[:, :], root[:, :]).then_inc(inverted, 1)
                dve.wait_ge(inverted, 1)
                nc.vector.tensor_tensor(s.X[:, :, :], s.X[:, :, :], over_f(rec), ALU.mult).then_inc(normed, 1)

            @block.scalar
            def _(act):
                act.wait_ge(centred, 1)
                nc.scalar.activation(sq[:, :, :], s.X[:, :, :], ACT.Square).then_inc(squared, 1)
                act.wait_ge(shifted, 1)
                nc.scalar.activation(root[:, :], var[:, :], ACT.Sqrt).then_inc(rooted, 1)

            if out is not None:
                @block.sync
                def _(sp):
                    sp.wait_ge(normed, 1)
                    sp.dma_start(out.rearrange("b (t p) f -> p (b t) f", p=P), s.X[:, :, :]).then_inc(stored, 16)
                    sp.wait_ge(stored, 16)


def layer1(nc, s):
    with ExitStack() as ctx:
        def sb(name, shape, dt=F32):
            return ctx.enter_context(nc.sbuf_tensor(name, shape, dt))

        def pb(name, shape, dt=F32):
            return ctx.enter_context(nc.psum_tensor(name, shape, dt))

        def sem(name):
            return ctx.enter_context(nc.semaphore(name))

        ps_s, ps_t, acc, misc = pb("ps_scores", [P, 2, N]), pb("ps_probsT", [P, N]), pb("ps_acc", [P, HALF]), pb("ps_misc", [P, HALF])
        misc16 = misc[:, :].bitcast(F16)
        xn = sb("l1_x", [P, NT, F])
        xs = sb("l1_x_split", [P, 2, NT, 2, F], F16)
        xh, xl = sb("l1_keys_hi", [P, N], F16), sb("l1_keys_lo", [P, N], F16)
        y = sb("l1_queries", [P, 2, N], F16)
        tb, pbuf, pt = sb("l1_scores", [P, 4, N]), sb("l1_probs", [P, 2, N]), sb("l1_probsT", [P, 2, N])
        nm, rs, rr = sb("l1_shift", [P, 4]), sb("l1_sums", [P, 2, NT]), sb("l1_rec", [P, NT])
        zf, zs, zT = sb("l1_z", [P, NT, F]), sb("l1_z_split", [P, NT, 2, F], F16), sb("l1_zT", [P, N], F16)
        cv, cat = sb("l1_head_out", [P, 2, HALF]), sb("l1_cat", [P, HEADS, N])
        ob = sb("l1_out", [P, NT, F])

        (scored, masked, exped, turned, kept_a, kept_b, mixed) = (
            sem(n) for n in ("scored", "masked", "exped", "turned", "kept_a", "kept_b", "mixed"))
        misc_full, misc_free, y_hi, cat_ready = (sem(n) for n in ("misc_full", "misc_free", "y_hi", "cat_ready"))
        xn_ready, x_hi, x_split, z_rec, z_ready, z_hi, z_split = (
            sem(n) for n in ("xn_ready", "x_hi", "x_split", "z_rec", "z_ready", "z_hi", "z_split"))
        h2_psum, y_out, o_bias, o_leak, out_added = (sem(n) for n in ("h2_psum", "y_out", "o_bias", "o_leak", "out_added"))


        with nc.Block() as block:
            @block.gpsimd
            def _(pool):
                def split_z(h, b):
                    pool.wait_ge(z_ready, 9 * b + h + 1)
                    if not (isinstance(h, int) and h == 0):
                        pool.wait_ge(cat_ready, 16 * b + 2 * h)
                    pool.nop(nofuse=True)
                    nc.gpsimd.tensor_copy(zs[:, :, 0, :], zf[:, :, :]).then_inc(z_hi, 1)
                    pool.wait_ge(z_hi, 8 * b + h + 1)
                    nc.gpsimd.tensor_tensor(zs[:, :, 1, :], zf[:, :, :], zs[:, :, 0, :], ALU.subtract).then_inc(z_split, 1)

                def heads(b):
                    split_z(0, b)
                    with pool.Fori(1, HEADS) as h:
                        split_z(h, b)

                nc.gpsimd.tensor_copy(xn[:, :, :], s.X[:, 0:NT, :]).then_inc(xn_ready, 1)
                with pool.Fori(0, B - 1) as b:
                    heads(b)
                    pool.wait_ge(out_added, b + 1)
                    pool.nop(nofuse=True)
                    nc.gpsimd.tensor_copy(xn[:, :, :], s.X[:, bass.ds((b + 1) * NT, NT), :]).then_inc(xn_ready, 1)
                heads(B - 1)

            @block.tensor
            def _(pe):
                def keys(b, use):
                    for c in range(2):
                        if use + c > 0:
                            pe.wait_ge(misc_free, USES * b + use + c)
                        for t in range(NT):
                            last = nc.tensor.transpose(misc16[:, t * P:(t + 1) * P],
                                                       xs[:, c, t, :, :].rearrange("p j f -> p (j f)"), s.ident16[:, :])
                        last.then_inc(misc_full, 1)

                def queries(b, h, half, use):
                    pe.wait_ge(misc_free, USES * b + use)
                    w = s.gram[:, bass.ds(h * P, P)]
                    cols = slice(half * HALF, (half + 1) * HALF)
                    nc.tensor.matmul(misc[:, :], w, xh[:, cols], start=True, stop=False)
                    nc.tensor.matmul(misc[:, :], w, xl[:, cols], start=False, stop=True).then_inc(misc_full, 1)

                def score(b, h, par, t):
                    for half in range(2):
                        cols = slice(half * HALF, (half + 1) * HALF)
                        q = y[:, par, t * P:(t + 1) * P]
                        nc.tensor.matmul(ps_s[:, t % 2, cols], q, xh[:, cols], start=True, stop=False)
                        last = nc.tensor.matmul(ps_s[:, t % 2, cols], q, xl[:, cols], start=False, stop=True)
                    last.then_inc(scored, 1)

                def turn(b, h, t, first):
                    i = TILES * b + NT * h + t
                    pe.wait_ge(exped, i + 1)
                    if t > 0 or not first:
                        pe.wait_ge(kept_a, i)
                        pe.wait_ge(kept_b, i)
                    for m in range(NT):
                        last = nc.tensor.transpose(ps_t[:, m * P:(m + 1) * P], pbuf[:, t % 2, m * P:(m + 1) * P], s.ident[:, :])
                    last.then_inc(turned, 1)

                def mix(b, h, t):
                    i = TILES * b + NT * h + t
                    pe.wait_ge(kept_a, i + 1)
                    pe.wait_ge(kept_b, i + 1)
                    for m in range(NT):
                        last = nc.tensor.matmul(acc[:, t * F:(t + 1) * F], pt[:, t % 2, m * P:(m + 1) * P], xn[:, m, :],
                                                start=(m == 0), stop=(m == NT - 1))
                    last.then_inc(mixed, 1)

                def turn_z(b, h, use):
                    pe.wait_ge(z_split, 8 * b + h + 1)
                    pe.wait_ge(misc_free, USES * b + use)
                    for t in range(NT):
                        last = nc.tensor.transpose(misc16[:, t * P:(t + 1) * P], zs[:, t, :, :].rearrange("p j f -> p (j f)"), s.ident16[:, :])
                    last.then_inc(misc_full, 1)

                def head_out(b, h, half, use):
                    pe.wait_ge(misc_free, USES * b + use)
                    cols = slice(half * HALF, (half + 1) * HALF)
                    for w, st in ((s.w_hi, True), (s.w_lo, False)):
                        last = nc.tensor.matmul(misc[:, :], w[:, bass.ds(h, 1), :].rearrange("p o k -> p (o k)"), zT[:, cols],
                                                start=st, stop=not st)
                    last.then_inc(misc_full, 1)

                def body(b, h, par, first, prefetch, use):
                    for t in range(NT):
                        turn(b, h, t, first)
                        if t < NT - 2 or prefetch:
                            pe.wait_ge(masked, TILES * b + NT * h + t + 1)
                            if t == NT - 2:
                                pe.wait_ge(misc_free, USES * b + use + 2)
                            score(b, h, par if t < NT - 2 else 1 - par, (t + 2) % NT)
                        if prefetch and t in (1, 2):
                            queries(b, h + 1, t - 1, use + t - 1)
                        off = 2 if prefetch else 0
                        if t > 0:
                            mix(b, h, t - 1)
                        elif not first:
                            mix(b, h - 1, NT - 1)
                        if not first and t == 3:
                            turn_z(b, h - 1, use + off)
                        if not first and t in (5, 6):
                            head_out(b, h - 1, t - 5, use + off + 1 + t - 5)
                        if t == 0 and not first:
                            pe.wait_ge(z_ready, 9 * b + h)
                with pe.Fori(0, B) as b:
                    pe.wait_ge(x_split, 2 * b + 1)
                    keys(b, USE_X)
                    pe.wait_ge(misc_free, USES * b + USE_Y0)
                    for half in range(2):
                        queries(b, 0, half, USE_Y0 + half)
                    pe.wait_ge(misc_free, USES * b + USE_Y0 + 2)
                    score(b, 0, 0, 0)
                    score(b, 0, 0, 1)
                    body(b, 0, 0, True, True, USE_Y0 + 2)
                    with pe.Fori(0, HEADS // 2 - 1) as pair:
                        h = 2 * pair + 1
                        body(b, h, 1, False, True, use_body(h))
                        body(b, h + 1, 0, False, True, use_body(h + 1))
                    body(b, HEADS - 1, 1, False, False, use_body(HEADS - 1))
                    mix(b, HEADS - 1, NT - 1)
                    turn_z(b, HEADS - 1, USE_TAIL)
                    head_out(b, HEADS - 1, 0, USE_TAIL + 1)
                    head_out(b, HEADS - 1, 1, USE_TAIL + 2)
                    pe.wait_ge(cat_ready, 16 * b + 16)
                    for t in range(NT):
                        for h in range(HEADS):
                            last = nc.tensor.matmul(acc[:, t * F:(t + 1) * F], cat[:, h, t * P:(t + 1) * P], s.wout[:, h, :],
                                                    start=(h == 0), stop=(h == HEADS - 1))
                    last.then_inc(h2_psum, 1)
                    pe.wait_ge(x_split, 2 * b + 2)
                    keys(b, USE_OUT)
                    pe.wait_ge(y_out, b + 1)
                    pe.wait_ge(misc_free, USES * b + USES)
                    score(b, HEADS, 0, 0)
                    score(b, HEADS, 0, 1)
                    body(b, HEADS, 0, True, False, 0)
                    mix(b, HEADS, NT - 1)

            @block.scalar
            def _(act):
                def expo(b, h, par, t):
                    i = TILES * b + NT * h + t
                    act.wait_ge(masked, i + 1)
                    if not (isinstance(h, int) and h == 0 and t < 2):
                        act.wait_ge(turned, i - 1)
                    nc.scalar.activation(pbuf[:, t % 2, :], tb[:, t % 4, :], ACT.Exp, bias=nm[:, t % 4:t % 4 + 1], scale=-1.0,
                                         accum_out=rs[:, par, t:t + 1]).then_inc(exped, 1)

                def keep(b, h, t):
                    i = TILES * b + NT * h + t
                    act.wait_ge(turned, i + 1)
                    if not (isinstance(h, int) and h == 0 and t < 2):
                        act.wait_ge(mixed, i - 1)
                    nc.scalar.copy(pt[:, t % 2, 0:HALF], ps_t[:, 0:HALF]).then_inc(kept_a, 1)

                def keep_keys(b, use):
                    for c, dst in enumerate((xh, xl)):
                        act.wait_ge(misc_full, USES * b + use + c + 1)
                        nc.scalar.copy(dst[:, :], misc16).then_inc(misc_free, 1)

                def queries_hi(b, half, par, use):
                    act.wait_ge(misc_full, USES * b + use + 1)
                    nc.scalar.copy(y[:, par, half * HALF:(half + 1) * HALF], misc[:, :]).then_inc(y_hi, 1)

                def keep_zT(b, use):
                    act.wait_ge(misc_full, USES * b + use + 1)
                    nc.scalar.copy(zT[:, :], misc16).then_inc(misc_free, 1)

                def bias(b, h, half, use):
                    act.wait_ge(misc_full, USES * b + use + 1)
                    act.nop(nofuse=True)
                    nc.scalar.activation(cv[:, half, :], misc[:, :], ACT.Identity, bias=s.bh[:, bass.ds(h, 1)]).then_inc(misc_free, 1)

                def body(b, h, par, first, prefetch, use):
                    off = 2 if prefetch else 0
                    for t in range(NT):
                        if t < NT - 1:
                            expo(b, h, par, t + 1)
                        elif prefetch:
                            expo(b, h + 1, 1 - par, 0)
                        keep(b, h, t)
                        if prefetch and t in (1, 2):
                            queries_hi(b, t - 1, 1 - par, use + t - 1)
                        if not first and t == 3:
                            keep_zT(b, use + off)
                        if not first and t in (5, 6):
                            bias(b, h - 1, t - 5, use + off + 1 + t - 5)
                with act.Fori(0, B) as b:
                    keep_keys(b, USE_X)
                    for half in range(2):
                        queries_hi(b, half, 0, USE_Y0 + half)
                    expo(b, 0, 0, 0)
                    body(b, 0, 0, True, True, USE_Y0 + 2)
                    with act.Fori(0, HEADS // 2 - 1) as pair:
                        h = 2 * pair + 1
                        body(b, h, 1, False, True, use_body(h))
                        body(b, h + 1, 0, False, True, use_body(h + 1))
                    body(b, HEADS - 1, 1, False, False, use_body(HEADS - 1))
                    keep_zT(b, USE_TAIL)
                    bias(b, HEADS - 1, 0, USE_TAIL + 1)
                    bias(b, HEADS - 1, 1, USE_TAIL + 2)
                    keep_keys(b, USE_OUT)
                    act.wait_ge(misc_free, USES * b + USES)
                    nc.scalar.copy(y[0:F, 0, :], xh[0:F, :])
                    nc.scalar.copy(y[F:P, 0, :], xl[F:P, :]).then_inc(y_out, 1)
                    expo(b, HEADS, 0, 0)
                    body(b, HEADS, 0, True, False, 0)

            @block.vector
            def _(dve):
                def mask(b, h, t):
                    i = TILES * b + NT * h + t
                    dve.wait_ge(scored, i + 1)
                    if not (isinstance(h, int) and h == 0 and t < 4):
                        dve.wait_ge(exped, i - 3)
                    dve.nop(nofuse=True)
                    nc.vector.tensor_tensor_reduce(tb[:, t % 4, :], ps_s[:, t % 2, :], s.offgraph[:, t, :], -1.0, BIG, ALU.add,
                                                   ALU.min, nm[:, t % 4:t % 4 + 1]).then_inc(masked, 1)

                def keep(b, h, t):
                    i = TILES * b + NT * h + t
                    dve.wait_ge(turned, i + 1)
                    if not (isinstance(h, int) and h == 0 and t < 2):
                        dve.wait_ge(mixed, i - 1)
                    nc.vector.tensor_copy(pt[:, t % 2, HALF:N], ps_t[:, HALF:N]).then_inc(kept_b, 1)

                def queries_lo(b, h, half, par):
                    dve.wait_ge(y_hi, 16 * b + 2 * h + half + 1)
                    q = y[F:P, par, half * HALF:(half + 1) * HALF]
                    nc.vector.tensor_tensor(q, misc[F:P, :], q, ALU.subtract).then_inc(misc_free, 1)

                def split_x(b, n):
                    twice = xn[:, :, :].unsqueeze(2).broadcast_to([P, NT, 2, F])
                    dve.wait_ge(xn_ready, 2 * b + n + 1)
                    nc.vector.tensor_copy(xs[:, 0, :, :, :], twice).then_inc(x_hi, 1)
                    dve.wait_ge(x_hi, 2 * b + n + 1)
                    for j in range(2):
                        last = nc.vector.tensor_tensor(xs[:, 1, :, j, :], xn[:, :, :], xs[:, 0, :, j, :], ALU.subtract)
                    last.then_inc(x_split, 1)

                def normalise(b, h, par):
                    dve.wait_ge(mixed, TILES * b + NT * h + NT)
                    nc.vector.reciprocal(rr[:, :], rs[:, par, :]).then_inc(z_rec, 1)
                    dve.wait_ge(z_rec, 9 * b + h + 1)
                    nc.vector.tensor_tensor(zf[:, :, :], acc[:, :].rearrange("p (t f) -> p t f", t=NT),
                                            rr[:, :].unsqueeze(2).broadcast_to([P, NT, F]), ALU.mult).then_inc(z_ready, 1)

                def leak(b, h, half, use):
                    dve.wait_ge(misc_free, USES * b + use + 1)
                    nc.vector.scalar_tensor_tensor(
                        out=cat[:, bass.ds(h, 1), half * HALF:(half + 1) * HALF].rearrange("p o n -> p (o n)"),
                        in0=cv[:, half, :], scalar=0.01, in1=cv[:, half, :], op0=ALU.mult, op1=ALU.max).then_inc(cat_ready, 1)

                def body(b, h, par, first, prefetch, use):
                    off = 2 if prefetch else 0
                    for t in range(NT):
                        keep(b, h, t)
                        if t < NT - 2:
                            mask(b, h, t + 2)
                        elif prefetch:
                            mask(b, h + 1, t + 2 - NT)
                        if prefetch and t in (1, 2):
                            queries_lo(b, h + 1, t - 1, 1 - par)
                        if not first and t == 0:
                            normalise(b, h - 1, 1 - par)
                        if not first and t in (5, 6):
                            leak(b, h - 1, t - 5, use + off + 1 + t - 5)
                with dve.Fori(0, B) as b:
                    split_x(b, 0)
                    for half in range(2):
                        queries_lo(b, 0, half, 0)
                    mask(b, 0, 0)
                    mask(b, 0, 1)
                    body(b, 0, 0, True, True, USE_Y0 + 2)
                    with dve.Fori(0, HEADS // 2 - 1) as pair:
                        h = 2 * pair + 1
                        body(b, h, 1, False, True, use_body(h))
                        body(b, h + 1, 0, False, True, use_body(h + 1))
                    body(b, HEADS - 1, 1, False, False, use_body(HEADS - 1))
                    normalise(b, HEADS - 1, 1)
                    leak(b, HEADS - 1, 0, USE_TAIL + 1)
                    leak(b, HEADS - 1, 1, USE_TAIL + 2)
                    dve.wait_ge(h2_psum, b + 1)
                    nc.vector.tensor_copy(xn[:, :, :], acc[:, :].rearrange("p (t f) -> p t f", t=NT)).then_inc(xn_ready, 1)
                    split_x(b, 1)
                    mask(b, HEADS, 0)
                    mask(b, HEADS, 1)
                    body(b, HEADS, 0, True, False, 0)
                    normalise(b, HEADS, 0)
                    dve.wait_ge(z_ready, 9 * b + 9)
                    nc.vector.tensor_tensor(ob[:, :, :], zf[:, :, :], s.bout[:, :].unsqueeze(1).broadcast_to([P, NT, F]), ALU.add).then_inc(o_bias, 1)
                    dve.wait_ge(o_bias, b + 1)
                    nc.vector.scalar_tensor_tensor(out=zf[:, :, :], in0=ob[:, :, :], scalar=0.01, in1=ob[:, :, :], op0=ALU.mult,
                                                   op1=ALU.max).then_inc(o_leak, 1)
                    dve.wait_ge(o_leak, b + 1)
                    rows = s.X[:, bass.ds(b * NT, NT), :]
                    nc.vector.tensor_tensor(rows, rows, zf[:, :, :], ALU.add).then_inc(out_added, 1)


def build(nc, g, out):
    with ExitStack() as ctx:
        def sb(name, shape, dt=F32):
            return ctx.enter_context(nc.sbuf_tensor(name, shape, dt))

        s = Net()
        s.X = sb("x_all", [P, B * NT, F])
        s.industry = sb("industry", [P, NT, B * F])
        s.offgraph = sb("off_graph", [P, NT, N], BF16)
        s.ident, s.ident16, s.ones = sb("ident", [P, P]), sb("ident16", [P, P], F16), sb("ones", [P, F])
        s.twice, s.pick = sb("twice", [P, F]), sb("pick_edge", [P, K2, 2, F], F16)
        s.w2, s.fcw, s.fcb = sb("w_twice", [F, P]), sb("fcw", [F, P]), sb("fcb", [P, 1])
        s.anode, s.agn, s.age = sb("a_node", [F, E]), sb("a_gn", [F, P]), sb("a_ge", [F, 1])
        s.av, s.nav = sb("av", [P, P]), sb("minus_av", [P, F])
        s.mask, s.off = sb("mask", [P, NT, E]), sb("off_edge", [P, NT, E])
        s.maskT, s.offT = sb("maskT", [E, N]), sb("off_edgeT", [E, N])
        s.w_hi, s.w_lo = sb("w_hi", [P, HEADS, HID], F16), sb("w_lo", [P, HEADS, HID], F16)
        s.gram = sb("gram", [P, HEADS * P], F16)
        s.wout, s.bh, s.bout = sb("wout", [P, HEADS, F]), sb("bh", [P, HEADS]), sb("bout", [P, F])
        setup(nc, g, s)
        layer0(nc, s)
        norm(nc, s, "norm0")
        layer1(nc, s)
        norm(nc, s, "norm1", out)


_INS = {"x": "x", "adj": "adj", "L0_gnn_H": "H", "L0_gnn_W": "W", "L0_gnn_W_ind": "W_ind", "L0_gnn_a_node": "a_node",
        "L0_gnn_a_gn": "a_gn", "L0_gnn_a_ge": "a_ge", "L0_gnn_fcW": "fcW", "L0_gnn_fcb": "fcb", "L0_gnn_av": "av",
        "L1_gnn_Wh": "Wh", "L1_gnn_bh": "bh", "L1_gnn_W_out": "W_out", "L1_gnn_b_out": "b_out"}


def kernel(**inputs):
    import numpy as _np
    import concourse.bacc as _bacc
    from concourse import mybir as _mybir
    from concourse.bass_utils import run_bass_kernel_spmd as _run

    nc = _bacc.Bacc("TRN2", target_bir_lowering=False, num_devices=1)
    arrays, g = {}, Net()
    for name, short in _INS.items():
        a = _np.ascontiguousarray(inputs[name])
        arrays[f"in_{name}"] = a
        g.__dict__[short] = nc.dram_tensor(f"in_{name}", a.shape, _mybir.dt.from_np(a.dtype), kind="ExternalInput").ap()
    out = nc.dram_tensor("out", (B, N, F), F32, kind="ExternalOutput").ap()
    build(nc, g, out)
    r = _run(nc, [arrays], core_ids=[0])
    return r.results[0]["out"]
```

```python
from contextlib import ExitStack

import concourse.bass as bass
from concourse import mybir

ALU = mybir.AluOpType
ACT = mybir.ActivationFunctionType
AX = mybir.AxisListType
F32 = mybir.dt.float32
F16 = mybir.dt.float16
BF16 = mybir.dt.bfloat16

P = 128
B, N, F = 8, 1024, 64
E = 64
NT = N // P
HEADS, HID = 8, 128
HALF = 512
K2 = E // 2
OFF_EDGE = 1.0e9
OFF_GRAPH = -float(2 ** 53)
EPS = 1e-5
BIG = 3.0e38

class Net:
    pass


def setup(nc, g, s):
    with ExitStack() as ctx:
        def sb(name, shape, dt=F32):
            return ctx.enter_context(nc.sbuf_tensor(name, shape, dt))

        def sem(name):
            return ctx.enter_context(nc.semaphore(name))

        ps = ctx.enter_context(nc.psum_tensor("ps_setup", [P, 8, HALF], F32))
        adj = sb("adj_rows", [P, NT, N])
        adjT = sb("adj_cols", [P, NT, N])
        wh = sb("wh_twice", [P, HEADS, HID])
        whT = sb("wh_transposed", [P, HEADS, 2, F])
        hrow = sb("incidence", [P, NT, E])
        cols = sb("attention_columns", [F, 3])
        avc = sb("av_column", [P, 1])
        xb = sb("x_one_batch", [P, NT, F])
        xT = sb("x_transposed", [F, N])
        wind = sb("w_ind", [F, F])
        deg = sb("degree", [P, NT])
        rdeg = sb("degree_reciprocal", [P, NT])
        v = sb("x_w_ind", [P, NT, B, F])

        loaded_w, loaded_x, loaded_adj = sem("loaded_w"), sem("loaded_x"), sem("loaded_adj")
        zeroed, ident_ready = sem("zeroed"), sem("ident_ready")
        whT_psum, whT_ready, gram_psum, gram_hi = sem("whT_psum"), sem("whT_ready"), sem("gram_psum"), sem("gram_hi")
        wa_ready, stacked = sem("wa_ready"), sem("stacked")
        mask_ready, maskT_psum, maskT_ready = sem("mask_ready"), sem("maskT_psum"), sem("maskT_ready")
        deg_step = sem("deg_step")
        adjT_psum, adjT_act, adjT_dve = sem("adjT_psum"), sem("adjT_act"), sem("adjT_dve")
        xb_ready, xT_psum, xT_ready = sem("xb_ready"), sem("xT_psum"), sem("xT_ready")
        v_psum, v_ready, ind_psum, ind_ready = sem("v_psum"), sem("v_ready"), sem("ind_psum"), sem("ind_ready")

        WEIGHTS = 15
        with nc.Block() as block:
            @block.sync
            def _(sp):
                def load(dst, src, slow=False):
                    sp.dma_start(dst, src, allow_slow_non_contiguous=slow).then_inc(loaded_w, 16)
                sp.dma_start(s.X[:, :, :], g.x.rearrange("b (t p) f -> p (b t) f", p=P)).then_inc(loaded_x, 16)
                load(wh[0:F, :, :], g.Wh.rearrange("h f k -> f h k"))
                load(wh[F:P, :, :], g.Wh.rearrange("h f k -> f h k"))
                load(hrow[:, :, :], g.H.rearrange("(t p) e -> p t e", p=P))
                load(s.w2[:, 0:F], g.W)
                load(s.w2[:, F:P], g.W)
                load(wind[:, :], g.W_ind)
                for c, a in enumerate((g.a_node, g.a_gn, g.a_ge)):
                    load(cols[:, c:c + 1], a.rearrange("(f o) -> f o", o=1))
                load(s.fcw[:, :], g.fcW)
                load(s.fcb[:, :], g.fcb.rearrange("(k o) -> k o", o=1))
                load(avc[:, :], g.av.rearrange("(k o) -> k o", o=1))
                load(s.wout[:, :, :], g.W_out.rearrange("(h k) f -> k h f", k=HID))
                load(s.bh[:, :], g.bh.rearrange("h k -> k h"), slow=True)
                load(s.bout[:, :], g.b_out.rearrange("(o f) -> o f", o=1).broadcast_to([P, F]))
                for t in range(NT):
                    sp.dma_start(adj[:, t, :], g.adj[t * P:(t + 1) * P, :]).then_inc(loaded_adj, 16)

            @block.gpsimd
            def _(pool):
                nc.gpsimd.memset(s.ident[:, :], 0.0).then_inc(zeroed, 1)
                pool.wait_ge(zeroed, 1)
                nc.gpsimd.affine_select(out=s.ident[:, :], in_=s.ident[:, :], compare_op=ALU.not_equal, fill=1.0,
                                        base=0, pattern=[[-1, P]], channel_multiplier=1).then_inc(ident_ready, 1)
                nc.gpsimd.memset(s.ones[:, :], 1.0).then_inc(zeroed, 1)
                pool.wait_ge(loaded_x, 16)
                nc.gpsimd.tensor_copy(xb[:, :, :], s.X[:, 0:NT, :]).then_inc(xb_ready, 1)
                with pool.Fori(1, B) as b:
                    pool.wait_ge(xT_psum, b)
                    pool.nop(nofuse=True)
                    nc.gpsimd.tensor_copy(xb[:, :, :], s.X[:, bass.ds(b * NT, NT), :]).then_inc(xb_ready, 1)

            @block.vector
            def _(dve):
                dve.wait_ge(ident_ready, 1)
                nc.vector.tensor_copy(s.ident16[:, :], s.ident[:, :]).then_inc(stacked, 1)
                nc.vector.tensor_tensor(s.twice[:, :], s.ident[:, 0:F], s.ident[:, F:P], ALU.add).then_inc(stacked, 1)
                dve.wait_ge(stacked, 2)
                nc.vector.tensor_copy(
                    s.pick[:, :, :, :],
                    s.twice[:, :].rearrange("p (j k) -> p k j", j=2).unsqueeze(3).broadcast_to([P, K2, 2, F])).then_inc(stacked, 1)
                dve.wait_ge(loaded_w, 16 * WEIGHTS)
                nc.vector.tensor_copy(s.w_hi[:, :, :], wh[:, :, :]).then_inc(wa_ready, 1)
                dve.wait_ge(wa_ready, 1)
                nc.vector.tensor_tensor(s.w_lo[:, :, :], wh[:, :, :], s.w_hi[:, :, :], ALU.subtract).then_inc(stacked, 1)
                nc.vector.tensor_copy(s.anode[:, :], cols[:, 0:1].broadcast_to([F, E])).then_inc(stacked, 1)
                nc.vector.tensor_copy(s.agn[:, :], cols[:, 1:2].broadcast_to([F, P])).then_inc(stacked, 1)
                nc.vector.tensor_copy(s.age[:, :], cols[:, 2:3]).then_inc(stacked, 1)
                nc.vector.tensor_copy(s.av[:, :], avc[:, 0:1].broadcast_to([P, P])).then_inc(stacked, 1)
                nc.vector.tensor_scalar(s.nav[:, :], avc[:, 0:1].broadcast_to([P, F]), -1.0, None, ALU.mult).then_inc(stacked, 1)
                nc.vector.tensor_scalar(s.mask[:, :, :], hrow[:, :, :], 0.0, None, ALU.is_gt).then_inc(mask_ready, 1)
                dve.wait_ge(mask_ready, 1)
                nc.vector.tensor_scalar(s.off[:, :, :], s.mask[:, :, :], 1.0, OFF_EDGE, ALU.subtract, ALU.mult).then_inc(stacked, 1)
                dve.wait_ge(whT_psum, 1)
                nc.vector.tensor_copy(whT[:, :, :, :],
                                      ps[:, 0, :].rearrange("p (h f) -> p h f", h=HEADS).unsqueeze(2).broadcast_to([P, HEADS, 2, F])
                                      ).then_inc(whT_ready, 1)
                dve.wait_ge(maskT_psum, 1)
                nc.vector.tensor_copy(s.maskT[:, :], ps[0:E, 4:6, :].rearrange("p a n -> p (a n)")).then_inc(maskT_ready, 1)
                dve.wait_ge(maskT_ready, 1)
                nc.vector.tensor_scalar(s.offT[:, :], s.maskT[:, :], 1.0, OFF_EDGE, ALU.subtract, ALU.mult).then_inc(stacked, 1)
                dve.wait_ge(gram_psum, 1)
                gp = ps[:, 1:3, :].rearrange("p a n -> p (a n)")
                nc.vector.tensor_copy(s.gram[:, :], gp).then_inc(gram_hi, 1)
                dve.wait_ge(gram_hi, 1)
                nc.vector.tensor_tensor(s.gram[F:P, :], gp[F:P, :], s.gram[F:P, :], ALU.subtract).then_inc(gram_hi, 1)
                for t in range(NT):
                    dve.wait_ge(loaded_adj, 16 * NT)
                    nc.vector.tensor_scalar(s.offgraph[:, t, :], adj[:, t, :], 0.0, OFF_GRAPH, ALU.is_equal, ALU.mult).then_inc(stacked, 1)
                    nc.vector.tensor_reduce(deg[:, t:t + 1], adj[:, t, :], AX.X, ALU.add).then_inc(deg_step, 1)
                dve.wait_ge(deg_step, NT)
                nc.vector.tensor_scalar(deg[:, :], deg[:, :], 1.0, None, ALU.max).then_inc(deg_step, 1)
                dve.wait_ge(deg_step, NT + 1)
                nc.vector.reciprocal(rdeg[:, :], deg[:, :]).then_inc(deg_step, 1)
                for t in range(NT):
                    dve.wait_ge(adjT_psum, 2 * t + 2)
                    nc.vector.tensor_copy(adjT[:, t, HALF:N], ps[:, 2 * (t % 2) + 1, :]).then_inc(adjT_dve, 1)
                with dve.Fori(0, B) as b:
                    dve.wait_ge(v_psum, b + 1)
                    nc.vector.tensor_copy(v[:, :, bass.ds(b, 1), :],
                                          ps[:, 6, :].rearrange("p (t o f) -> p t o f", t=NT, o=1)).then_inc(v_ready, 1)
                dve.wait_ge(deg_step, NT + 2)
                for t in range(NT):
                    dve.wait_ge(ind_psum, t + 1)
                    nc.vector.tensor_scalar(s.industry[:, t, :], ps[:, t % 2, :], rdeg[:, t:t + 1], None, ALU.mult).then_inc(ind_ready, 1)

            @block.scalar
            def _(act):
                for t in range(NT):
                    act.wait_ge(adjT_psum, 2 * t + 1)
                    nc.scalar.copy(adjT[:, t, 0:HALF], ps[:, 2 * (t % 2), :]).then_inc(adjT_act, 1)
                with act.Fori(0, B) as b:
                    act.wait_ge(xT_psum, b + 1)
                    nc.scalar.copy(xT[:, :], ps[0:F, 4:6, :].rearrange("p a n -> p (a n)")).then_inc(xT_ready, 1)

            @block.tensor
            def _(pe):
                pe.wait_ge(ident_ready, 1)
                pe.wait_ge(loaded_w, 16 * WEIGHTS)
                for h in range(HEADS):
                    last = nc.tensor.transpose(ps[:, 0, h * F:(h + 1) * F], wh[0:F, h, :], s.ident[0:F, 0:F])
                last.then_inc(whT_psum, 1)
                pe.wait_ge(mask_ready, 1)
                for t in range(NT):
                    last = nc.tensor.transpose(ps[0:E, 4 + t // 4, (t % 4) * P:(t % 4 + 1) * P], s.mask[:, t, :], s.ident[:, :])
                last.then_inc(maskT_psum, 1)
                pe.wait_ge(whT_ready, 1)
                for h in range(HEADS):
                    w = whT[:, h, :, :].rearrange("p j f -> p (j f)")
                    last = nc.tensor.matmul(ps[:, 1 + h // 4, (h % 4) * P:(h % 4 + 1) * P], w, w, start=True, stop=True)
                last.then_inc(gram_psum, 1)
                pe.wait_ge(gram_hi, 2)
                pe.wait_ge(loaded_adj, 16 * NT)
                for m in range(NT):
                    if m >= 2:
                        pe.wait_ge(adjT_act, m - 1)
                        pe.wait_ge(adjT_dve, m - 1)
                    for half in range(2):
                        for q in range(4):
                            last = nc.tensor.transpose(ps[:, 2 * (m % 2) + half, q * P:(q + 1) * P],
                                                       adj[:, 4 * half + q, m * P:(m + 1) * P], s.ident[:, :])
                        last.then_inc(adjT_psum, 1)
                pe.wait_ge(maskT_ready, 1)
                with pe.Fori(0, B) as b:
                    pe.wait_ge(xb_ready, b + 1)
                    pe.nop(nofuse=True)
                    for t in range(NT):
                        last = nc.tensor.transpose(ps[0:F, 4 + t // 4, (t % 4) * P:(t % 4 + 1) * P], xb[:, t, :], s.ident[:, :])
                    last.then_inc(xT_psum, 1)
                    pe.wait_ge(xT_ready, b + 1)
                    for t in range(NT):
                        last = nc.tensor.matmul(ps[:, 6, t * F:(t + 1) * F], xT[:, t * P:(t + 1) * P], wind[:, :],
                                                start=True, stop=True)
                    last.then_inc(v_psum, 1)
                    pe.wait_ge(v_ready, b + 1)
                pe.wait_ge(adjT_act, NT)
                pe.wait_ge(adjT_dve, NT)
                for t in range(NT):
                    if t >= 2:
                        pe.wait_ge(ind_ready, t - 1)
                    for m in range(NT):
                        last = nc.tensor.matmul(ps[:, t % 2, :], adjT[:, m, t * P:(t + 1) * P],
                                                v[:, m, :, :].rearrange("p b f -> p (b f)"), start=(m == 0), stop=(m == NT - 1))
                    last.then_inc(ind_psum, 1)


def layer0(nc, s):
    with ExitStack() as ctx:
        def sb(name, shape, dt=F32):
            return ctx.enter_context(nc.sbuf_tensor(name, shape, dt))

        def sem(name):
            return ctx.enter_context(nc.semaphore(name))

        ps = ctx.enter_context(nc.psum_tensor("ps_layer0", [P, 8, HALF], F32))

        def banks(a, rows=P):
            return ps[0:rows, a:a + 2, :].rearrange("p a n -> p (a n)")

        GATES, COEFS, SUMS, MISC = 0, 2, 4, 6
        BUFS = 4
        LAG_W, LAG_SUM = 3, 4

        h2T, bst, cst = sb("l0_hT_twice", [P, 2, N]), sb("l0_beta_stack", [P, 2, N], F16), sb("l0_c_stack", [P, 2, N], F16)
        aggc, nagg, glin = sb("l0_agg_cols", [P, 2, K2]), sb("l0_neg_agg_cols", [P, 2, K2]), sb("l0_linear", [F, 2, N])
        vb, rb = sb("l0_v_exp", [P, BUFS, N]), sb("l0_relu_w", [P, BUFS, N])
        xb, xT, h2 = sb("l0_x", [P, NT, F]), sb("l0_xT", [F, N]), sb("l0_h_twice", [P, NT, 2 * F])
        z, al, alT = sb("l0_node_score", [E, N]), sb("l0_alpha", [E, N]), sb("l0_alphaT", [P, NT, E])
        nmx, asum, arec = sb("l0_alpha_shift", [E, 1]), sb("l0_alpha_sum", [E, 1]), sb("l0_alpha_rec", [E, 1])
        agg, aggT, qh = sb("l0_agg", [E, F]), sb("l0_aggT_twice", [F, 2, E]), sb("l0_edge_gate", [P, 1])
        beta = sb("l0_beta", [P, N])
        r64, e64, ur, heT, thf = (sb("l0_relu", [F, E]), sb("l0_exp", [F, E]), sb("l0_u_plus_relu", [F, E]),
                                  sb("l0_heT", [F, E]), sb("l0_tanh", [P, E]))
        l2, cmx, csum, crec = sb("l0_logits", [P, NT, E]), sb("l0_c_max", [P, NT]), sb("l0_c_sum", [P, NT]), sb("l0_c_rec", [P, NT])
        cd, cT, cob = sb("l0_c_twice", [P, NT, 2, E]), sb("l0_cT_twice", [P, N]), sb("l0_c_rest", [E, N])
        cb = z
        ib, gT, iT = sb("l0_industry", [P, NT, F]), sb("l0_gT", [F, N]), sb("l0_indT", [F, N])
        t1, t2, sg = sb("l0_tanh_ind", [P, N]), sb("l0_tanh_g", [P, N]), sb("l0_sigma", [F, N])

        gate_ps, gated, relu_rdy, exp_rdy, added, coef_ps, weighted, summed = (
            sem(n) for n in ("gate_ps", "gated", "relu_rdy", "exp_rdy", "added", "coef_ps", "weighted", "summed"))
        names = ("xb_rdy ib_rdy leaked masked sh_rdy al_exp arec_rdy al_rdy aggc_rdy r_rdy e_rdy ur_rdy he_rdy "
                 "be_rdy bhi_rdy bst_rdy l2b l2m l2c l2_exp l2s l2r cd_rdy chi_rdy cst_rdy cb_rdy cob_rdy "
                 "gT_rdy df_rdy sg_rdy dfs_rdy o_rdy").split()
        S = {n: sem("l0_" + n) for n in names}
        misc_full, misc_free = sem("l0_misc_full"), sem("l0_misc_free")
        PREP = "xT h2T s h2 alT agg q fc se p cT cbB".split()
        TAIL = "ind fi fg d oT".split()
        BOTH = "ind xT h2T s h2 fi alT agg q fc se p fg cT d cbB oT".split()

        class Phase:

            def __init__(self, b, par, base, run=True, prev=True, prep=True, tail=True):
                self.b, self.par, self.base, self.run, self.prev, self.prep, self.tail = b, par, base, run, prev, prep, tail
                order = BOTH if prep and tail else PREP if prep else TAIL
                self.use = {name: base + i for i, name in enumerate(order)}

            def lagging(self, k, lag):
                if k >= lag:
                    return (k - lag, K2 * self.b + k - lag, self.par) if self.run else None
                return (k - lag + K2, K2 * self.b + k - lag, 1 - self.par) if self.prev else None

            def reused(self, k):
                return self.prev or k >= BUFS

        def in_order(eng, slot):
            def phase(ph):
                for k in range(K2):
                    slot(ph, k)

            def base(b):
                return (len(PREP) - len(TAIL)) + len(BOTH) * b

            phase(Phase(-1, 1, 0, run=False, prev=False, tail=False))
            phase(Phase(0, 0, len(PREP), prev=False, tail=False))
            with eng.Fori(0, B // 2 - 1) as two:
                phase(Phase(2 * two + 1, 1, len(BOTH) * 2 * two + base(1)))
                phase(Phase(2 * two + 2, 0, len(BOTH) * 2 * two + base(2)))
            phase(Phase(B - 1, 1, base(B - 1), prep=False))
            phase(Phase(B, 0, base(B - 1) + len(TAIL), run=False, prep=False))

        with nc.Block() as block:
            @block.sync
            def _(sp):
                def fetch_x(n):
                    sp.dma_start(xb[:, :, :], s.X[:, bass.ds(n * NT, NT), :]).then_inc(S["xb_rdy"], 16)

                def slot(ph, k):
                    if ph.prep and k == 0:
                        if ph.run:
                            sp.wait_ge(misc_full, ph.base)
                        fetch_x(ph.b + 1)
                    if ph.run and k == 12:
                        if ph.tail:
                            sp.wait_ge(misc_full, ph.use["ind"] + 1)
                        sp.dma_start(ib[:, :, :], s.industry[:, :, bass.ds(ph.b * F, F)]).then_inc(S["ib_rdy"], 16)

                in_order(sp, slot)

            @block.gpsimd
            def _(pool):
                def slot(ph, k):
                    i = K2 * ph.b + k
                    if ph.run:
                        pool.wait_ge(exp_rdy, i + 1)
                        nc.gpsimd.tensor_tensor(rb[:, k % BUFS, :], rb[:, k % BUFS, :], vb[:, k % BUFS, :], ALU.add).then_inc(added, 1)

                in_order(pool, slot)

            @block.scalar
            def _(act):
                def slot(ph, k):
                    b, use, i = ph.b, ph.use, K2 * ph.b + k
                    if ph.run:
                        v, r = vb[:, k % BUFS, :], rb[:, k % BUFS, :]
                        act.wait_ge(gated, i + 1)
                        if ph.reused(k):
                            act.wait_ge(summed, i - BUFS + 1)
                        nc.scalar.activation(r, v, ACT.Relu, bias=nagg[:, ph.par, k:k + 1], scale=-1.0).then_inc(relu_rdy, 1)
                        act.wait_ge(relu_rdy, i + 1)
                        nc.scalar.activation(v, r, ACT.Exp, scale=-1.0).then_inc(exp_rdy, 1)

                    def full(name):
                        act.wait_ge(misc_full, use[name] + 1)

                    if ph.tail:
                        if k == 0:
                            full("ind")
                            nc.scalar.copy(iT[:, :], banks(MISC, F)).then_inc(misc_free, 1)
                        if k == 10:
                            full("fi")
                            nc.scalar.activation(t1[:, :], banks(MISC), ACT.Tanh, bias=s.fcb[:, 0:1]).then_inc(misc_free, 1)
                        if k == 22:
                            full("fg")
                            nc.scalar.activation(t2[:, :], banks(MISC), ACT.Tanh, bias=s.fcb[:, 0:1]).then_inc(misc_free, 1)
                        if k == 26:
                            full("d")
                            nc.scalar.activation(sg[:, :], banks(MISC, F), ACT.Tanh, scale=0.5).then_inc(misc_free, 1)
                    if ph.prep:
                        if k == 2:
                            full("xT")
                            nc.scalar.copy(xT[:, :], banks(MISC, F)).then_inc(misc_free, 1)
                        if k == 4:
                            full("h2T")
                            nc.scalar.copy(h2T[:, 1 - ph.par, :], banks(MISC)).then_inc(misc_free, 1)
                        if k == 6:
                            full("s")
                            nc.scalar.copy(z[:, :], banks(MISC, E)).then_inc(misc_free, 1)
                        if k == 8:
                            full("h2")
                            nc.scalar.copy(h2[:, :, :].rearrange("p t f -> p (t f)"), banks(MISC)).then_inc(misc_free, 1)
                            act.wait_ge(S["sh_rdy"], b + 2)
                            nc.scalar.activation(al[:, :], al[:, :], ACT.Exp, bias=nmx[:, 0:1], scale=-1.0,
                                                 accum_out=asum[:, 0:1]).then_inc(S["al_exp"], 1)
                        if k == 14:
                            act.wait_ge(misc_free, use["agg"] + 1)
                            nc.scalar.activation(r64[:, :], aggT[:, 0, :], ACT.Relu, scale=-1.0).then_inc(S["r_rdy"], 1)
                            act.wait_ge(S["r_rdy"], b + 2)
                            nc.scalar.activation(e64[:, :], r64[:, :], ACT.Exp, scale=-1.0).then_inc(S["e_rdy"], 1)
                        if k == 16:
                            full("fc")
                            nc.scalar.activation(thf[:, :], ps[:, MISC, 0:E], ACT.Tanh, bias=s.fcb[:, 0:1]).then_inc(misc_free, 1)
                        if k == 20:
                            full("p")
                            nc.scalar.activation(beta[:, :], banks(MISC), ACT.Tanh, bias=qh[:, 0:1], scale=0.5).then_inc(misc_free, 1)
                            act.wait_ge(S["l2c"], b + 2)
                            nc.scalar.activation(l2[:, :, :], l2[:, :, :], ACT.Exp).then_inc(S["l2_exp"], 1)
                        if k == 24:
                            full("cT")
                            nc.scalar.copy(cT[:, :], banks(MISC)).then_inc(misc_free, 1)

                in_order(act, slot)

            @block.vector
            def _(dve):
                def slot(ph, k):
                    b, use, i = ph.b, ph.use, K2 * ph.b + k
                    if ph.run:
                        dve.wait_ge(gate_ps, i + 1)
                        if ph.reused(k):
                            dve.wait_ge(added, i - BUFS + 1)
                        nc.vector.scalar_tensor_tensor(out=vb[:, k % BUFS, :], in0=h2T[:, ph.par, :], scalar=aggc[:, ph.par, k:k + 1],
                                                       in1=banks(GATES), op0=ALU.subtract, op1=ALU.mult).then_inc(gated, 1)
                    late = ph.lagging(k, LAG_W)
                    if late:
                        j, i_late, _ = late
                        dve.wait_ge(coef_ps, i_late + 1)
                        dve.wait_ge(added, i_late + 1)
                        nc.vector.tensor_tensor(rb[:, j % BUFS, :], rb[:, j % BUFS, :], banks(COEFS), ALU.mult).then_inc(weighted, 1)
                    if ph.prev and k == LAG_SUM - 1:
                        dve.wait_ge(summed, K2 * b)
                        nc.vector.scalar_tensor_tensor(out=gT[:, :], in0=banks(SUMS, F), scalar=-1.0, in1=glin[:, 1 - ph.par, :],
                                                       op0=ALU.add, op1=ALU.add).then_inc(S["gT_rdy"], 1)
                    if ph.tail:
                        finish(ph, k)
                    if ph.prep:
                        prepare(ph, k)

                def finish(ph, k):
                    b, use = ph.b, ph.use
                    if k == 28:
                        dve.wait_ge(misc_free, use["d"] + 1)
                        nc.vector.tensor_tensor(iT[:, :], iT[:, :], gT[:, :], ALU.subtract).then_inc(S["df_rdy"], 1)
                        nc.vector.tensor_scalar(sg[:, :], sg[:, :], 0.5, 0.5, ALU.mult, ALU.add).then_inc(S["sg_rdy"], 1)
                    if k == 29:
                        dve.wait_ge(S["df_rdy"], b)
                        dve.wait_ge(S["sg_rdy"], b)
                        nc.vector.tensor_tensor(sg[:, :], sg[:, :], iT[:, :], ALU.mult).then_inc(S["dfs_rdy"], 1)
                        dve.wait_ge(S["dfs_rdy"], b)
                        nc.vector.tensor_tensor(sg[:, :], sg[:, :], gT[:, :], ALU.add).then_inc(S["o_rdy"], 1)
                    if k == 31:
                        dve.wait_ge(misc_full, use["oT"] + 1)
                        rows = s.X[:, bass.ds((b - 1) * NT, NT), :]
                        nc.vector.tensor_tensor(rows, ps[:, MISC, :].rearrange("p (t f) -> p t f", t=NT), rows, ALU.add).then_inc(misc_free, 1)

                def prepare(ph, k):
                    b, use, nxt = ph.b, ph.use, 1 - ph.par

                    def step(name):
                        dve.wait_ge(S[name], b + 2)

                    def full(name):
                        dve.wait_ge(misc_full, use[name] + 1)

                    if k == 7:
                        dve.wait_ge(misc_free, use["s"] + 1)
                        nc.vector.scalar_tensor_tensor(out=al[:, :], in0=z[:, :], scalar=0.2, in1=z[:, :], op0=ALU.mult,
                                                       op1=ALU.max).then_inc(S["leaked"], 1)
                        step("leaked")
                        nc.vector.tensor_tensor(z[:, :], al[:, :], s.maskT[:, :], ALU.mult).then_inc(S["masked"], 1)
                    if k == 8:
                        step("masked")
                        dve.nop(nofuse=True)
                        nc.vector.tensor_tensor_reduce(al[:, :], z[:, :], s.offT[:, :], -1.0, BIG, ALU.add, ALU.min,
                                                       nmx[:, 0:1]).then_inc(S["sh_rdy"], 1)
                    if k == 10:
                        step("al_exp")
                        nc.vector.reciprocal(arec[:, :], asum[:, :]).then_inc(S["arec_rdy"], 1)
                        step("arec_rdy")
                        nc.vector.tensor_scalar(al[:, :], al[:, :], arec[:, 0:1], None, ALU.mult).then_inc(S["al_rdy"], 1)
                    if k == 11:
                        full("alT")
                        nc.vector.tensor_copy(alT[:, :, :].rearrange("p t e -> p (t e)"), ps[:, MISC, :]).then_inc(misc_free, 1)
                    if k == 13:
                        full("agg")
                        nc.vector.tensor_copy(agg[:, :], ps[0:E, MISC, 0:F])
                        nc.vector.tensor_copy(aggc[0:F, nxt, :], ps[0:F, MISC + 1, 0:K2])
                        nc.vector.tensor_copy(aggc[F:P, nxt, :], ps[F:P, MISC + 1, K2:E]).then_inc(S["aggc_rdy"], 1)
                        nc.vector.tensor_copy(aggT[:, :, :], ps[0:F, MISC + 1, 0:E].unsqueeze(1).broadcast_to([F, 2, E])).then_inc(misc_free, 1)
                        step("aggc_rdy")
                        nc.vector.tensor_scalar(nagg[:, nxt, :], aggc[:, nxt, :], -1.0, None, ALU.mult)
                    if k == 15:
                        full("q")
                        nc.vector.tensor_scalar(qh[:, :], ps[:, MISC, 0:1], 0.5, None, ALU.mult).then_inc(misc_free, 1)
                        step("e_rdy")
                        nc.vector.tensor_tensor(ur[:, :], aggT[:, 0, :], r64[:, :], ALU.add).then_inc(S["ur_rdy"], 1)
                        step("ur_rdy")
                        nc.vector.scalar_tensor_tensor(out=heT[:, :], in0=e64[:, :], scalar=-1.0, in1=ur[:, :], op0=ALU.add,
                                                       op1=ALU.add).then_inc(S["he_rdy"], 1)
                    if k == 18:
                        full("se")
                        nc.vector.tensor_tensor(l2[:, :, :], ps[:, MISC, 0:E].unsqueeze(1).broadcast_to([P, NT, E]), s.mask[:, :, :],
                                                ALU.mult).then_inc(misc_free, 1)
                        dve.wait_ge(misc_free, use["se"] + 1)
                        nc.vector.tensor_tensor(l2[:, :, :], l2[:, :, :], s.off[:, :, :], ALU.add).then_inc(S["l2b"], 1)
                    if k == 19:
                        step("l2b")
                        nc.vector.tensor_reduce(cmx[:, :], l2[:, :, :], AX.X, ALU.max).then_inc(S["l2m"], 1)
                        step("l2m")
                        nc.vector.tensor_tensor(l2[:, :, :], l2[:, :, :], cmx[:, :].unsqueeze(2).broadcast_to([P, NT, E]),
                                                ALU.subtract).then_inc(S["l2c"], 1)
                    if k == 21:
                        dve.wait_ge(misc_free, use["p"] + 1)
                        nc.vector.tensor_scalar(beta[:, :], beta[:, :], 0.5, 0.5, ALU.mult, ALU.add).then_inc(S["be_rdy"], 1)
                        step("be_rdy")
                        nc.vector.tensor_copy(bst[:, nxt, :], beta[:, :]).then_inc(S["bhi_rdy"], 1)
                    if k == 22:
                        step("l2_exp")
                        nc.vector.tensor_reduce(csum[:, :], l2[:, :, :], AX.X, ALU.add).then_inc(S["l2s"], 1)
                        step("l2s")
                        nc.vector.reciprocal(crec[:, :], csum[:, :]).then_inc(S["l2r"], 1)
                        step("l2r")
                        nc.vector.tensor_tensor(cd[:, :, 0, :], l2[:, :, :], crec[:, :].unsqueeze(2).broadcast_to([P, NT, E]), ALU.mult)
                    if k == 23:
                        nc.vector.tensor_tensor(cd[:, :, 1, :], l2[:, :, :], crec[:, :].unsqueeze(2).broadcast_to([P, NT, E]),
                                                ALU.mult).then_inc(S["cd_rdy"], 1)
                    if k == 24:
                        step("bhi_rdy")
                        nc.vector.tensor_tensor(bst[F:P, nxt, :], beta[F:P, :], bst[F:P, nxt, :], ALU.subtract).then_inc(S["bst_rdy"], 1)
                    if k == 25:
                        dve.wait_ge(misc_free, use["cT"] + 1)
                        nc.vector.tensor_tensor(cb[:, :], cT[0:E, :], beta[0:E, :], ALU.mult).then_inc(S["cb_rdy"], 1)
                        nc.vector.tensor_copy(cst[:, nxt, :], cT[:, :]).then_inc(S["chi_rdy"], 1)
                    if k == 26:
                        step("cb_rdy")
                        nc.vector.tensor_tensor(cob[:, :], cT[0:E, :], cb[:, :], ALU.subtract).then_inc(S["cob_rdy"], 1)
                    if k == 27:
                        step("chi_rdy")
                        nc.vector.tensor_tensor(cst[F:P, nxt, :], cT[F:P, :], cst[F:P, nxt, :], ALU.subtract).then_inc(S["cst_rdy"], 1)
                    if k == 30:
                        full("cbB")
                        nc.vector.tensor_tensor(glin[:, nxt, :], banks(MISC, F), h2T[0:F, nxt, :], ALU.mult).then_inc(misc_free, 1)

                in_order(dve, slot)

            @block.tensor
            def _(pe):
                def wide(bank, lhsT, rhs, start=True, stop=True, rows=P):
                    for half in range(2):
                        last = nc.tensor.matmul(ps[0:rows, bank + half, :], lhsT, rhs[:, half * HALF:(half + 1) * HALF],
                                                start=start, stop=stop)
                    return last

                def pick(k):
                    return s.pick[:, k, :, :].rearrange("p j f -> p (j f)")

                def slot(ph, k):
                    b, i = ph.b, K2 * ph.b + k
                    if ph.run:
                        if k == 0:
                            pe.wait_ge(S["bst_rdy"], b + 1)
                        if not (isinstance(i, int) and i == 0):
                            pe.wait_ge(gated, i)
                        wide(GATES, pick(k), bst[:, ph.par, :]).then_inc(gate_ps, 1)
                    late = ph.lagging(k, LAG_W)
                    if late:
                        j, i_late, par = late
                        if j == 0:
                            pe.wait_ge(S["cst_rdy"], b + 1)
                        if not (isinstance(i_late, int) and i_late == 0):
                            pe.wait_ge(weighted, i_late)
                        wide(COEFS, pick(j), cst[:, par, :]).then_inc(coef_ps, 1)
                    late = ph.lagging(k, LAG_SUM)
                    if late:
                        j, i_late, par = late
                        if j == 0:
                            pe.wait_ge(S["cob_rdy"], b + 1)
                            if ph.prev:
                                pe.wait_ge(S["gT_rdy"], b)
                            pe.nop(nofuse=True)
                            wide(SUMS, agg[:, :], cob[:, :], stop=False, rows=F)
                        pe.wait_ge(weighted, i_late + 1)
                        wide(SUMS, s.twice[:, :], rb[:, j % BUFS, :], start=False, stop=(j == K2 - 1), rows=F).then_inc(summed, 1)
                    if ph.tail:
                        finish(ph, k)
                    if ph.prep:
                        prepare(ph, k)

                def freed(ph, name):
                    use = ph.use[name]
                    if not (isinstance(use, int) and use == 0):
                        pe.wait_ge(misc_free, use)
                    pe.nop(nofuse=True)

                def transposed(source):
                    for t in range(NT):
                        last = nc.tensor.transpose(ps[0:F, MISC + t // 4, (t % 4) * P:(t % 4 + 1) * P], source[:, t, :], s.ident[:, :])
                    last.then_inc(misc_full, 1)

                def finish(ph, k):
                    b = ph.b
                    if k == 0:
                        pe.wait_ge(S["ib_rdy"], 16 * b)
                        freed(ph, "ind")
                        transposed(ib)
                    if k == 10:
                        freed(ph, "fi")
                        wide(MISC, s.fcw[:, :], iT[:, :]).then_inc(misc_full, 1)
                    if k == 22:
                        pe.wait_ge(S["gT_rdy"], b)
                        freed(ph, "fg")
                        wide(MISC, s.fcw[:, :], gT[:, :]).then_inc(misc_full, 1)
                    if k == 26:
                        freed(ph, "d")
                        for half in range(2):
                            cols = slice(half * HALF, (half + 1) * HALF)
                            nc.tensor.matmul(ps[0:F, MISC + half, :], s.av[:, 0:F], t1[:, cols], start=True, stop=False)
                            last = nc.tensor.matmul(ps[0:F, MISC + half, :], s.nav[:, :], t2[:, cols], start=False, stop=True)
                        last.then_inc(misc_full, 1)
                    if k == 30:
                        pe.wait_ge(S["o_rdy"], b)
                        freed(ph, "oT")
                        for t in range(NT):
                            last = nc.tensor.transpose(ps[:, MISC, t * F:(t + 1) * F], sg[:, t * P:(t + 1) * P], s.ident[0:F, 0:F])
                        last.then_inc(misc_full, 1)

                def prepare(ph, k):
                    b, nxt = ph.b, 1 - ph.par

                    def step(name):
                        pe.wait_ge(S[name], b + 2)

                    if k == 2:
                        pe.wait_ge(S["xb_rdy"], 16 * (b + 2))
                        freed(ph, "xT")
                        transposed(xb)
                    if k == 4:
                        freed(ph, "h2T")
                        wide(MISC, s.w2[:, :], xT[:, :]).then_inc(misc_full, 1)
                    if k == 6:
                        freed(ph, "s")
                        wide(MISC, s.anode[:, :], h2T[0:F, nxt, :], rows=E).then_inc(misc_full, 1)
                    if k == 8:
                        freed(ph, "h2")
                        for t in range(NT):
                            last = nc.tensor.matmul(ps[:, MISC + t // 4, (t % 4) * P:(t % 4 + 1) * P], xT[:, t * P:(t + 1) * P],
                                                    s.w2[:, :], start=True, stop=True)
                        last.then_inc(misc_full, 1)
                    if k == 11:
                        step("al_rdy")
                        freed(ph, "alT")
                        for t in range(NT):
                            last = nc.tensor.transpose(ps[:, MISC, t * E:(t + 1) * E], al[:, t * P:(t + 1) * P], s.ident[0:E, 0:E])
                        last.then_inc(misc_full, 1)
                    if k == 13:
                        freed(ph, "agg")
                        for t in range(NT):
                            nc.tensor.matmul(ps[0:E, MISC, 0:F], alT[:, t, :], h2[:, t, 0:F], start=(t == 0), stop=(t == NT - 1))
                        for t in range(NT):
                            last = nc.tensor.matmul(ps[:, MISC + 1, 0:E], h2[:, t, :], alT[:, t, :], start=(t == 0), stop=(t == NT - 1))
                        last.then_inc(misc_full, 1)
                    if k == 15:
                        freed(ph, "q")
                        nc.tensor.matmul(ps[:, MISC, 0:1], aggT[:, :, :].rearrange("p j e -> p (j e)"), s.age[:, :], start=True,
                                         stop=True).then_inc(misc_full, 1)
                    if k == 16:
                        step("he_rdy")
                        freed(ph, "fc")
                        nc.tensor.matmul(ps[:, MISC, 0:E], s.fcw[:, :], heT[:, :], start=True, stop=True).then_inc(misc_full, 1)
                    if k == 18:
                        freed(ph, "se")
                        nc.tensor.matmul(ps[:, MISC, 0:E], s.av[:, :], thf[:, :], start=True, stop=True).then_inc(misc_full, 1)
                    if k == 20:
                        freed(ph, "p")
                        wide(MISC, s.agn[:, :], h2T[0:F, nxt, :]).then_inc(misc_full, 1)
                    if k == 24:
                        step("cd_rdy")
                        freed(ph, "cT")
                        for t in range(NT):
                            last = nc.tensor.transpose(ps[:, MISC + t // 4, (t % 4) * P:(t % 4 + 1) * P],
                                                       cd[:, t, :, :].rearrange("p j e -> p (j e)"), s.ident[:, :])
                        last.then_inc(misc_full, 1)
                    if k == 29:
                        step("cb_rdy")
                        freed(ph, "cbB")
                        wide(MISC, s.ones[0:E, 0:F], cb[:, :], rows=F).then_inc(misc_full, 1)

                in_order(pe, slot)


def norm(nc, s, name, out=None):
    with ExitStack() as ctx:
        def sb(n, shape, dt=F32):
            return ctx.enter_context(nc.sbuf_tensor(f"{name}_{n}", shape, dt))

        def sem(n):
            return ctx.enter_context(nc.semaphore(f"{name}_{n}"))

        T = B * NT
        sq, mean, var, root, rec = sb("squares", [P, T, F]), sb("mean", [P, T]), sb("var", [P, T]), sb("root", [P, T]), sb("rec", [P, T])
        summed, meaned, centred, squared, square_sum, shifted, rooted, inverted, normed, stored = (
            sem(n) for n in ("summed", "meaned", "centred", "squared", "square_sum", "shifted", "rooted", "inverted", "normed", "stored"))

        def over_f(a):
            return a[:, :].unsqueeze(2).broadcast_to([P, T, F])

        with nc.Block() as block:
            @block.vector
            def _(dve):
                nc.vector.tensor_reduce(mean[:, :], s.X[:, :, :], AX.X, ALU.add).then_inc(summed, 1)
                dve.wait_ge(summed, 1)
                nc.vector.tensor_scalar(mean[:, :], mean[:, :], 1.0 / F, None, ALU.mult).then_inc(meaned, 1)
                dve.wait_ge(meaned, 1)
                nc.vector.tensor_tensor(s.X[:, :, :], s.X[:, :, :], over_f(mean), ALU.subtract).then_inc(centred, 1)
                dve.wait_ge(squared, 1)
                nc.vector.tensor_reduce(var[:, :], sq[:, :, :], AX.X, ALU.add).then_inc(square_sum, 1)
                dve.wait_ge(square_sum, 1)
                nc.vector.tensor_scalar(var[:, :], var[:, :], 1.0 / F, EPS, ALU.mult, ALU.add).then_inc(shifted, 1)
                dve.wait_ge(rooted, 1)
                nc.vector.reciprocal(rec[:, :], root[:, :]).then_inc(inverted, 1)
                dve.wait_ge(inverted, 1)
                nc.vector.tensor_tensor(s.X[:, :, :], s.X[:, :, :], over_f(rec), ALU.mult).then_inc(normed, 1)

            @block.scalar
            def _(act):
                act.wait_ge(centred, 1)
                nc.scalar.activation(sq[:, :, :], s.X[:, :, :], ACT.Square).then_inc(squared, 1)
                act.wait_ge(shifted, 1)
                nc.scalar.activation(root[:, :], var[:, :], ACT.Sqrt).then_inc(rooted, 1)

            if out is not None:
                @block.sync
                def _(sp):
                    sp.wait_ge(normed, 1)
                    sp.dma_start(out.rearrange("b (t p) f -> p (b t) f", p=P), s.X[:, :, :]).then_inc(stored, 16)
                    sp.wait_ge(stored, 16)


def layer1(nc, s):
    with ExitStack() as ctx:
        def sb(name, shape, dt=F32):
            return ctx.enter_context(nc.sbuf_tensor(name, shape, dt))

        def pb(name, shape, dt=F32):
            return ctx.enter_context(nc.psum_tensor(name, shape, dt))

        def sem(name):
            return ctx.enter_context(nc.semaphore(name))

        ps_s, ps_t, acc, misc = pb("ps_scores", [P, 2, N]), pb("ps_probsT", [P, N]), pb("ps_acc", [P, HALF]), pb("ps_misc", [P, HALF])
        misc16, ps_t16 = misc[:, :].bitcast(F16), ps_t[:, :].bitcast(F16)
        tb, pbuf = sb("l1_scores", [P, 4, N]), sb("l1_probs", [P, 4, N])
        ph, pl, pt = sb("l1_probs_hi", [P, 4, N], F16), sb("l1_probs_lo", [P, 4, N], F16), sb("l1_probsT", [P, 2, 2 * N], F16)
        nm, rs, rr = sb("l1_shift", [P, 4]), sb("l1_sums", [P, 3, NT]), sb("l1_rec", [P, NT])
        zf, zs, zT = sb("l1_z", [P, NT, F]), sb("l1_z_split", [P, NT, 2, F], F16), sb("l1_zT", [P, N], F16)
        cv, cat, ob = sb("l1_head_out", [P, 2, HALF]), sb("l1_cat", [P, HEADS, N]), sb("l1_out", [P, NT, F])

        class Source:

            def __init__(self, features, y, sums):
                self.xs, self.xh, self.xl = features
                self.y, self.sums = y, sums

        def features(name):
            return sb(f"l1_{name}_split", [P, 2, NT, 2, F], F16), sb(f"l1_{name}_hi", [P, N], F16), sb(f"l1_{name}_lo", [P, N], F16)

        of_x = features("x")
        head = [Source(of_x, sb(f"l1_y{p}", [P, N], F16), rs[:, p, :]) for p in range(2)]
        output = Source(features("h2"), sb("l1_y_out", [P, N], F16), rs[:, 2, :])

        (scored, masked, exped, hi_done, lo_done, turned, kept_hi, kept_lo, mixed) = (
            sem(n) for n in ("scored", "masked", "exped", "hi_done", "lo_done", "turned", "kept_hi", "kept_lo", "mixed"))
        misc_full, misc_free, y_hi, cat_ready = (sem(n) for n in ("misc_full", "misc_free", "y_hi", "cat_ready"))
        x_hi, x_split, z_rec, z_ready, z_hi, z_split = (sem(n) for n in ("x_hi", "x_split", "z_rec", "z_ready", "z_hi", "z_split"))
        h2_hi, y_out, o_bias, o_leak, out_added = (sem(n) for n in ("h2_hi", "y_out", "o_bias", "o_leak", "out_added"))

        def is_0(b):
            return isinstance(b, int) and b == 0

        def first_q(b):
            return 0 if is_0(b) else 9 * b - 1

        def use_base(b):
            return 0 if is_0(b) else 45 * b + 1

        def use_head(b, h):
            return use_base(b) + (6 if is_0(b) else 5) + 5 * (h - 1)

        def use_switch(b):
            return use_base(b) + (6 if is_0(b) else 5) + 33

        USE_END = use_switch(B - 1) + 3

        def reused(i, buffers):
            return not (isinstance(i, int) and i < buffers)

        def in_order(eng, steps):
            def batch(b, after_out, has_next):
                q = first_q(b)
                steps.head_0(b, q, after_out)
                with eng.Fori(0, HEADS // 2 - 1) as pair:
                    for j in range(2):
                        steps.head_h(b, q + 2 * pair + 1 + j, 2 * pair + 1 + j, 1 - j)
                steps.head_7(b, q + 7)
                if is_0(b):
                    steps.switch(b, q + 8)
                else:
                    steps.out(b, q + 8, has_next)

            steps.start()
            batch(0, False, True)
            batch(1, False, True)
            with eng.Fori(2, B - 1) as b:
                batch(b, True, True)
            batch(B - 1, True, False)
            steps.end(first_q(B - 1) + 9)

        with nc.Block() as block:
            @block.tensor
            def _(pe):
                def score(q, src, t):
                    i = NT * q + t
                    if reused(i, 2):
                        pe.wait_ge(masked, i - 1)
                    rows = src.y[:, t * P:(t + 1) * P]
                    for half in range(2):
                        cols = slice(half * HALF, (half + 1) * HALF)
                        nc.tensor.matmul(ps_s[:, t % 2, cols], rows, src.xh[:, cols], start=True, stop=False)
                        last = nc.tensor.matmul(ps_s[:, t % 2, cols], rows, src.xl[:, cols], start=False, stop=True)
                    last.then_inc(scored, 1)

                def turn(q, t):
                    i = NT * q + t
                    if reused(i, 1):
                        pe.wait_ge(kept_lo, i)
                        if t % 2 == 1:
                            pe.wait_ge(kept_hi, 4 * q + t // 2 + 1)
                    pe.wait_ge(hi_done, i + 1)
                    for m in range(NT):
                        nc.tensor.transpose(ps_t16[:, m * P:(m + 1) * P], ph[:, t % 4, m * P:(m + 1) * P], s.ident16[:, :])
                    pe.wait_ge(lo_done, i + 1)
                    for m in range(NT):
                        last = nc.tensor.transpose(ps_t16[:, N + m * P:N + (m + 1) * P], pl[:, t % 4, m * P:(m + 1) * P], s.ident16[:, :])
                    last.then_inc(turned, 1)

                def mix(q, src, t):
                    i = NT * q + t
                    pe.wait_ge(kept_lo, i + 1)
                    if t % 2 == 0:
                        pe.wait_ge(kept_hi, 4 * q + t // 2 + 1)
                    for m in range(NT):
                        hi, lo = pt[:, t % 2, m * P:(m + 1) * P], pt[:, t % 2, N + m * P:N + (m + 1) * P]
                        to = acc[:, t * F:(t + 1) * F]
                        nc.tensor.matmul(to, hi, src.xs[:, 0, m, 0, :], start=(m == 0), stop=False)
                        nc.tensor.matmul(to, hi, src.xs[:, 1, m, 0, :], start=False, stop=False)
                        last = nc.tensor.matmul(to, lo, src.xs[:, 0, m, 0, :], start=False, stop=(m == NT - 1))
                    last.then_inc(mixed, 1)

                def keys(src, c, use):
                    if not (isinstance(use, int) and use == 0):
                        pe.wait_ge(misc_free, use)
                    for t in range(NT):
                        last = nc.tensor.transpose(misc16[:, t * P:(t + 1) * P], src.xs[:, c, t, :, :].rearrange("p j f -> p (j f)"),
                                                   s.ident16[:, :])
                    last.then_inc(misc_full, 1)

                def queries(h, half, use):
                    pe.wait_ge(misc_free, use)
                    gram = s.gram[:, bass.ds(h * P, P)]
                    cols = slice(half * HALF, (half + 1) * HALF)
                    nc.tensor.matmul(misc[:, :], gram, head[0].xh[:, cols], start=True, stop=False)
                    nc.tensor.matmul(misc[:, :], gram, head[0].xl[:, cols], start=False, stop=True).then_inc(misc_full, 1)

                def turn_z(n, use):
                    pe.wait_ge(z_split, n + 1)
                    pe.wait_ge(misc_free, use)
                    for t in range(NT):
                        last = nc.tensor.transpose(misc16[:, t * P:(t + 1) * P], zs[:, t, :, :].rearrange("p j f -> p (j f)"), s.ident16[:, :])
                    last.then_inc(misc_full, 1)

                def head_out(h, half, use):
                    pe.wait_ge(misc_free, use)
                    for w, first in ((s.w_hi, True), (s.w_lo, False)):
                        last = nc.tensor.matmul(misc[:, :], w[:, bass.ds(h, 1), :].rearrange("p o k -> p (o k)"),
                                                zT[:, half * HALF:(half + 1) * HALF], start=first, stop=not first)
                    last.then_inc(misc_full, 1)

                def h2(b, use):
                    pe.wait_ge(cat_ready, 2 * HEADS * (b + 1))
                    pe.wait_ge(misc_free, use)
                    for t in range(NT):
                        for h in range(HEADS):
                            last = nc.tensor.matmul(misc[:, t * F:(t + 1) * F], cat[:, h, t * P:(t + 1) * P], s.wout[:, h, :],
                                                    start=(h == 0), stop=(h == HEADS - 1))
                    last.then_inc(misc_full, 1)

                def body(q, src, nxt, ready, prev, extra):
                    for t in range(NT):
                        turn(q, t)
                        if t + 3 < NT:
                            score(q, src, t + 3)
                        elif nxt is not None:
                            if t + 3 == NT:
                                pe.wait_ge(*ready)
                            score(q + 1, nxt, t + 3 - NT)
                        extra(t)
                        if t > 0:
                            mix(q, src, t - 1)
                        else:
                            if prev is not None:
                                mix(q - 1, prev, NT - 1)
                            if reused(q, 1):
                                pe.wait_ge(z_ready, q)

                class Steps:
                    def start(self):
                        pe.wait_ge(x_split, 1)
                        keys(head[0], 0, 0)
                        keys(head[0], 1, 1)
                        queries(0, 0, 2)
                        queries(0, 1, 3)
                        pe.wait_ge(misc_free, 4)
                        for t in range(3):
                            score(0, head[0], t)

                    def head_0(self, b, q, after_out):
                        use = use_base(b)

                        def extra(t):
                            if is_0(b) and t in (1, 2):
                                queries(1, t - 1, use + 3 + t)
                            if not is_0(b):
                                if t == 0:
                                    h2(b - 1, use)
                                if t in (2, 3):
                                    queries(1, t - 2, use + t - 1)
                                if t in (5, 6):
                                    keys(output, t - 5, use + t - 2)
                        body(q, head[0], head[1], (misc_free, use + (6 if is_0(b) else 3)), output if after_out else None, extra)

                    def head_h(self, b, q, h, par):
                        use = use_head(b, h)

                        def extra(t):
                            if t in (1, 2):
                                queries(h + 1, t - 1, use + t - 1)
                            if t == 3:
                                turn_z(8 * b + h - 1, use + 2)
                            if t in (5, 6):
                                head_out(h - 1, t - 5, use + t - 2)
                        body(q, head[par], head[1 - par], (misc_free, use + 2), head[1 - par], extra)

                    def head_7(self, b, q):
                        use = use_head(b, 7)

                        def extra(t):
                            if t == 3:
                                turn_z(8 * b + 6, use)
                            if t in (5, 6):
                                head_out(6, t - 5, use + t - 4)
                        if is_0(b):
                            body(q, head[1], None, None, head[0], extra)
                        else:
                            body(q, head[1], output, (y_out, b), head[0], extra)

                    def out(self, b, q, has_next):
                        use = use_switch(b)

                        def extra(t):
                            if has_next:
                                if t in (1, 2):
                                    if t == 1:
                                        pe.wait_ge(x_split, b + 2)
                                    keys(head[0], t - 1, use + t - 1)
                                if t in (3, 4):
                                    queries(0, t - 3, use + t - 1)
                            at = 5 if has_next else 3
                            last = use + (4 if has_next else 0)
                            if t == at:
                                turn_z(8 * b + 7, last)
                            if t in (6, 7):
                                head_out(7, t - 6, last + t - 5)
                        body(q, output, head[0] if has_next else None, (misc_free, use + 4), head[1], extra)

                    def switch(self, b, q):
                        use = use_switch(b)
                        mix(q - 1, head[1], NT - 1)
                        pe.wait_ge(x_split, b + 2)
                        keys(head[0], 0, use)
                        keys(head[0], 1, use + 1)
                        queries(0, 0, use + 2)
                        queries(0, 1, use + 3)
                        pe.wait_ge(misc_free, use + 4)
                        for t in range(3):
                            score(q, head[0], t)
                        turn_z(8 * b + 7, use + 4)
                        head_out(7, 0, use + 5)
                        head_out(7, 1, use + 6)

                    def end(self, q):
                        mix(q - 1, output, NT - 1)
                        h2(B - 1, USE_END)
                        keys(output, 0, USE_END + 1)
                        keys(output, 1, USE_END + 2)
                        pe.wait_ge(y_out, B)
                        for t in range(3):
                            score(q, output, t)
                        body(q, output, None, None, None, lambda t: None)
                        mix(q, output, NT - 1)

                in_order(pe, Steps())

            @block.scalar
            def _(act):
                def expo(q, src, t):
                    i = NT * q + t
                    act.wait_ge(masked, i + 1)
                    if reused(i, 4):
                        act.wait_ge(lo_done, i - 3)
                    nc.scalar.activation(pbuf[:, t % 4, :], tb[:, t % 4, :], ACT.Exp, bias=nm[:, t % 4:t % 4 + 1], scale=-1.0,
                                         accum_out=src.sums[:, t:t + 1]).then_inc(exped, 1)

                def hi(q, t):
                    i = NT * q + t
                    act.wait_ge(exped, i + 1)
                    if reused(i, 4):
                        act.wait_ge(turned, i - 3)
                    nc.scalar.copy(ph[:, t % 4, :], pbuf[:, t % 4, :]).then_inc(hi_done, 1)

                def keep(q, t):
                    i = NT * q + t
                    act.wait_ge(turned, i + 1)
                    if reused(i, 2):
                        act.wait_ge(mixed, i - 1)
                    nc.scalar.copy(pt[:, t % 2, 0:N].bitcast(F32), ps_t[:, 0:HALF]).then_inc(kept_hi, 1)

                def keep_keys(src, c, use):
                    act.wait_ge(misc_full, use + 1)
                    nc.scalar.copy((src.xl if c else src.xh)[:, :].bitcast(F32), misc[:, :]).then_inc(misc_free, 1)

                def queries_hi(src, half, use):
                    act.wait_ge(misc_full, use + 1)
                    nc.scalar.copy(src.y[:, half * HALF:(half + 1) * HALF], misc[:, :]).then_inc(y_hi, 1)

                def keep_zT(use):
                    act.wait_ge(misc_full, use + 1)
                    nc.scalar.copy(zT[:, :].bitcast(F32), misc[:, :]).then_inc(misc_free, 1)

                def bias(h, half, use):
                    act.wait_ge(misc_full, use + 1)
                    act.nop(nofuse=True)
                    nc.scalar.activation(cv[:, half, :], misc[:, :], ACT.Identity, bias=s.bh[:, bass.ds(h, 1)]).then_inc(misc_free, 1)

                def queries_out(use):
                    act.wait_ge(misc_free, use)
                    nc.scalar.copy(output.y[0:F, :], output.xh[0:F, :])
                    nc.scalar.copy(output.y[F:P, :], output.xl[F:P, :]).then_inc(y_out, 1)

                def body(q, src, nxt, extra):
                    for t in range(NT):
                        u, of, v = (q, src, t + 2) if t + 2 < NT else (q + 1, nxt, t + 2 - NT)
                        if of is not None:
                            expo(u, of, v)
                        if t % 2 == 0:
                            keep(q, t)
                        if of is not None:
                            hi(u, v)
                        extra(t)

                class Steps:
                    def start(self):
                        keep_keys(head[0], 0, 0)
                        keep_keys(head[0], 1, 1)
                        queries_hi(head[0], 0, 2)
                        queries_hi(head[0], 1, 3)
                        for t in range(2):
                            expo(0, head[0], t)
                            hi(0, t)

                    def head_0(self, b, q, after_out):
                        use = use_base(b)

                        def extra(t):
                            if is_0(b) and t in (1, 2):
                                queries_hi(head[1], t - 1, use + 3 + t)
                            if not is_0(b):
                                if t in (2, 3):
                                    queries_hi(head[1], t - 2, use + t - 1)
                                if t in (5, 6):
                                    keep_keys(output, t - 5, use + t - 2)
                                if t == 7:
                                    queries_out(use + 5)
                        body(q, head[0], head[1], extra)

                    def head_h(self, b, q, h, par):
                        use = use_head(b, h)

                        def extra(t):
                            if t in (1, 2):
                                queries_hi(head[1 - par], t - 1, use + t - 1)
                            if t == 3:
                                keep_zT(use + 2)
                            if t in (5, 6):
                                bias(h - 1, t - 5, use + t - 2)
                        body(q, head[par], head[1 - par], extra)

                    def head_7(self, b, q):
                        use = use_head(b, 7)

                        def extra(t):
                            if t == 3:
                                keep_zT(use)
                            if t in (5, 6):
                                bias(6, t - 5, use + t - 4)
                        body(q, head[1], None if is_0(b) else output, extra)

                    def out(self, b, q, has_next):
                        use = use_switch(b)

                        def extra(t):
                            if has_next:
                                if t in (1, 2):
                                    keep_keys(head[0], t - 1, use + t - 1)
                                if t in (3, 4):
                                    queries_hi(head[0], t - 3, use + t - 1)
                            last = use + (4 if has_next else 0)
                            if t == (5 if has_next else 3):
                                keep_zT(last)
                            if t in (6, 7):
                                bias(7, t - 6, last + t - 5)
                        body(q, output, head[0] if has_next else None, extra)

                    def switch(self, b, q):
                        use = use_switch(b)
                        keep_keys(head[0], 0, use)
                        keep_keys(head[0], 1, use + 1)
                        queries_hi(head[0], 0, use + 2)
                        queries_hi(head[0], 1, use + 3)
                        keep_zT(use + 4)
                        bias(7, 0, use + 5)
                        bias(7, 1, use + 6)
                        for t in range(2):
                            expo(q, head[0], t)
                            hi(q, t)

                    def end(self, q):
                        keep_keys(output, 0, USE_END + 1)
                        keep_keys(output, 1, USE_END + 2)
                        queries_out(USE_END + 3)
                        for t in range(2):
                            expo(q, output, t)
                            hi(q, t)
                        body(q, output, None, lambda t: None)

                in_order(act, Steps())

            @block.vector
            def _(dve):
                def mask(q, t):
                    i = NT * q + t
                    dve.wait_ge(scored, i + 1)
                    if reused(i, 4):
                        dve.wait_ge(exped, i - 3)
                    dve.nop(nofuse=True)
                    nc.vector.tensor_tensor_reduce(tb[:, t % 4, :], ps_s[:, t % 2, :], s.offgraph[:, t, :], -1.0, BIG, ALU.add,
                                                   ALU.min, nm[:, t % 4:t % 4 + 1]).then_inc(masked, 1)

                def keep(q, t):
                    i = NT * q + t
                    dve.wait_ge(turned, i + 1)
                    if reused(i, 2):
                        dve.wait_ge(mixed, i - 1)
                    start = 0 if t % 2 else HALF
                    nc.vector.tensor_copy(pt[:, t % 2, 2 * start:2 * N].bitcast(F32), ps_t[:, start:N]).then_inc(kept_lo, 1)

                def queries_lo(b, h, half, src):
                    dve.wait_ge(y_hi, 16 * b + 2 * h + half + 1)
                    lo = src.y[F:P, half * HALF:(half + 1) * HALF]
                    nc.vector.tensor_tensor(lo, misc[F:P, :], lo, ALU.subtract).then_inc(misc_free, 1)

                def split_x(b):
                    rows, xs = s.X[:, bass.ds(b * NT, NT), :], head[0].xs
                    nc.vector.tensor_copy(xs[:, 0, :, :, :], rows.unsqueeze(2).broadcast_to([P, NT, 2, F])).then_inc(x_hi, 1)
                    dve.wait_ge(x_hi, b + 1)
                    for j in range(2):
                        last = nc.vector.tensor_tensor(xs[:, 1, :, j, :], rows, xs[:, 0, :, j, :], ALU.subtract)
                    last.then_inc(x_split, 1)

                def split_h2(b, use):
                    rows, xs = misc[:, :].rearrange("p (t f) -> p t f", t=NT), output.xs
                    dve.wait_ge(misc_full, use + 1)
                    nc.vector.tensor_copy(xs[:, 0, :, :, :], rows.unsqueeze(2).broadcast_to([P, NT, 2, F])).then_inc(h2_hi, 1)
                    dve.wait_ge(h2_hi, b + 1)
                    for j in range(2):
                        last = nc.vector.tensor_tensor(xs[:, 1, :, j, :], rows, xs[:, 0, :, j, :], ALU.subtract)
                    last.then_inc(misc_free, 1)

                def normalise(q, src):
                    dve.wait_ge(mixed, NT * q + NT)
                    nc.vector.reciprocal(rr[:, :], src.sums).then_inc(z_rec, 1)
                    dve.wait_ge(z_rec, q + 1)
                    nc.vector.tensor_tensor(zf[:, :, :], acc[:, :].rearrange("p (t f) -> p t f", t=NT),
                                            rr[:, :].unsqueeze(2).broadcast_to([P, NT, F]), ALU.mult).then_inc(z_ready, 1)

                def leak(h, half, use):
                    dve.wait_ge(misc_free, use + 1)
                    nc.vector.scalar_tensor_tensor(
                        out=cat[:, bass.ds(h, 1), half * HALF:(half + 1) * HALF].rearrange("p o n -> p (o n)"),
                        in0=cv[:, half, :], scalar=0.01, in1=cv[:, half, :], op0=ALU.mult, op1=ALU.max).then_inc(cat_ready, 1)

                def finish(b, q):
                    normalise(q, output)
                    dve.wait_ge(z_ready, q + 1)
                    nc.vector.tensor_tensor(ob[:, :, :], zf[:, :, :], s.bout[:, :].unsqueeze(1).broadcast_to([P, NT, F]), ALU.add).then_inc(o_bias, 1)
                    dve.wait_ge(o_bias, b + 1)
                    nc.vector.scalar_tensor_tensor(out=zf[:, :, :], in0=ob[:, :, :], scalar=0.01, in1=ob[:, :, :], op0=ALU.mult,
                                                   op1=ALU.max).then_inc(o_leak, 1)
                    dve.wait_ge(o_leak, b + 1)
                    rows = s.X[:, bass.ds(b * NT, NT), :]
                    nc.vector.tensor_tensor(rows, rows, zf[:, :, :], ALU.add).then_inc(out_added, 1)

                def body(q, src, nxt, extra):
                    for t in range(NT):
                        keep(q, t)
                        if t + 3 < NT:
                            mask(q, t + 3)
                        elif nxt:
                            mask(q + 1, t + 3 - NT)
                        extra(t)

                class Steps:
                    def start(self):
                        split_x(0)
                        queries_lo(0, 0, 0, head[0])
                        queries_lo(0, 0, 1, head[0])
                        for t in range(3):
                            mask(0, t)

                    def head_0(self, b, q, after_out):
                        use = use_base(b)

                        def extra(t):
                            if t == 0 and after_out:
                                finish(b - 2, q - 1)
                            if is_0(b) and t in (1, 2):
                                queries_lo(b, 1, t - 1, head[1])
                            if not is_0(b):
                                if t == 0:
                                    split_h2(b - 1, use)
                                if t in (2, 3):
                                    queries_lo(b, 1, t - 2, head[1])
                        body(q, head[0], True, extra)

                    def head_h(self, b, q, h, par):
                        use = use_head(b, h)

                        def extra(t):
                            if t == 0:
                                normalise(q - 1, head[1 - par])
                            if t in (1, 2):
                                queries_lo(b, h + 1, t - 1, head[1 - par])
                            if t in (5, 6):
                                leak(h - 1, t - 5, use + t - 2)
                        body(q, head[par], True, extra)

                    def head_7(self, b, q):
                        use = use_head(b, 7)

                        def extra(t):
                            if t == 0:
                                normalise(q - 1, head[0])
                            if t in (5, 6):
                                leak(6, t - 5, use + t - 4)
                        body(q, head[1], not is_0(b), extra)

                    def out(self, b, q, has_next):
                        use = use_switch(b)

                        def extra(t):
                            if t == 0:
                                normalise(q - 1, head[1])
                                if has_next:
                                    split_x(b + 1)
                            if has_next and t in (3, 4):
                                queries_lo(b + 1, 0, t - 3, head[0])
                            if t in (6, 7):
                                leak(7, t - 6, use + (4 if has_next else 0) + t - 5)
                        body(q, output, has_next, extra)

                    def switch(self, b, q):
                        use = use_switch(b)
                        normalise(q - 1, head[1])
                        split_x(b + 1)
                        queries_lo(b + 1, 0, 0, head[0])
                        queries_lo(b + 1, 0, 1, head[0])
                        for t in range(3):
                            mask(q, t)
                        leak(7, 0, use + 5)
                        leak(7, 1, use + 6)

                    def end(self, q):
                        finish(B - 2, q - 1)
                        split_h2(B - 1, USE_END)
                        for t in range(3):
                            mask(q, t)
                        body(q, output, False, lambda t: None)
                        finish(B - 1, q)

                in_order(dve, Steps())

            @block.gpsimd
            def _(pool):
                def lo(q, t):
                    i = NT * q + t
                    if reused(i, 4):
                        pool.wait_ge(turned, i - 3)
                    pool.wait_ge(hi_done, i + 1)
                    nc.gpsimd.tensor_tensor(pl[:, t % 4, :], pbuf[:, t % 4, :], ph[:, t % 4, :], ALU.subtract).then_inc(lo_done, 1)

                def split_z(n, q):
                    if reused(n, 1):
                        pool.wait_ge(cat_ready, 2 * n)
                    pool.wait_ge(z_ready, q + 1)
                    pool.nop(nofuse=True)
                    nc.gpsimd.tensor_scalar(zs[:, :, 0, :], zf[:, :, :], 1.0, 0.0, ALU.mult, ALU.add).then_inc(z_hi, 1)
                    pool.wait_ge(z_hi, n + 1)
                    nc.gpsimd.tensor_tensor(zs[:, :, 1, :], zf[:, :, :], zs[:, :, 0, :], ALU.subtract).then_inc(z_split, 1)

                def body(q, nxt, extra):
                    for t in range(NT):
                        if t + 2 < NT:
                            lo(q, t + 2)
                        elif nxt:
                            lo(q + 1, t + 2 - NT)
                        extra(t)

                class Steps:
                    def start(self):
                        lo(0, 0)
                        lo(0, 1)

                    def head_0(self, b, q, after_out):
                        body(q, True, lambda t: None)

                    def head_h(self, b, q, h, par):
                        body(q, True, lambda t: split_z(8 * b + h - 1, q - 1) if t == 1 else None)

                    def head_7(self, b, q):
                        body(q, not is_0(b), lambda t: split_z(8 * b + 6, q - 1) if t == 1 else None)

                    def out(self, b, q, has_next):
                        body(q, has_next, lambda t: split_z(8 * b + 7, q - 1) if t == 1 else None)

                    def switch(self, b, q):
                        split_z(8 * b + 7, q - 1)
                        lo(q, 0)
                        lo(q, 1)

                    def end(self, q):
                        lo(q, 0)
                        lo(q, 1)
                        body(q, False, lambda t: None)

                in_order(pool, Steps())


def build(nc, g, out):
    with ExitStack() as ctx:
        def sb(name, shape, dt=F32):
            return ctx.enter_context(nc.sbuf_tensor(name, shape, dt))

        s = Net()
        s.X = sb("x_all", [P, B * NT, F])
        s.industry = sb("industry", [P, NT, B * F])
        s.offgraph = sb("off_graph", [P, NT, N], BF16)
        s.ident, s.ident16, s.ones = sb("ident", [P, P]), sb("ident16", [P, P], F16), sb("ones", [P, F])
        s.twice, s.pick = sb("twice", [P, F]), sb("pick_edge", [P, K2, 2, F], F16)
        s.w2, s.fcw, s.fcb = sb("w_twice", [F, P]), sb("fcw", [F, P]), sb("fcb", [P, 1])
        s.anode, s.agn, s.age = sb("a_node", [F, E]), sb("a_gn", [F, P]), sb("a_ge", [F, 1])
        s.av, s.nav = sb("av", [P, P]), sb("minus_av", [P, F])
        s.mask, s.off = sb("mask", [P, NT, E]), sb("off_edge", [P, NT, E])
        s.maskT, s.offT = sb("maskT", [E, N]), sb("off_edgeT", [E, N])
        s.w_hi, s.w_lo = sb("w_hi", [P, HEADS, HID], F16), sb("w_lo", [P, HEADS, HID], F16)
        s.gram = sb("gram", [P, HEADS * P], F16)
        s.wout, s.bh, s.bout = sb("wout", [P, HEADS, F]), sb("bh", [P, HEADS]), sb("bout", [P, F])
        setup(nc, g, s)
        layer0(nc, s)
        norm(nc, s, "norm0")
        layer1(nc, s)
        norm(nc, s, "norm1", out)


_INS = {"x": "x", "adj": "adj", "L0_gnn_H": "H", "L0_gnn_W": "W", "L0_gnn_W_ind": "W_ind", "L0_gnn_a_node": "a_node",
        "L0_gnn_a_gn": "a_gn", "L0_gnn_a_ge": "a_ge", "L0_gnn_fcW": "fcW", "L0_gnn_fcb": "fcb", "L0_gnn_av": "av",
        "L1_gnn_Wh": "Wh", "L1_gnn_bh": "bh", "L1_gnn_W_out": "W_out", "L1_gnn_b_out": "b_out"}


def kernel(**inputs):
    import numpy as _np
    import concourse.bacc as _bacc
    from concourse import mybir as _mybir
    from concourse.bass_utils import run_bass_kernel_spmd as _run

    nc = _bacc.Bacc("TRN2", target_bir_lowering=False, num_devices=1)
    arrays, g = {}, Net()
    for name, short in _INS.items():
        a = _np.ascontiguousarray(inputs[name])
        arrays[f"in_{name}"] = a
        g.__dict__[short] = nc.dram_tensor(f"in_{name}", a.shape, _mybir.dt.from_np(a.dtype), kind="ExternalInput").ap()
    out = nc.dram_tensor("out", (B, N, F), F32, kind="ExternalOutput").ap()
    build(nc, g, out)
    r = _run(nc, [arrays], core_ids=[0])
    return r.results[0]["out"]
```

```python
from contextlib import ExitStack

import concourse.bass as bass
from concourse import mybir

ALU = mybir.AluOpType
ACT = mybir.ActivationFunctionType
AX = mybir.AxisListType
F32 = mybir.dt.float32
F16 = mybir.dt.float16
BF16 = mybir.dt.bfloat16

P = 128
B, N, F = 8, 1024, 64
E = 64
NT = N // P
HEADS, HID = 8, 128
HALF = 512
K2 = E // 2
OFF = float(2 ** 53)
EPS = 1e-5
BIG = 3.0e38

class Net:
    pass


def setup(nc, g, s):
    with ExitStack() as ctx:
        def sb(name, shape, dt=F32):
            return ctx.enter_context(nc.sbuf_tensor(name, shape, dt))

        def sem(name):
            return ctx.enter_context(nc.semaphore(name))

        ps = ctx.enter_context(nc.psum_tensor("ps_setup", [P, 8, HALF], F32))
        adj = sb("adj_rows", [P, NT, N])
        adj16, adjT = sb("adj_rows16", [P, NT, N], F16), sb("adj_cols16", [P, NT, N], F16)
        x_hi, x_lo = sb("x_hi", [P, NT, B, F], F16), sb("x_lo", [P, NT, B, F], F16)
        wh = sb("wh_twice", [P, HEADS, HID])
        wout = sb("w_out", [P, HEADS, F])
        whT = sb("wh_transposed", [P, HEADS, 2, F])
        hrow = sb("incidence", [P, NT, E])
        cols = sb("attention_columns", [F, 3])
        avc = sb("av_column", [P, 1])
        ones16, rdeg = sb("ones16", [P, P], F16), sb("degree_reciprocal", [P, N])

        loaded_w, loaded_x, loaded_adj = sem("loaded_w"), sem("loaded_x"), [sem(f"loaded_adj{t}") for t in range(NT)]
        zeroed, ident_ready = sem("zeroed"), sem("ident_ready")
        whT_psum, whT_ready, gram_psum, gram_hi = sem("whT_psum"), sem("whT_ready"), sem("gram_psum"), sem("gram_hi")
        wout_ready = sem("wout_ready")
        wa_ready, stacked = sem("wa_ready"), sem("stacked")
        mask_ready, maskT_psum, maskT_ready = sem("mask_ready"), sem("maskT_psum"), sem("maskT_ready")
        adj16_ready, adjT_psum, adjT_ready = sem("adj16_ready"), sem("adjT_psum"), sem("adjT_ready")
        x_hi_ready, x_lo_ready = sem("x_hi_ready"), sem("x_lo_ready")
        deg_psum, deg_floor, rdeg_ready, mean_psum, mean_ready = (
            sem(n) for n in ("deg_psum", "deg_floor", "rdeg_ready", "mean_psum", "mean_ready"))

        WEIGHTS = 15
        with nc.Block() as block:
            @block.sync
            def _(sp):
                def load(dst, src, slow=False):
                    sp.dma_start(dst, src, allow_slow_non_contiguous=slow).then_inc(loaded_w, 16)
                sp.dma_start(s.X[:, :, :], g.x.rearrange("b (t p) f -> p (b t) f", p=P)).then_inc(loaded_x, 16)
                load(wh[0:F, :, :], g.Wh.rearrange("h f k -> f h k"))
                load(wh[F:P, :, :], g.Wh.rearrange("h f k -> f h k"))
                load(hrow[:, :, :], g.H.rearrange("(t p) e -> p t e", p=P))
                load(s.w2[:, 0:F], g.W)
                load(s.w2[:, F:P], g.W)
                load(s.wind[:, :], g.W_ind)
                for c, a in enumerate((g.a_node, g.a_gn, g.a_ge)):
                    load(cols[:, c:c + 1], a.rearrange("(f o) -> f o", o=1))
                load(s.fcw[:, :], g.fcW)
                load(s.fcb[:, :], g.fcb.rearrange("(k o) -> k o", o=1))
                load(avc[:, :], g.av.rearrange("(k o) -> k o", o=1))
                load(wout[:, :, :], g.W_out.rearrange("(h k) f -> k h f", k=HID))
                load(s.bh[:, :], g.bh.rearrange("h k -> k h"), slow=True)
                load(s.bout[:, :], g.b_out.rearrange("(o f) -> o f", o=1).broadcast_to([P, F]))
                for t in range(NT):
                    sp.dma_start(adj[:, t, :], g.adj[t * P:(t + 1) * P, :]).then_inc(loaded_adj[t], 16)

            @block.gpsimd
            def _(pool):
                nc.gpsimd.memset(s.ident[:, :], 0.0).then_inc(zeroed, 1)
                pool.wait_ge(zeroed, 1)
                nc.gpsimd.affine_select(out=s.ident[:, :], in_=s.ident[:, :], compare_op=ALU.not_equal, fill=1.0,
                                        base=0, pattern=[[-1, P]], channel_multiplier=1).then_inc(ident_ready, 1)
                nc.gpsimd.memset(s.ones[:, :], 1.0).then_inc(zeroed, 1)
                nc.gpsimd.memset(ones16[:, :], 1.0).then_inc(zeroed, 1)
                pool.wait_ge(x_hi_ready, 1)
                nc.gpsimd.tensor_tensor(x_lo[:, :, :, :], s.X[:, :, :].rearrange("p (b t) f -> p t b f", b=B), x_hi[:, :, :, :],
                                        ALU.subtract).then_inc(x_lo_ready, 1)

            @block.vector
            def _(dve):
                dve.wait_ge(ident_ready, 1)
                nc.vector.tensor_copy(s.ident16[:, :], s.ident[:, :]).then_inc(stacked, 1)
                nc.vector.tensor_tensor(s.twice[:, :], s.ident[:, 0:F], s.ident[:, F:P], ALU.add).then_inc(stacked, 1)
                dve.wait_ge(stacked, 2)
                nc.vector.tensor_copy(
                    s.pick[:, :, :, :],
                    s.twice[:, :].rearrange("p (j k) -> p k j", j=2).unsqueeze(3).broadcast_to([P, K2, 2, F])).then_inc(stacked, 1)
                dve.wait_ge(loaded_x, 16)
                nc.vector.tensor_copy(x_hi[:, :, :, :], s.X[:, :, :].rearrange("p (b t) f -> p t b f", b=B)).then_inc(x_hi_ready, 1)
                dve.wait_ge(loaded_w, 16 * WEIGHTS)
                nc.vector.tensor_copy(s.w_hi[:, :, :], wh[:, :, :]).then_inc(wa_ready, 1)
                dve.wait_ge(wa_ready, 1)
                nc.vector.tensor_tensor(s.w_lo[:, :, :], wh[:, :, :], s.w_hi[:, :, :], ALU.subtract).then_inc(stacked, 1)
                nc.vector.tensor_copy(s.wout_hi[:, :, :], wout[:, :, :]).then_inc(wout_ready, 1)
                dve.wait_ge(wout_ready, 1)
                nc.vector.tensor_tensor(s.wout_lo[:, :, :], wout[:, :, :], s.wout_hi[:, :, :], ALU.subtract).then_inc(stacked, 1)
                nc.vector.tensor_copy(s.anode[:, :], cols[:, 0:1].broadcast_to([F, E])).then_inc(stacked, 1)
                nc.vector.tensor_copy(s.agn[:, :], cols[:, 1:2].broadcast_to([F, P])).then_inc(stacked, 1)
                nc.vector.tensor_copy(s.age[:, :], cols[:, 2:3]).then_inc(stacked, 1)
                nc.vector.tensor_copy(s.av[:, :], avc[:, 0:1].broadcast_to([P, P])).then_inc(stacked, 1)
                nc.vector.tensor_scalar(s.nav[:, :], avc[:, 0:1].broadcast_to([P, F]), -1.0, None, ALU.mult).then_inc(stacked, 1)
                nc.vector.tensor_scalar(s.off[:, :, :], hrow[:, :, :], 0.0, -OFF, ALU.is_le, ALU.mult).then_inc(mask_ready, 1)
                dve.wait_ge(whT_psum, 1)
                nc.vector.tensor_copy(whT[:, :, :, :],
                                      ps[:, 0, :].rearrange("p (h f) -> p h f", h=HEADS).unsqueeze(2).broadcast_to([P, HEADS, 2, F])
                                      ).then_inc(whT_ready, 1)
                dve.wait_ge(maskT_psum, 1)
                nc.vector.tensor_copy(s.offT[:, :], ps[0:E, 4:6, :].rearrange("p a n -> p (a n)")).then_inc(maskT_ready, 1)
                dve.wait_ge(gram_psum, 1)
                gp = ps[:, 1:3, :].rearrange("p a n -> p (a n)")
                nc.vector.tensor_copy(s.gram[:, :], gp).then_inc(gram_hi, 1)
                dve.wait_ge(gram_hi, 1)
                nc.vector.tensor_tensor(s.gram[F:P, :], gp[F:P, :], s.gram[F:P, :], ALU.subtract).then_inc(gram_hi, 1)
                for t in range(NT):
                    dve.wait_ge(loaded_adj[t], 16)
                    nc.vector.tensor_scalar(s.offgraph[:, t, :], adj[:, t, :], 0.0, -OFF, ALU.is_equal, ALU.mult).then_inc(stacked, 1)
                dve.wait_ge(deg_psum, 1)
                nc.vector.tensor_scalar(rdeg[:, :], ps[:, 4:6, :].rearrange("p a n -> p (a n)"), 1.0, None, ALU.max).then_inc(deg_floor, 1)
                dve.wait_ge(deg_floor, 1)
                nc.vector.reciprocal(rdeg[:, :], rdeg[:, :]).then_inc(rdeg_ready, 1)
                dve.wait_ge(rdeg_ready, 1)
                for c in range(B // 2):
                    dve.wait_ge(mean_psum, c + 1)
                    a = 2 * (c % 2)
                    nc.vector.tensor_tensor(s.meanT[:, c, :], ps[:, a:a + 2, :].rearrange("p a n -> p (a n)"), rdeg[:, :],
                                            ALU.mult).then_inc(mean_ready, 1)

            @block.scalar
            def _(act):
                for t in range(NT):
                    act.wait_ge(loaded_adj[t], 16)
                    nc.scalar.copy(adj16[:, t, :], adj[:, t, :]).then_inc(adj16_ready, 1)
                for m in range(NT):
                    act.wait_ge(adjT_psum, m + 1)
                    nc.scalar.copy(adjT[:, m, :].bitcast(F32), ps[:, 6 + m % 2, :]).then_inc(adjT_ready, 1)

            @block.tensor
            def _(pe):
                pe.wait_ge(ident_ready, 1)
                pe.wait_ge(loaded_w, 16 * WEIGHTS)
                for h in range(HEADS):
                    last = nc.tensor.transpose(ps[:, 0, h * F:(h + 1) * F], wh[0:F, h, :], s.ident[0:F, 0:F])
                last.then_inc(whT_psum, 1)
                pe.wait_ge(mask_ready, 1)
                for t in range(NT):
                    last = nc.tensor.transpose(ps[0:E, 4 + t // 4, (t % 4) * P:(t % 4 + 1) * P], s.off[:, t, :], s.ident[:, :])
                last.then_inc(maskT_psum, 1)
                pe.wait_ge(whT_ready, 1)
                for h in range(HEADS):
                    w = whT[:, h, :, :].rearrange("p j f -> p (j f)")
                    last = nc.tensor.matmul(ps[:, 1 + h // 4, (h % 4) * P:(h % 4 + 1) * P], w, w, start=True, stop=True)
                last.then_inc(gram_psum, 1)
                pe.wait_ge(adj16_ready, NT)
                for m in range(NT):
                    if m >= 2:
                        pe.wait_ge(adjT_ready, m - 1)
                    for t in range(NT):
                        last = nc.tensor.transpose(ps[:, 6 + m % 2, :].bitcast(F16)[:, t * P:(t + 1) * P], adj16[:, t, m * P:(m + 1) * P],
                                                   s.ident16[:, :])
                    last.then_inc(adjT_psum, 1)

                def columns(a, lhsT, m, start, stop):
                    for half in range(2):
                        last = nc.tensor.matmul(ps[:, a + half, :], lhsT, adjT[:, m, half * HALF:(half + 1) * HALF], start=start, stop=stop)
                    return last
                pe.wait_ge(maskT_ready, 1)
                pe.wait_ge(adjT_ready, NT)
                pe.wait_ge(zeroed, 3)
                for m in range(NT):
                    last = columns(4, ones16[:, :], m, m == 0, m == NT - 1)
                last.then_inc(deg_psum, 1)
                pe.wait_ge(gram_hi, 2)
                pe.wait_ge(x_lo_ready, 1)
                for c in range(B // 2):
                    if c >= 2:
                        pe.wait_ge(mean_ready, c - 1)
                    for m in range(NT):
                        columns(2 * (c % 2), x_hi[:, m, 2 * c:2 * c + 2, :].rearrange("p b f -> p (b f)"), m, m == 0, False)
                        last = columns(2 * (c % 2), x_lo[:, m, 2 * c:2 * c + 2, :].rearrange("p b f -> p (b f)"), m, False, m == NT - 1)
                    last.then_inc(mean_psum, 1)


def layer0(nc, s):
    with ExitStack() as ctx:
        def sb(name, shape, dt=F32):
            return ctx.enter_context(nc.sbuf_tensor(name, shape, dt))

        def sem(name):
            return ctx.enter_context(nc.semaphore(name))

        ps = ctx.enter_context(nc.psum_tensor("ps_layer0", [P, 8, HALF], F32))

        def banks(a, rows=P):
            return ps[0:rows, a:a + 2, :].rearrange("p a n -> p (a n)")

        GATES, COEFS, SUMS, MISC = 0, 2, 4, 6
        BUFS, BUFS_W = 4, 8
        LAG_W, LAG_MERGE, LAG_SUM = 3, 4, 6

        def merged_into(j):
            return j % 4 == 3


        h2T, bst, cst = sb("l0_hT_twice", [P, 2, N]), sb("l0_beta_stack", [P, 2, N], F16), sb("l0_c_stack", [P, 2, N], F16)
        aggc, nagg, glin = sb("l0_agg_cols", [P, 2, K2]), sb("l0_neg_agg_cols", [P, 2, K2]), sb("l0_linear", [F, 2, N])
        vb, rb = sb("l0_v_exp", [P, BUFS, N]), sb("l0_relu_w", [P, BUFS_W, N])
        xb, xT, h2 = sb("l0_x", [P, NT, F]), sb("l0_xT", [F, N]), sb("l0_h_twice", [P, NT, 2 * F])
        z, al, alT = sb("l0_node_score", [E, N]), sb("l0_alpha", [P, N]), sb("l0_alphaT", [P, NT, E])
        nmx, asum, arec = sb("l0_alpha_shift", [E, 1]), sb("l0_alpha_sum", [E, 1]), sb("l0_alpha_rec", [E, 1])
        agg, aggT, qh = sb("l0_agg", [E, F]), sb("l0_aggT_twice", [F, 2, E]), sb("l0_edge_gate", [P, 1])
        beta = sb("l0_beta", [P, N])
        r64, e64, ur, heT, thf = (sb("l0_relu", [F, E]), sb("l0_exp", [F, E]), sb("l0_u_plus_relu", [F, E]),
                                  sb("l0_heT", [F, E]), sb("l0_tanh", [P, E]))
        l2, cmx, csum, crec = sb("l0_logits", [P, NT, E]), sb("l0_c_max", [P, NT]), sb("l0_c_sum", [P, NT]), sb("l0_c_rec", [P, NT])
        cd, cT, cob = sb("l0_c_twice", [P, NT, 2, E]), sb("l0_cT_twice", [P, N]), sb("l0_c_rest", [E, N])
        cb = z
        mb, gT, iT = sb("l0_mean", [F, N]), sb("l0_gT", [F, N]), sb("l0_indT", [F, N])
        t1, t2, sg = al, h2[:, :, :].rearrange("p t f -> p (t f)"), xT

        gate_ps, gated, relu_rdy, exp_rdy, added, coef_ps, weighted, merged, summed = (
            sem(n) for n in ("gate_ps", "gated", "relu_rdy", "exp_rdy", "added", "coef_ps", "weighted", "merged", "summed"))
        names = ("xb_rdy mean_rdy leaked sh_rdy al_exp arec_rdy al_rdy aggc_rdy r_rdy e_rdy ur_rdy he_rdy "
                 "be_rdy bhi_rdy bst_rdy l2m l2c l2_exp l2s l2r cd_rdy chi_rdy cst_rdy cb_rdy cob_rdy "
                 "gT_rdy df_rdy dfs_rdy o_rdy").split()
        S = {n: sem("l0_" + n) for n in names}
        misc_full, misc_free = sem("l0_misc_full"), sem("l0_misc_free")
        PREP = "xT h2T s h2 alT agg q fc se p cT cbB".split()
        TAIL = "ind fg fi d oT".split()
        BOTH = "ind xT h2T s h2 alT agg q fg fc fi se d p oT cT cbB".split()

        class Phase:

            def __init__(self, b, pair, par, base, run=True, prev=True, prep=True, tail=True):
                self.b, self.pair, self.par, self.base, self.run, self.prev, self.prep, self.tail = b, pair, par, base, run, prev, prep, tail
                order = BOTH if prep and tail else PREP if prep else TAIL
                self.use = {name: base + i for i, name in enumerate(order)}

            def lagging(self, k, lag):
                if k >= lag:
                    return (k - lag, self.b, self.par) if self.run else None
                return (k - lag + K2, self.b - 1, 1 - self.par) if self.prev else None

            def reused(self, k, bufs):
                return self.prev or k >= bufs

        def in_order(eng, slot):
            def phase(ph):
                for k in range(K2):
                    slot(ph, k)

            def base(b):
                return (len(PREP) - len(TAIL)) + len(BOTH) * b

            phase(Phase(-1, None, 1, 0, run=False, prev=False, tail=False))
            phase(Phase(0, 0, 0, len(PREP), prev=False, tail=False))
            with eng.Fori(0, B // 2 - 1) as two:
                phase(Phase(2 * two + 1, two, 1, len(BOTH) * 2 * two + base(1)))
                phase(Phase(2 * two + 2, two + 1, 0, len(BOTH) * 2 * two + base(2)))
            phase(Phase(B - 1, B // 2 - 1, 1, base(B - 1), prep=False))
            phase(Phase(B, None, 0, base(B - 1) + len(TAIL), run=False, prep=False))

        with nc.Block() as block:
            @block.sync
            def _(sp):
                def fetch_x(n):
                    sp.dma_start(xb[:, :, :], s.X[:, bass.ds(n * NT, NT), :]).then_inc(S["xb_rdy"], 16)

                def slot(ph, k):
                    if ph.prep and k == 0:
                        if ph.run:
                            sp.wait_ge(misc_full, ph.base)
                        fetch_x(ph.b + 1)
                    if ph.run and k == 12:
                        if ph.tail:
                            sp.wait_ge(misc_full, ph.use["ind"] + 1)
                        rows = slice(ph.par * F, ph.par * F + F)
                        sp.dma_start(mb[:, :], s.meanT[rows, bass.ds(ph.pair, 1), :].rearrange("p o n -> p (o n)")).then_inc(S["mean_rdy"], 16)

                in_order(sp, slot)

            @block.gpsimd
            def _(pool):
                def slot(ph, k):
                    i = K2 * ph.b + k
                    late = ph.lagging(k, LAG_MERGE)
                    if late and merged_into(late[0]):
                        j, b, _ = late
                        pool.wait_ge(weighted, K2 * b + j + 1)
                        w = rb[:, j % BUFS_W, :]
                        nc.gpsimd.tensor_tensor(w, w, rb[:, (j - 1) % BUFS_W, :], ALU.add).then_inc(merged, 1)
                    if ph.run:
                        pool.wait_ge(exp_rdy, i + 1)
                        r = rb[:, k % BUFS_W, :]
                        nc.gpsimd.tensor_tensor(r, r, vb[:, k % BUFS, :], ALU.add).then_inc(added, 1)

                in_order(pool, slot)

            @block.scalar
            def _(act):
                def slot(ph, k):
                    b, use, i = ph.b, ph.use, K2 * ph.b + k
                    if ph.run:
                        v, r = vb[:, k % BUFS, :], rb[:, k % BUFS_W, :]
                        act.wait_ge(gated, i + 1)
                        if ph.reused(k, BUFS_W):
                            act.wait_ge(summed, i - BUFS_W + 1)
                        nc.scalar.activation(r, v, ACT.Relu, bias=nagg[:, ph.par, k:k + 1], scale=-1.0).then_inc(relu_rdy, 1)
                        act.wait_ge(relu_rdy, i + 1)
                        nc.scalar.activation(v, r, ACT.Exp, scale=-1.0).then_inc(exp_rdy, 1)

                    def full(name):
                        act.wait_ge(misc_full, use[name] + 1)

                    if ph.tail:
                        if k == 0:
                            full("ind")
                            nc.scalar.copy(iT[:, :], banks(MISC, F)).then_inc(misc_free, 1)
                        if k == 16:
                            full("fi")
                            nc.scalar.activation(t1[:, :], banks(MISC), ACT.Tanh, bias=s.fcb[:, 0:1]).then_inc(misc_free, 1)
                        if k == 14:
                            full("fg")
                            nc.scalar.activation(t2[:, :], banks(MISC), ACT.Tanh, bias=s.fcb[:, 0:1]).then_inc(misc_free, 1)
                        if k == 20:
                            full("d")
                            nc.scalar.activation(sg[:, :], banks(MISC, F), ACT.Tanh, scale=0.5).then_inc(misc_free, 1)
                    if ph.prep:
                        if k == 2:
                            full("xT")
                            nc.scalar.copy(xT[:, :], banks(MISC, F)).then_inc(misc_free, 1)
                        if k == 4:
                            full("h2T")
                            nc.scalar.copy(h2T[:, 1 - ph.par, :], banks(MISC)).then_inc(misc_free, 1)
                        if k == 5:
                            full("s")
                            nc.scalar.copy(z[:, :], banks(MISC, E)).then_inc(misc_free, 1)
                        if k == 7:
                            full("h2")
                            nc.scalar.copy(h2[:, :, :].rearrange("p t f -> p (t f)"), banks(MISC)).then_inc(misc_free, 1)
                        if k == 8:
                            act.wait_ge(S["sh_rdy"], b + 2)
                            nc.scalar.activation(al[0:E, :], al[0:E, :], ACT.Exp, bias=nmx[:, 0:1], scale=-1.0,
                                                 accum_out=asum[:, 0:1]).then_inc(S["al_exp"], 1)
                        if k == 9:
                            act.wait_ge(S["arec_rdy"], b + 2)
                            nc.scalar.activation(al[0:E, :], al[0:E, :], ACT.Copy, scale=arec[:, 0:1]).then_inc(S["al_rdy"], 1)
                        if k == 13:
                            act.wait_ge(misc_free, use["agg"] + 1)
                            nc.scalar.activation(r64[:, :], aggT[:, 0, :], ACT.Relu, scale=-1.0).then_inc(S["r_rdy"], 1)
                            act.wait_ge(S["r_rdy"], b + 2)
                            nc.scalar.activation(e64[:, :], r64[:, :], ACT.Exp, scale=-1.0).then_inc(S["e_rdy"], 1)
                        if k == 15:
                            full("fc")
                            nc.scalar.activation(thf[:, :], ps[:, MISC, 0:E], ACT.Tanh, bias=s.fcb[:, 0:1]).then_inc(misc_free, 1)
                        if k == 22:
                            full("p")
                            nc.scalar.activation(beta[:, :], banks(MISC), ACT.Tanh, bias=qh[:, 0:1], scale=0.5).then_inc(misc_free, 1)
                        if k == 19:
                            act.wait_ge(S["l2c"], b + 2)
                            nc.scalar.activation(l2[:, :, :], l2[:, :, :], ACT.Exp).then_inc(S["l2_exp"], 1)
                        if k == 24:
                            act.wait_ge(S["be_rdy"], b + 2)
                            nc.scalar.copy(bst[:, 1 - ph.par, :], beta[:, :]).then_inc(S["bhi_rdy"], 1)
                        if k == 25:
                            full("cT")
                            nc.scalar.copy(cT[:, :], banks(MISC)).then_inc(misc_free, 1)
                        if k == 26:
                            act.wait_ge(misc_free, use["cT"] + 1)
                            nc.scalar.copy(cst[:, 1 - ph.par, :], cT[:, :]).then_inc(S["chi_rdy"], 1)

                in_order(act, slot)

            @block.vector
            def _(dve):
                def slot(ph, k):
                    b, use, i = ph.b, ph.use, K2 * ph.b + k
                    if ph.run:
                        dve.wait_ge(gate_ps, i + 1)
                        if ph.reused(k, BUFS):
                            dve.wait_ge(added, i - BUFS + 1)
                        nc.vector.scalar_tensor_tensor(out=vb[:, k % BUFS, :], in0=h2T[:, ph.par, :], scalar=aggc[:, ph.par, k:k + 1],
                                                       in1=banks(GATES), op0=ALU.subtract, op1=ALU.mult).then_inc(gated, 1)
                    late = ph.lagging(k, LAG_W)
                    if late:
                        j, b_late, _ = late
                        dve.wait_ge(coef_ps, K2 * b_late + j + 1)
                        dve.wait_ge(added, K2 * b_late + j + 1)
                        nc.vector.tensor_tensor(rb[:, j % BUFS_W, :], rb[:, j % BUFS_W, :], banks(COEFS), ALU.mult).then_inc(weighted, 1)
                    if ph.prev and k == LAG_SUM - 1:
                        dve.wait_ge(summed, K2 * b)
                        nc.vector.scalar_tensor_tensor(out=gT[:, :], in0=banks(SUMS, F), scalar=-1.0, in1=glin[:, 1 - ph.par, :],
                                                       op0=ALU.add, op1=ALU.add).then_inc(S["gT_rdy"], 1)
                    if ph.tail:
                        finish(ph, k)
                    if ph.prep:
                        prepare(ph, k)

                def finish(ph, k):
                    b, use = ph.b, ph.use
                    if k == 17:
                        dve.wait_ge(S["gT_rdy"], b)
                        dve.wait_ge(misc_full, use["fi"] + 1)
                        nc.vector.tensor_tensor(iT[:, :], iT[:, :], gT[:, :], ALU.subtract).then_inc(S["df_rdy"], 1)
                    if k == 22:
                        dve.wait_ge(misc_free, use["d"] + 1)
                        dve.wait_ge(S["df_rdy"], b)
                        nc.vector.scalar_tensor_tensor(out=sg[:, :], in0=sg[:, :], scalar=1.0, in1=iT[:, :], op0=ALU.add,
                                                       op1=ALU.mult).then_inc(S["dfs_rdy"], 1)
                    if k == 23:
                        dve.wait_ge(S["dfs_rdy"], b)
                        nc.vector.scalar_tensor_tensor(out=sg[:, :], in0=sg[:, :], scalar=0.5, in1=gT[:, :], op0=ALU.mult,
                                                       op1=ALU.add).then_inc(S["o_rdy"], 1)
                    if k == 24:
                        dve.wait_ge(misc_full, use["oT"] + 1)
                        rows = s.X[:, bass.ds((b - 1) * NT, NT), :]
                        nc.vector.tensor_tensor(rows, ps[:, MISC, :].rearrange("p (t f) -> p t f", t=NT), rows, ALU.add).then_inc(misc_free, 1)

                def prepare(ph, k):
                    b, use, nxt = ph.b, ph.use, 1 - ph.par

                    def step(name):
                        dve.wait_ge(S[name], b + 2)

                    def full(name):
                        dve.wait_ge(misc_full, use[name] + 1)

                    if k == 6:
                        dve.wait_ge(misc_free, use["s"] + 1)
                        nc.vector.scalar_tensor_tensor(out=z[:, :], in0=z[:, :], scalar=0.2, in1=z[:, :], op0=ALU.mult,
                                                       op1=ALU.max).then_inc(S["leaked"], 1)
                    if k == 7:
                        step("leaked")
                        dve.nop(nofuse=True)
                        nc.vector.tensor_tensor_reduce(al[0:E, :], z[:, :], s.offT[:, :], -1.0, BIG, ALU.add, ALU.min,
                                                       nmx[:, 0:1]).then_inc(S["sh_rdy"], 1)
                    if k == 9:
                        step("al_exp")
                        nc.vector.reciprocal(arec[:, :], asum[:, :]).then_inc(S["arec_rdy"], 1)
                    if k == 11:
                        full("alT")
                        nc.vector.tensor_copy(alT[:, :, :].rearrange("p t e -> p (t e)"), ps[:, MISC, :]).then_inc(misc_free, 1)
                    if k == 12:
                        full("agg")
                        nc.vector.tensor_copy(aggc[0:F, nxt, :], ps[0:F, MISC + 1, 0:K2])
                        nc.vector.tensor_copy(aggc[F:P, nxt, :], ps[F:P, MISC + 1, K2:E]).then_inc(S["aggc_rdy"], 1)
                        nc.vector.tensor_copy(aggT[:, :, :], ps[0:F, MISC + 1, 0:E].unsqueeze(1).broadcast_to([F, 2, E])).then_inc(misc_free, 1)
                        step("aggc_rdy")
                        nc.vector.tensor_scalar(nagg[:, nxt, :], aggc[:, nxt, :], -1.0, None, ALU.mult)
                    if k == 13:
                        full("q")
                        nc.vector.tensor_copy(agg[:, :], ps[0:E, MISC + 1, 0:F])
                        nc.vector.tensor_scalar(qh[:, :], ps[:, MISC, 0:1], 0.5, None, ALU.mult).then_inc(misc_free, 1)
                    if k == 14:
                        step("e_rdy")
                        nc.vector.tensor_tensor(ur[:, :], aggT[:, 0, :], r64[:, :], ALU.add).then_inc(S["ur_rdy"], 1)
                        step("ur_rdy")
                        nc.vector.scalar_tensor_tensor(out=heT[:, :], in0=e64[:, :], scalar=-1.0, in1=ur[:, :], op0=ALU.add,
                                                       op1=ALU.add).then_inc(S["he_rdy"], 1)
                    if k == 18:
                        full("se")
                        nc.vector.tensor_tensor(l2[:, :, :], ps[:, MISC, 0:E].unsqueeze(1).broadcast_to([P, NT, E]), s.off[:, :, :],
                                                ALU.add).then_inc(misc_free, 1)
                        dve.wait_ge(misc_free, use["se"] + 1)
                        nc.vector.tensor_reduce(cmx[:, :], l2[:, :, :], AX.X, ALU.max).then_inc(S["l2m"], 1)
                    if k == 19:
                        step("l2m")
                        nc.vector.tensor_tensor(l2[:, :, :], l2[:, :, :], cmx[:, :].unsqueeze(2).broadcast_to([P, NT, E]),
                                                ALU.subtract).then_inc(S["l2c"], 1)
                    if k == 24:
                        dve.wait_ge(misc_free, use["p"] + 1)
                        nc.vector.tensor_scalar(beta[:, :], beta[:, :], 0.5, 0.5, ALU.mult, ALU.add).then_inc(S["be_rdy"], 1)
                    if k == 20:
                        step("l2_exp")
                        nc.vector.tensor_reduce(csum[:, :], l2[:, :, :], AX.X, ALU.add).then_inc(S["l2s"], 1)
                        step("l2s")
                        nc.vector.reciprocal(crec[:, :], csum[:, :]).then_inc(S["l2r"], 1)
                        step("l2r")
                        nc.vector.tensor_tensor(cd[:, :, 0, :], l2[:, :, :], crec[:, :].unsqueeze(2).broadcast_to([P, NT, E]), ALU.mult)
                    if k == 21:
                        nc.vector.tensor_tensor(cd[:, :, 1, :], l2[:, :, :], crec[:, :].unsqueeze(2).broadcast_to([P, NT, E]),
                                                ALU.mult).then_inc(S["cd_rdy"], 1)
                    if k == 25:
                        step("bhi_rdy")
                        nc.vector.tensor_tensor(bst[F:P, nxt, :], beta[F:P, :], bst[F:P, nxt, :], ALU.subtract).then_inc(S["bst_rdy"], 1)
                    if k == 26:
                        dve.wait_ge(misc_free, use["cT"] + 1)
                        nc.vector.tensor_tensor(cb[:, :], cT[0:E, :], beta[0:E, :], ALU.mult).then_inc(S["cb_rdy"], 1)
                    if k == 29:
                        step("cb_rdy")
                        nc.vector.tensor_tensor(cob[:, :], cT[0:E, :], cb[:, :], ALU.subtract).then_inc(S["cob_rdy"], 1)
                    if k == 27:
                        step("chi_rdy")
                        nc.vector.tensor_tensor(cst[F:P, nxt, :], cT[F:P, :], cst[F:P, nxt, :], ALU.subtract).then_inc(S["cst_rdy"], 1)
                    if k == 28:
                        full("cbB")
                        nc.vector.tensor_tensor(glin[:, nxt, :], banks(MISC, F), h2T[0:F, nxt, :], ALU.mult).then_inc(misc_free, 1)

                in_order(dve, slot)

            @block.tensor
            def _(pe):
                def wide(bank, lhsT, rhs, start=True, stop=True, rows=P):
                    for half in range(2):
                        last = nc.tensor.matmul(ps[0:rows, bank + half, :], lhsT, rhs[:, half * HALF:(half + 1) * HALF],
                                                start=start, stop=stop)
                    return last

                def pick(k):
                    return s.pick[:, k, :, :].rearrange("p j f -> p (j f)")

                def slot(ph, k):
                    b, i = ph.b, K2 * ph.b + k
                    if ph.run:
                        if k == 0:
                            pe.wait_ge(S["bst_rdy"], b + 1)
                        if not (isinstance(i, int) and i == 0):
                            pe.wait_ge(gated, i)
                        wide(GATES, pick(k), bst[:, ph.par, :]).then_inc(gate_ps, 1)
                    late = ph.lagging(k, LAG_W)
                    if late:
                        j, b_late, par = late
                        if j == 0:
                            pe.wait_ge(S["cst_rdy"], b + 1)
                        if j > 0 or ph.prev:
                            pe.wait_ge(weighted, K2 * b_late + j)
                        wide(COEFS, pick(j), cst[:, par, :]).then_inc(coef_ps, 1)
                    late = ph.lagging(k, LAG_SUM)
                    if late:
                        j, b_late, _ = late
                        if j == 0:
                            if ph.prev:
                                pe.wait_ge(S["gT_rdy"], b)
                        if merged_into(j):
                            pe.wait_ge(merged, K2 // 4 * b_late + j // 4 + 1)
                        else:
                            pe.wait_ge(weighted, K2 * b_late + j + 1)
                        if not merged_into(j + 1):
                            wide(SUMS, s.twice[:, :], rb[:, j % BUFS_W, :], start=(j == 0), stop=(j == K2 - 1), rows=F
                                 ).then_inc(summed, 2 if merged_into(j) else 1)
                    if ph.run and k == 8:
                        pe.wait_ge(S["cob_rdy"], b + 1)
                        pe.nop(nofuse=True)
                        wide(SUMS, agg[:, :], cob[:, :], start=False, stop=False, rows=F)
                    if ph.tail:
                        finish(ph, k)
                    if ph.prep:
                        prepare(ph, k)

                def freed(ph, name):
                    use = ph.use[name]
                    if not (isinstance(use, int) and use == 0):
                        pe.wait_ge(misc_free, use)
                    pe.nop(nofuse=True)

                def transposed(source):
                    for t in range(NT):
                        last = nc.tensor.transpose(ps[0:F, MISC + t // 4, (t % 4) * P:(t % 4 + 1) * P], source[:, t, :], s.ident[:, :])
                    last.then_inc(misc_full, 1)

                def finish(ph, k):
                    b = ph.b
                    if k == 0:
                        pe.wait_ge(S["mean_rdy"], 16 * b)
                        freed(ph, "ind")
                        wide(MISC, s.wind[:, :], mb[:, :], rows=F).then_inc(misc_full, 1)
                    if k == 16:
                        freed(ph, "fi")
                        wide(MISC, s.fcw[:, :], iT[:, :]).then_inc(misc_full, 1)
                    if k == 14:
                        pe.wait_ge(S["gT_rdy"], b)
                        freed(ph, "fg")
                        wide(MISC, s.fcw[:, :], gT[:, :]).then_inc(misc_full, 1)
                    if k == 20:
                        freed(ph, "d")
                        for half in range(2):
                            cols = slice(half * HALF, (half + 1) * HALF)
                            nc.tensor.matmul(ps[0:F, MISC + half, :], s.av[:, 0:F], t1[:, cols], start=True, stop=False)
                            last = nc.tensor.matmul(ps[0:F, MISC + half, :], s.nav[:, :], t2[:, cols], start=False, stop=True)
                        last.then_inc(misc_full, 1)
                    if k == 24:
                        pe.wait_ge(S["o_rdy"], b)
                        freed(ph, "oT")
                        for t in range(NT):
                            last = nc.tensor.transpose(ps[:, MISC, t * F:(t + 1) * F], sg[:, t * P:(t + 1) * P], s.ident[0:F, 0:F])
                        last.then_inc(misc_full, 1)

                def prepare(ph, k):
                    b, nxt = ph.b, 1 - ph.par

                    def step(name):
                        pe.wait_ge(S[name], b + 2)

                    if k == 2:
                        pe.wait_ge(S["xb_rdy"], 16 * (b + 2))
                        freed(ph, "xT")
                        transposed(xb)
                    if k == 4:
                        freed(ph, "h2T")
                        wide(MISC, s.w2[:, :], xT[:, :]).then_inc(misc_full, 1)
                    if k == 5:
                        freed(ph, "s")
                        wide(MISC, s.anode[:, :], h2T[0:F, nxt, :], rows=E).then_inc(misc_full, 1)
                    if k == 7:
                        freed(ph, "h2")
                        for t in range(NT):
                            last = nc.tensor.matmul(ps[:, MISC + t // 4, (t % 4) * P:(t % 4 + 1) * P], xT[:, t * P:(t + 1) * P],
                                                    s.w2[:, :], start=True, stop=True)
                        last.then_inc(misc_full, 1)
                    if k == 11:
                        step("al_rdy")
                        freed(ph, "alT")
                        for t in range(NT):
                            last = nc.tensor.transpose(ps[:, MISC, t * E:(t + 1) * E], al[0:E, t * P:(t + 1) * P], s.ident[0:E, 0:E])
                        last.then_inc(misc_full, 1)
                    if k == 12:
                        freed(ph, "agg")
                        for t in range(NT):
                            last = nc.tensor.matmul(ps[:, MISC + 1, 0:E], h2[:, t, :], alT[:, t, :], start=(t == 0), stop=(t == NT - 1))
                        last.then_inc(misc_full, 1)
                    if k == 13:
                        freed(ph, "q")
                        nc.tensor.transpose(ps[0:E, MISC + 1, 0:F], aggT[:, 0, :], s.ident[0:F, 0:F])
                        nc.tensor.matmul(ps[:, MISC, 0:1], aggT[:, :, :].rearrange("p j e -> p (j e)"), s.age[:, :], start=True,
                                         stop=True).then_inc(misc_full, 1)
                    if k == 15:
                        step("he_rdy")
                        freed(ph, "fc")
                        nc.tensor.matmul(ps[:, MISC, 0:E], s.fcw[:, :], heT[:, :], start=True, stop=True).then_inc(misc_full, 1)
                    if k == 18:
                        freed(ph, "se")
                        nc.tensor.matmul(ps[:, MISC, 0:E], s.av[:, :], thf[:, :], start=True, stop=True).then_inc(misc_full, 1)
                    if k == 22:
                        freed(ph, "p")
                        wide(MISC, s.agn[:, :], h2T[0:F, nxt, :]).then_inc(misc_full, 1)
                    if k == 25:
                        step("cd_rdy")
                        freed(ph, "cT")
                        for t in range(NT):
                            last = nc.tensor.transpose(ps[:, MISC + t // 4, (t % 4) * P:(t % 4 + 1) * P],
                                                       cd[:, t, :, :].rearrange("p j e -> p (j e)"), s.ident[:, :])
                        last.then_inc(misc_full, 1)
                    if k == 27:
                        step("cb_rdy")
                        freed(ph, "cbB")
                        wide(MISC, s.ones[0:E, 0:F], cb[:, :], rows=F).then_inc(misc_full, 1)

                in_order(pe, slot)


def norm(nc, s, name):
    with ExitStack() as ctx:
        def sb(n, shape, dt=F32):
            return ctx.enter_context(nc.sbuf_tensor(f"{name}_{n}", shape, dt))

        def sem(n):
            return ctx.enter_context(nc.semaphore(f"{name}_{n}"))

        T = B * NT
        sq, mean, var, root, rec = sb("squares", [P, T, F]), sb("mean", [P, T]), sb("var", [P, T]), sb("root", [P, T]), sb("rec", [P, T])
        summed, meaned, centred, squared, square_sum, shifted, rooted, inverted, normed = (
            sem(n) for n in ("summed", "meaned", "centred", "squared", "square_sum", "shifted", "rooted", "inverted", "normed"))

        def over_f(a):
            return a[:, :].unsqueeze(2).broadcast_to([P, T, F])

        with nc.Block() as block:
            @block.vector
            def _(dve):
                nc.vector.tensor_reduce(mean[:, :], s.X[:, :, :], AX.X, ALU.add).then_inc(summed, 1)
                dve.wait_ge(summed, 1)
                nc.vector.tensor_scalar(mean[:, :], mean[:, :], 1.0 / F, None, ALU.mult).then_inc(meaned, 1)
                dve.wait_ge(meaned, 1)
                nc.vector.tensor_tensor(s.X[:, :, :], s.X[:, :, :], over_f(mean), ALU.subtract).then_inc(centred, 1)
                dve.wait_ge(squared, 1)
                nc.vector.tensor_reduce(var[:, :], sq[:, :, :], AX.X, ALU.add).then_inc(square_sum, 1)
                dve.wait_ge(square_sum, 1)
                nc.vector.tensor_scalar(var[:, :], var[:, :], 1.0 / F, EPS, ALU.mult, ALU.add).then_inc(shifted, 1)
                dve.wait_ge(rooted, 1)
                nc.vector.reciprocal(rec[:, :], root[:, :]).then_inc(inverted, 1)
                dve.wait_ge(inverted, 1)
                nc.vector.tensor_tensor(s.X[:, :, :], s.X[:, :, :], over_f(rec), ALU.mult).then_inc(normed, 1)

            @block.scalar
            def _(act):
                act.wait_ge(centred, 1)
                nc.scalar.activation(sq[:, :, :], s.X[:, :, :], ACT.Square).then_inc(squared, 1)
                act.wait_ge(shifted, 1)
                nc.scalar.activation(root[:, :], var[:, :], ACT.Sqrt).then_inc(rooted, 1)


def layer1(nc, s, out):
    with ExitStack() as ctx:
        def sb(name, shape, dt=F32):
            return ctx.enter_context(nc.sbuf_tensor(name, shape, dt))

        def pb(name, shape, dt=F32):
            return ctx.enter_context(nc.psum_tensor(name, shape, dt))

        def sem(name):
            return ctx.enter_context(nc.semaphore(name))

        ps_s, ps_t, acc, misc = pb("ps_scores", [P, 2, N]), pb("ps_probsT", [P, 2, HALF]), pb("ps_acc", [P, HALF]), pb("ps_misc", [P, HALF])
        misc16 = misc[:, :].bitcast(F16)
        tb, pbuf = sb("l1_scores", [P, 4, N]), sb("l1_probs", [P, 4, N])
        ph, pl = sb("l1_probs_hi", [P, 4, N], F16), sb("l1_probs_lo", [P, 4, N], F16)
        phT, plT = sb("l1_probsT_hi", [P, 2, N], F16), sb("l1_probsT_lo", [P, 4, N], F16)
        nm, rs, rr = sb("l1_shift", [P, 4]), sb("l1_sums", [P, 3, NT]), sb("l1_rec", [P, NT])
        zf, zs, zT = sb("l1_z", [P, NT, F]), sb("l1_z_split", [P, NT, 2, F], F16), sb("l1_zT", [P, N], F16)
        cv, catf, ob = sb("l1_head_out", [P, 2, HALF]), sb("l1_cat_part", [P, 2, HALF]), sb("l1_out", [P, NT, F])
        cat = [sb("l1_cat_hi", [P, HEADS, N], F16), sb("l1_cat_lo", [P, HEADS, N], F16)]

        def cat_part(c, h, half):
            return cat[c][:, bass.ds(h, 1), half * HALF:(half + 1) * HALF].rearrange("p o n -> p (o n)")

        class Source:

            def __init__(self, features, y, sums):
                self.xs, self.xh, self.xl = features
                self.y, self.sums = y, sums

        def features(name):
            return sb(f"l1_{name}_split", [P, 2, NT, 2, F], F16), sb(f"l1_{name}_hi", [P, N], F16), sb(f"l1_{name}_lo", [P, N], F16)

        of_x = features("x")
        head = [Source(of_x, sb(f"l1_y{p}", [P, N], F16), rs[:, p, :]) for p in range(2)]
        output = Source(features("h2"), sb("l1_y_out", [P, N], F16), rs[:, 2, :])

        (scored, masked, exped, hi_done, lo_done, turned, kept, mixed) = (
            sem(n) for n in ("scored", "masked", "exped", "hi_done", "lo_done", "turned", "kept", "mixed"))
        lo_turned = [sem("lo_turned_even"), sem("lo_turned_odd")]
        misc_full, misc_free, y_hi, cat_ready = (sem(n) for n in ("misc_full", "misc_free", "y_hi", "cat_ready"))
        x_hi, x_split, z_rec, z_ready, z_hi, z_split = (sem(n) for n in ("x_hi", "x_split", "z_rec", "z_ready", "z_hi", "z_split"))
        cat_split = sem("cat_split")
        n_sum, n_mean, n_centred, n_squared, n_var, n_shift, n_root, n_inverse, normed, stored = (
            sem("out_" + n) for n in ("sum", "mean", "centred", "squared", "var", "shift", "root", "inverse", "normed", "stored"))
        mean, var, var_all = sb("l1_mean", [P, NT]), sb("l1_var", [P, NT]), sb("l1_var_all", [P, B * NT])
        h2_hi, y_out, o_bias, o_leak, out_added = (sem(n) for n in ("h2_hi", "y_out", "o_bias", "o_leak", "out_added"))

        def is_0(b):
            return isinstance(b, int) and b == 0

        def first_q(b):
            return 0 if is_0(b) else 9 * b - 1

        def use_base(b):
            return 0 if is_0(b) else 45 * b + 1

        def use_head(b, h):
            return use_base(b) + (6 if is_0(b) else 3) + 5 * (h - 1)

        def use_switch(b):
            return use_head(b, 7) + (3 if is_0(b) else 5)

        USE_END = use_switch(B - 1) + 3

        def reused(i, buffers):
            return not (isinstance(i, int) and i < buffers)

        def turns(q, t, earlier=0):
            return 16 * (4 * q + (t - earlier) // 2 + 1)

        def in_order(eng, steps):
            def batch(b, after_out, has_next):
                q = first_q(b)
                steps.head_0(b, q, after_out)
                with eng.Fori(0, HEADS // 2 - 1) as pair:
                    for j in range(2):
                        steps.head_h(b, q + 2 * pair + 1 + j, 2 * pair + 1 + j, 1 - j)
                steps.head_7(b, q + 7)
                if is_0(b):
                    steps.switch(b, q + 8)
                else:
                    steps.out(b, q + 8, has_next)

            steps.start()
            batch(0, False, True)
            batch(1, False, True)
            with eng.Fori(2, B - 1) as b:
                batch(b, True, True)
            batch(B - 1, True, False)
            steps.end(first_q(B - 1) + 9)

        with nc.Block() as block:
            @block.sync
            def _(sp):
                def turn_lo(q, t):
                    i = NT * q + t
                    if reused(i, 2):
                        sp.wait_ge(lo_turned[t % 2], turns(q, t, 2))
                        sp.nop(nofuse=True)
                    if reused(i, 4):
                        sp.wait_ge(mixed, i - 3)
                        sp.nop(nofuse=True)
                    sp.wait_ge(lo_done, i + 1)
                    sp.nop(nofuse=True)
                    sp.dma_start_transpose(plT[:, t % 4, :].rearrange("p (m n) -> p m n", n=P), pl[:, t % 4, :]).then_inc(lo_turned[t % 2], 16)

                def store(b):
                    sp.wait_ge(normed, b + 1)
                    sp.dma_start(out[b:b + 1, :, :].rearrange("b (t p) f -> p (b t) f", p=P), s.X[:, b * NT:(b + 1) * NT, :]).then_inc(stored, 16)

                def body(q, nxt, extra=lambda t: None):
                    for t in range(NT):
                        if t + 2 < NT:
                            turn_lo(q, t + 2)
                        elif nxt:
                            turn_lo(q + 1, t + 2 - NT)
                        extra(t)

                def first_two(q):
                    turn_lo(q, 0)
                    turn_lo(q, 1)

                class Steps:
                    def start(self):
                        first_two(0)

                    def head_0(self, b, q, after_out):
                        body(q, True)

                    def head_h(self, b, q, h, par):
                        body(q, True)

                    def head_7(self, b, q):
                        body(q, not is_0(b))

                    def out(self, b, q, has_next):
                        body(q, has_next)

                    def switch(self, b, q):
                        first_two(q)

                    def end(self, q):
                        first_two(q)
                        body(q, False)
                        for b in range(B):
                            store(b)

                in_order(sp, Steps())
                sp.wait_ge(stored, 16 * B)

            @block.tensor
            def _(pe):
                def score(q, src, t):
                    i = NT * q + t
                    if reused(i, 2):
                        pe.wait_ge(masked, i - 1)
                    rows = src.y[:, t * P:(t + 1) * P]
                    for half in range(2):
                        cols = slice(half * HALF, (half + 1) * HALF)
                        nc.tensor.matmul(ps_s[:, t % 2, cols], rows, src.xh[:, cols], start=True, stop=False)
                        last = nc.tensor.matmul(ps_s[:, t % 2, cols], rows, src.xl[:, cols], start=False, stop=True)
                    last.then_inc(scored, 1)

                def turn(q, t):
                    i = NT * q + t
                    if reused(i, 2):
                        pe.wait_ge(kept, i - 1)
                    pe.wait_ge(hi_done, i + 1)
                    for m in range(NT):
                        last = nc.tensor.transpose(ps_t[:, t % 2, :].bitcast(F16)[:, m * P:(m + 1) * P], ph[:, t % 4, m * P:(m + 1) * P],
                                                   s.ident16[:, :])
                    last.then_inc(turned, 1)

                def mix(q, src, t):
                    i = NT * q + t
                    pe.wait_ge(kept, i + 1)
                    pe.wait_ge(lo_turned[t % 2], turns(q, t))
                    for m in range(NT):
                        hi, lo = phT[:, t % 2, m * P:(m + 1) * P], plT[:, t % 4, m * P:(m + 1) * P]
                        to = acc[:, t * F:(t + 1) * F]
                        nc.tensor.matmul(to, hi, src.xs[:, 0, m, 0, :], start=(m == 0), stop=False)
                        nc.tensor.matmul(to, hi, src.xs[:, 1, m, 0, :], start=False, stop=False)
                        last = nc.tensor.matmul(to, lo, src.xs[:, 0, m, 0, :], start=False, stop=(m == NT - 1))
                    last.then_inc(mixed, 1)

                def keys(src, c, use):
                    if not (isinstance(use, int) and use == 0):
                        pe.wait_ge(misc_free, use)
                    for t in range(NT):
                        last = nc.tensor.transpose(misc16[:, t * P:(t + 1) * P], src.xs[:, c, t, :, :].rearrange("p j f -> p (j f)"),
                                                   s.ident16[:, :])
                    last.then_inc(misc_full, 1)

                def queries(h, half, use):
                    pe.wait_ge(misc_free, use)
                    gram = s.gram[:, bass.ds(h * P, P)]
                    cols = slice(half * HALF, (half + 1) * HALF)
                    nc.tensor.matmul(misc[:, :], gram, head[0].xh[:, cols], start=True, stop=False)
                    nc.tensor.matmul(misc[:, :], gram, head[0].xl[:, cols], start=False, stop=True).then_inc(misc_full, 1)

                def turn_z(n, use):
                    pe.wait_ge(z_split, n + 1)
                    pe.wait_ge(misc_free, use)
                    for t in range(NT):
                        last = nc.tensor.transpose(misc16[:, t * P:(t + 1) * P], zs[:, t, :, :].rearrange("p j f -> p (j f)"), s.ident16[:, :])
                    last.then_inc(misc_full, 1)

                def head_out(h, half, use):
                    pe.wait_ge(misc_free, use)
                    for w, first in ((s.w_hi, True), (s.w_lo, False)):
                        last = nc.tensor.matmul(misc[:, :], w[:, bass.ds(h, 1), :].rearrange("p o k -> p (o k)"),
                                                zT[:, half * HALF:(half + 1) * HALF], start=first, stop=not first)
                    last.then_inc(misc_full, 1)

                def h2(b, use, tiles):
                    if tiles[0] == 0:
                        pe.wait_ge(cat_split, 2 * HEADS * (b + 1) + 2)
                        pe.wait_ge(misc_free, use)
                    for t in tiles:
                        to = misc[:, t * F:(t + 1) * F]
                        for h in range(HEADS):
                            hi, lo = (c[:, h, t * P:(t + 1) * P] for c in cat)
                            nc.tensor.matmul(to, hi, s.wout_hi[:, h, :], start=(h == 0), stop=False)
                            nc.tensor.matmul(to, hi, s.wout_lo[:, h, :], start=False, stop=False)
                            last = nc.tensor.matmul(to, lo, s.wout_hi[:, h, :], start=False, stop=(h == HEADS - 1))
                    if tiles[-1] == NT - 1:
                        last.then_inc(misc_full, 1)

                def body(q, src, nxt, ready, prev, extra):
                    for t in range(NT):
                        turn(q, t)
                        if t + 3 < NT:
                            score(q, src, t + 3)
                        elif nxt is not None:
                            if t + 3 == NT:
                                pe.wait_ge(*ready)
                            score(q + 1, nxt, t + 3 - NT)
                        extra(t)
                        if t > 0:
                            if t == 1 and reused(q, 1):
                                pe.wait_ge(z_ready, q)
                            mix(q, src, t - 1)
                        elif prev is not None:
                            mix(q - 1, prev, NT - 1)

                class Steps:
                    def start(self):
                        pe.wait_ge(x_split, 1)
                        keys(head[0], 0, 0)
                        keys(head[0], 1, 1)
                        queries(0, 0, 2)
                        queries(0, 1, 3)
                        pe.wait_ge(misc_free, 4)
                        for t in range(3):
                            score(0, head[0], t)

                    def head_0(self, b, q, after_out):
                        use = use_base(b)

                        def extra(t):
                            if is_0(b) and t in (1, 2):
                                queries(1, t - 1, use + 3 + t)
                            if not is_0(b):
                                if t in (0, 1):
                                    queries(1, t, use + t)
                                if 2 <= t < 6:
                                    h2(b - 1, use + 2, (2 * t - 4, 2 * t - 3))
                        body(q, head[0], head[1], (misc_free, use + (6 if is_0(b) else 2)), output if after_out else None, extra)

                    def head_h(self, b, q, h, par):
                        use = use_head(b, h)

                        def extra(t):
                            if t in (1, 2):
                                queries(h + 1, t - 1, use + t - 1)
                            if t == 3:
                                turn_z(8 * b + h - 1, use + 2)
                            if t in (4, 5):
                                head_out(h - 1, t - 4, use + t - 1)
                        body(q, head[par], head[1 - par], (misc_free, use + 2), head[1 - par], extra)

                    def head_7(self, b, q):
                        use = use_head(b, 7)
                        last = use if is_0(b) else use + 2

                        def extra(t):
                            if not is_0(b) and t in (0, 1):
                                keys(output, t, use + t)
                            if t == 3:
                                turn_z(8 * b + 6, last)
                            if t in (4, 5):
                                head_out(6, t - 4, last + t - 3)
                        if is_0(b):
                            body(q, head[1], None, None, head[0], extra)
                        else:
                            body(q, head[1], output, (y_out, b), head[0], extra)

                    def out(self, b, q, has_next):
                        use = use_switch(b)

                        def extra(t):
                            if has_next:
                                if t in (1, 2):
                                    pe.wait_ge(x_hi if t == 1 else x_split, b + 2)
                                    keys(head[0], t - 1, use + t - 1)
                                if t in (3, 4):
                                    queries(0, t - 3, use + t - 1)
                            at = 5 if has_next else 3
                            last = use + (4 if has_next else 0)
                            if t == at:
                                turn_z(8 * b + 7, last)
                            if t in (6, 7):
                                head_out(7, t - 6, last + t - 5)
                        body(q, output, head[0] if has_next else None, (misc_free, use + 4), head[1], extra)

                    def switch(self, b, q):
                        use = use_switch(b)
                        mix(q - 1, head[1], NT - 1)
                        pe.wait_ge(x_split, b + 2)
                        keys(head[0], 0, use)
                        keys(head[0], 1, use + 1)
                        queries(0, 0, use + 2)
                        queries(0, 1, use + 3)
                        pe.wait_ge(misc_free, use + 4)
                        for t in range(3):
                            score(q, head[0], t)
                        turn_z(8 * b + 7, use + 4)
                        head_out(7, 0, use + 5)
                        head_out(7, 1, use + 6)

                    def end(self, q):
                        mix(q - 1, output, NT - 1)
                        h2(B - 1, USE_END, range(NT))
                        keys(output, 0, USE_END + 1)
                        keys(output, 1, USE_END + 2)
                        pe.wait_ge(y_out, B)
                        for t in range(3):
                            score(q, output, t)
                        body(q, output, None, None, None, lambda t: None)
                        mix(q, output, NT - 1)

                in_order(pe, Steps())

            @block.scalar
            def _(act):
                def expo(q, src, t):
                    i = NT * q + t
                    act.wait_ge(masked, i + 1)
                    if reused(i, 4):
                        act.wait_ge(lo_done, i - 3)
                    nc.scalar.activation(pbuf[:, t % 4, :], tb[:, t % 4, :], ACT.Exp, bias=nm[:, t % 4:t % 4 + 1], scale=-1.0,
                                         accum_out=src.sums[:, t:t + 1]).then_inc(exped, 1)

                def hi(q, t):
                    i = NT * q + t
                    act.wait_ge(exped, i + 1)
                    if reused(i, 4):
                        act.wait_ge(turned, i - 3)
                    nc.scalar.copy(ph[:, t % 4, :], pbuf[:, t % 4, :]).then_inc(hi_done, 1)

                def keep_keys(src, c, use):
                    act.wait_ge(misc_full, use + 1)
                    nc.scalar.copy((src.xl if c else src.xh)[:, :].bitcast(F32), misc[:, :]).then_inc(misc_free, 1)

                def queries_hi(src, half, use):
                    act.wait_ge(misc_full, use + 1)
                    nc.scalar.copy(src.y[:, half * HALF:(half + 1) * HALF], misc[:, :]).then_inc(y_hi, 1)

                def keep_zT(use):
                    act.wait_ge(misc_full, use + 1)
                    nc.scalar.copy(zT[:, :].bitcast(F32), misc[:, :]).then_inc(misc_free, 1)

                def bias(h, half, use):
                    act.wait_ge(misc_full, use + 1)
                    act.nop(nofuse=True)
                    nc.scalar.activation(cv[:, half, :], misc[:, :], ACT.Identity, bias=s.bh[:, bass.ds(h, 1)]).then_inc(misc_free, 1)

                def queries_out(use):
                    act.wait_ge(misc_free, use)
                    nc.scalar.copy(output.y[0:F, :], output.xh[0:F, :])
                    nc.scalar.copy(output.y[F:P, :], output.xl[F:P, :]).then_inc(y_out, 1)

                def body(q, src, nxt, extra):
                    for t in range(NT):
                        u, of, v = (q, src, t + 2) if t + 2 < NT else (q + 1, nxt, t + 2 - NT)
                        if of is not None:
                            expo(u, of, v)
                        if of is not None:
                            hi(u, v)
                        extra(t)

                def h2_first(b, use):
                    act.wait_ge(misc_full, use + 1)
                    nc.scalar.copy(output.xs[:, 0, :, :, :], misc[:, :].rearrange("p (t f) -> p t f", t=NT).unsqueeze(2).broadcast_to([P, NT, 2, F])
                                   ).then_inc(h2_hi, 1)

                def square(b):
                    act.wait_ge(n_centred, b + 1)
                    act.nop(nofuse=True)
                    nc.scalar.activation(zf[:, :, :], s.X[:, bass.ds(b * NT, NT), :], ACT.Square).then_inc(n_squared, 1)

                def root(first, last):
                    act.wait_ge(n_shift, last)
                    part = var_all[:, first * NT:last * NT]
                    nc.scalar.activation(part, part, ACT.Sqrt).then_inc(n_root, 1)

                class Steps:
                    def start(self):
                        keep_keys(head[0], 0, 0)
                        keep_keys(head[0], 1, 1)
                        queries_hi(head[0], 0, 2)
                        queries_hi(head[0], 1, 3)
                        for t in range(2):
                            expo(0, head[0], t)
                            hi(0, t)

                    def head_0(self, b, q, after_out):
                        use = use_base(b)

                        def extra(t):
                            if is_0(b) and t in (1, 2):
                                queries_hi(head[1], t - 1, use + 3 + t)
                            if not is_0(b) and t in (0, 1):
                                queries_hi(head[1], t, use + t)
                            if after_out and t == 5:
                                square(b - 2)
                            if not is_0(b) and t == 6:
                                h2_first(b - 1, use + 2)
                        body(q, head[0], head[1], extra)

                    def head_h(self, b, q, h, par):
                        use = use_head(b, h)

                        def extra(t):
                            if t in (1, 2):
                                queries_hi(head[1 - par], t - 1, use + t - 1)
                            if t == 3:
                                keep_zT(use + 2)
                            if t in (4, 5):
                                bias(h - 1, t - 4, use + t - 1)
                        body(q, head[par], head[1 - par], extra)

                    def head_7(self, b, q):
                        use = use_head(b, 7)
                        last = use if is_0(b) else use + 2

                        def extra(t):
                            if not is_0(b) and t in (0, 1):
                                keep_keys(output, t, use + t)
                            if not is_0(b) and t == 2:
                                queries_out(use + 2)
                            if t == 3:
                                keep_zT(last)
                            if t in (4, 5):
                                bias(6, t - 4, last + t - 3)
                        body(q, head[1], None if is_0(b) else output, extra)

                    def out(self, b, q, has_next):
                        use = use_switch(b)

                        def extra(t):
                            if has_next:
                                if t in (1, 2):
                                    keep_keys(head[0], t - 1, use + t - 1)
                                if t in (3, 4):
                                    queries_hi(head[0], t - 3, use + t - 1)
                            last = use + (4 if has_next else 0)
                            if t == (5 if has_next else 3):
                                keep_zT(last)
                            if t in (6, 7):
                                bias(7, t - 6, last + t - 5)
                        body(q, output, head[0] if has_next else None, extra)

                    def switch(self, b, q):
                        use = use_switch(b)
                        keep_keys(head[0], 0, use)
                        keep_keys(head[0], 1, use + 1)
                        queries_hi(head[0], 0, use + 2)
                        queries_hi(head[0], 1, use + 3)
                        keep_zT(use + 4)
                        bias(7, 0, use + 5)
                        bias(7, 1, use + 6)
                        for t in range(2):
                            expo(q, head[0], t)
                            hi(q, t)

                    def end(self, q):
                        h2_first(B - 1, USE_END)
                        square(B - 2)
                        keep_keys(output, 0, USE_END + 1)
                        keep_keys(output, 1, USE_END + 2)
                        queries_out(USE_END + 3)
                        root(0, B - 1)
                        for t in range(2):
                            expo(q, output, t)
                            hi(q, t)
                        body(q, output, None, lambda t: None)
                        square(B - 1)
                        root(B - 1, B)

                in_order(act, Steps())

            @block.vector
            def _(dve):
                def mask(q, t):
                    i = NT * q + t
                    dve.wait_ge(scored, i + 1)
                    if reused(i, 4):
                        dve.wait_ge(exped, i - 3)
                    dve.nop(nofuse=True)
                    nc.vector.tensor_tensor_reduce(tb[:, t % 4, :], ps_s[:, t % 2, :], s.offgraph[:, t, :], -1.0, BIG, ALU.add,
                                                   ALU.min, nm[:, t % 4:t % 4 + 1]).then_inc(masked, 1)

                def keep(q, t):
                    i = NT * q + t
                    dve.wait_ge(turned, i + 1)
                    if reused(i, 2):
                        dve.wait_ge(mixed, i - 1)
                    nc.vector.tensor_copy(phT[:, t % 2, :].bitcast(F32), ps_t[:, t % 2, :]).then_inc(kept, 1)

                def queries_lo(b, h, half, src):
                    dve.wait_ge(y_hi, 16 * b + 2 * h + half + 1)
                    lo = src.y[F:P, half * HALF:(half + 1) * HALF]
                    nc.vector.tensor_tensor(lo, misc[F:P, :], lo, ALU.subtract).then_inc(misc_free, 1)

                def split_x_hi(b):
                    rows = s.X[:, bass.ds(b * NT, NT), :]
                    nc.vector.tensor_copy(head[0].xs[:, 0, :, :, :], rows.unsqueeze(2).broadcast_to([P, NT, 2, F])).then_inc(x_hi, 1)

                def split_x_lo(b):
                    rows, xs = s.X[:, bass.ds(b * NT, NT), :], head[0].xs
                    dve.wait_ge(x_hi, b + 1)
                    for j in range(2):
                        last = nc.vector.tensor_tensor(xs[:, 1, :, j, :], rows, xs[:, 0, :, j, :], ALU.subtract)
                    last.then_inc(x_split, 1)

                def split_h2(b):
                    rows, xs = misc[:, :].rearrange("p (t f) -> p t f", t=NT), output.xs
                    dve.wait_ge(h2_hi, b + 1)
                    for j in range(2):
                        last = nc.vector.tensor_tensor(xs[:, 1, :, j, :], rows, xs[:, 0, :, j, :], ALU.subtract)
                    last.then_inc(misc_free, 1)

                def normalise(q, src):
                    dve.wait_ge(mixed, NT * q + NT)
                    nc.vector.reciprocal(rr[:, :], src.sums).then_inc(z_rec, 1)
                    dve.wait_ge(z_rec, q + 1)
                    nc.vector.tensor_tensor(zf[:, :, :], acc[:, :].rearrange("p (t f) -> p t f", t=NT),
                                            rr[:, :].unsqueeze(2).broadcast_to([P, NT, F]), ALU.mult).then_inc(z_ready, 1)

                def leak(n, h, half, use):
                    dve.wait_ge(misc_free, use + 1)
                    dve.wait_ge(cat_split, 2 * n + half + 1)
                    for to in (catf[:, half, :], cat_part(0, h, half)):
                        last = nc.vector.scalar_tensor_tensor(out=to, in0=cv[:, half, :], scalar=0.01, in1=cv[:, half, :],
                                                              op0=ALU.mult, op1=ALU.max)
                    last.then_inc(cat_ready, 1)

                def finish(b, q, part):
                    rows = s.X[:, bass.ds(b * NT, NT), :]
                    if part == 0:
                        normalise(q, output)
                    if part == 1:
                        dve.wait_ge(o_bias, b + 1)
                        nc.vector.scalar_tensor_tensor(out=zf[:, :, :], in0=ob[:, :, :], scalar=0.01, in1=ob[:, :, :], op0=ALU.mult,
                                                       op1=ALU.max).then_inc(o_leak, 1)
                    if part == 2:
                        dve.wait_ge(out_added, b + 1)
                        nc.vector.tensor_reduce(mean[:, :], ob[:, :, :], AX.X, ALU.add).then_inc(n_sum, 1)
                        dve.wait_ge(n_sum, b + 1)
                        nc.vector.tensor_scalar(mean[:, :], mean[:, :], 1.0 / F, None, ALU.mult).then_inc(n_mean, 1)
                    if part == 3:
                        dve.wait_ge(n_mean, b + 1)
                        nc.vector.tensor_tensor(rows, ob[:, :, :], mean[:, :].unsqueeze(2).broadcast_to([P, NT, F]), ALU.subtract).then_inc(n_centred, 1)
                    if part == 4:
                        dve.wait_ge(n_squared, b + 1)
                        nc.vector.tensor_reduce(var[:, :], zf[:, :, :], AX.X, ALU.add).then_inc(n_var, 1)
                        dve.wait_ge(n_var, b + 1)
                        nc.vector.tensor_scalar(var_all[:, bass.ds(b * NT, NT)], var[:, :], 1.0 / F, EPS, ALU.mult, ALU.add).then_inc(n_shift, 1)

                def invert(first, last):
                    part = var_all[:, first * NT:last * NT]
                    dve.wait_ge(n_root, last - B + 2)
                    nc.vector.reciprocal(part, part).then_inc(n_inverse, 1)
                    dve.wait_ge(n_inverse, last - B + 2)

                def scale(b):
                    rows = s.X[:, b * NT:(b + 1) * NT, :]
                    nc.vector.tensor_tensor(rows, rows, var_all[:, b * NT:(b + 1) * NT].unsqueeze(2).broadcast_to([P, NT, F]),
                                            ALU.mult).then_inc(normed, 1)

                def body(q, src, nxt, extra):
                    for t in range(NT):
                        keep(q, t)
                        if t + 3 < NT:
                            mask(q, t + 3)
                        elif nxt:
                            mask(q + 1, t + 3 - NT)
                        extra(t)

                class Steps:
                    def start(self):
                        split_x_hi(0)
                        split_x_lo(0)
                        queries_lo(0, 0, 0, head[0])
                        queries_lo(0, 0, 1, head[0])
                        for t in range(3):
                            mask(0, t)

                    def head_0(self, b, q, after_out):
                        use = use_base(b)

                        def extra(t):
                            if after_out and t in (0, 2, 4, 5, 6):
                                finish(b - 2, q - 1, (0, 2, 4, 5, 6).index(t))
                            if is_0(b) and t in (1, 2):
                                queries_lo(b, 1, t - 1, head[1])
                            if not is_0(b) and t in (0, 1):
                                queries_lo(b, 1, t, head[1])
                            if not is_0(b) and t == 7:
                                split_h2(b - 1)
                        body(q, head[0], True, extra)

                    def head_h(self, b, q, h, par):
                        use = use_head(b, h)

                        def extra(t):
                            if t == 0:
                                normalise(q - 1, head[1 - par])
                            if t in (1, 2):
                                queries_lo(b, h + 1, t - 1, head[1 - par])
                            if t in (5, 6):
                                leak(8 * b + h - 1, h - 1, t - 5, use + t - 2)
                        body(q, head[par], True, extra)

                    def head_7(self, b, q):
                        use = use_head(b, 7)

                        def extra(t):
                            if t == 0:
                                normalise(q - 1, head[0])
                            if t in (5, 6):
                                leak(8 * b + 6, 6, t - 5, use + (0 if is_0(b) else 2) + t - 4)
                        body(q, head[1], not is_0(b), extra)

                    def out(self, b, q, has_next):
                        use = use_switch(b)

                        def extra(t):
                            if t == 0:
                                normalise(q - 1, head[1])
                                if has_next:
                                    split_x_hi(b + 1)
                            if has_next and t == 1:
                                split_x_lo(b + 1)
                            if has_next and t in (3, 4):
                                queries_lo(b + 1, 0, t - 3, head[0])
                            if t in (6, 7):
                                leak(8 * b + 7, 7, t - 6, use + (4 if has_next else 0) + t - 5)
                        body(q, output, has_next, extra)

                    def switch(self, b, q):
                        use = use_switch(b)
                        normalise(q - 1, head[1])
                        split_x_hi(b + 1)
                        split_x_lo(b + 1)
                        queries_lo(b + 1, 0, 0, head[0])
                        queries_lo(b + 1, 0, 1, head[0])
                        for t in range(3):
                            mask(q, t)
                        leak(8 * b + 7, 7, 0, use + 5)
                        leak(8 * b + 7, 7, 1, use + 6)

                    def end(self, q):
                        for part in range(5):
                            finish(B - 2, q - 1, part)
                        split_h2(B - 1)
                        for t in range(3):
                            mask(q, t)

                        def extra(t):
                            if t == 1:
                                invert(0, B - 1)
                            if t > 0:
                                scale(t - 1)
                        body(q, output, False, extra)
                        for part in range(5):
                            finish(B - 1, q, part)
                        invert(B - 1, B)
                        scale(B - 1)

                in_order(dve, Steps())

            @block.gpsimd
            def _(pool):
                def lo(q, t):
                    i = NT * q + t
                    if reused(i, 4):
                        pool.wait_ge(lo_turned[t % 2], turns(q, t, 4))
                    pool.wait_ge(hi_done, i + 1)
                    nc.gpsimd.tensor_tensor(pl[:, t % 4, :], pbuf[:, t % 4, :], ph[:, t % 4, :], ALU.subtract).then_inc(lo_done, 1)

                def split_z(n, q):
                    pool.wait_ge(z_ready, q + 1)
                    pool.nop(nofuse=True)
                    nc.gpsimd.tensor_scalar(zs[:, :, 0, :], zf[:, :, :], 1.0, 0.0, ALU.mult, ALU.add).then_inc(z_hi, 1)
                    pool.wait_ge(z_hi, n + 1)
                    nc.gpsimd.tensor_tensor(zs[:, :, 1, :], zf[:, :, :], zs[:, :, 0, :], ALU.subtract).then_inc(z_split, 1)

                def finish(b, q, part):
                    if part == 0:
                        pool.wait_ge(z_ready, q + 1)
                        nc.gpsimd.tensor_tensor(ob[:, :, :], zf[:, :, :], s.bout[:, :].unsqueeze(1).broadcast_to([P, NT, F]), ALU.add).then_inc(o_bias, 1)
                    else:
                        pool.wait_ge(o_leak, b + 1)
                        nc.gpsimd.tensor_tensor(ob[:, :, :], s.X[:, bass.ds(b * NT, NT), :], zf[:, :, :], ALU.add).then_inc(out_added, 1)

                def split_cat(n, h, half):
                    pool.wait_ge(cat_ready, 2 * n + half + 1)
                    nc.gpsimd.tensor_tensor(cat_part(1, h, half), catf[:, half, :], cat_part(0, h, half), ALU.subtract).then_inc(cat_split, 1)

                def body(q, nxt, extra):
                    for t in range(NT):
                        if t + 2 < NT:
                            lo(q, t + 2)
                        elif nxt:
                            lo(q + 1, t + 2 - NT)
                        extra(t)

                class Steps:
                    def start(self):
                        pool.nop(nofuse=True).then_inc(cat_split, 2)
                        lo(0, 0)
                        lo(0, 1)

                    def head_0(self, b, q, after_out):
                        def extra(t):
                            if t == 0 and not is_0(b):
                                split_cat(8 * b - 1, 7, 1)
                            if t in (1, 3) and after_out:
                                finish(b - 2, q - 1, t // 2)
                        body(q, True, extra)

                    def head_h(self, b, q, h, par):
                        def extra(t):
                            if t == 1:
                                split_z(8 * b + h - 1, q - 1)
                            if t in (6, 7):
                                split_cat(8 * b + h - 1, h - 1, t - 6)
                        body(q, True, extra)

                    def head_7(self, b, q):
                        def extra(t):
                            if t == 1:
                                split_z(8 * b + 6, q - 1)
                            if t in (6, 7):
                                split_cat(8 * b + 6, 6, t - 6)
                        body(q, not is_0(b), extra)

                    def out(self, b, q, has_next):
                        def extra(t):
                            if t == 1:
                                split_z(8 * b + 7, q - 1)
                            if t == 7:
                                split_cat(8 * b + 7, 7, 0)
                        body(q, has_next, extra)

                    def switch(self, b, q):
                        split_z(8 * b + 7, q - 1)
                        lo(q, 0)
                        lo(q, 1)
                        split_cat(8 * b + 7, 7, 0)

                    def end(self, q):
                        split_cat(8 * B - 1, 7, 1)
                        finish(B - 2, q - 1, 0)
                        finish(B - 2, q - 1, 1)
                        lo(q, 0)
                        lo(q, 1)
                        body(q, False, lambda t: None)
                        finish(B - 1, q, 0)
                        finish(B - 1, q, 1)

                in_order(pool, Steps())


def build(nc, g, out):
    with ExitStack() as ctx:
        def sb(name, shape, dt=F32):
            return ctx.enter_context(nc.sbuf_tensor(name, shape, dt))

        s = Net()
        s.X = sb("x_all", [P, B * NT, F])
        s.meanT, s.wind = sb("neighbours_meanT", [P, B // 2, N]), sb("w_ind", [F, F])
        s.offgraph = sb("off_graph", [P, NT, N], BF16)
        s.ident, s.ident16, s.ones = sb("ident", [P, P]), sb("ident16", [P, P], F16), sb("ones", [P, F])
        s.twice, s.pick = sb("twice", [P, F]), sb("pick_edge", [P, K2, 2, F], F16)
        s.w2, s.fcw, s.fcb = sb("w_twice", [F, P]), sb("fcw", [F, P]), sb("fcb", [P, 1])
        s.anode, s.agn, s.age = sb("a_node", [F, E]), sb("a_gn", [F, P]), sb("a_ge", [F, 1])
        s.av, s.nav = sb("av", [P, P]), sb("minus_av", [P, F])
        s.off, s.offT = sb("off_edge", [P, NT, E]), sb("off_edgeT", [E, N])
        s.w_hi, s.w_lo = sb("w_hi", [P, HEADS, HID], F16), sb("w_lo", [P, HEADS, HID], F16)
        s.gram = sb("gram", [P, HEADS * P], F16)
        s.wout_hi, s.wout_lo = sb("wout_hi", [P, HEADS, F], F16), sb("wout_lo", [P, HEADS, F], F16)
        s.bh, s.bout = sb("bh", [P, HEADS]), sb("bout", [P, F])
        setup(nc, g, s)
        layer0(nc, s)
        norm(nc, s, "norm0")
        layer1(nc, s, out)


_INS = {"x": "x", "adj": "adj", "L0_gnn_H": "H", "L0_gnn_W": "W", "L0_gnn_W_ind": "W_ind", "L0_gnn_a_node": "a_node",
        "L0_gnn_a_gn": "a_gn", "L0_gnn_a_ge": "a_ge", "L0_gnn_fcW": "fcW", "L0_gnn_fcb": "fcb", "L0_gnn_av": "av",
        "L1_gnn_Wh": "Wh", "L1_gnn_bh": "bh", "L1_gnn_W_out": "W_out", "L1_gnn_b_out": "b_out"}


def kernel(**inputs):
    import numpy as _np
    import concourse.bacc as _bacc
    from concourse import mybir as _mybir
    from concourse.bass_utils import run_bass_kernel_spmd as _run

    nc = _bacc.Bacc("TRN2", target_bir_lowering=False, num_devices=1)
    arrays, g = {}, Net()
    for name, short in _INS.items():
        a = _np.ascontiguousarray(inputs[name])
        arrays[f"in_{name}"] = a
        g.__dict__[short] = nc.dram_tensor(f"in_{name}", a.shape, _mybir.dt.from_np(a.dtype), kind="ExternalInput").ap()
    out = nc.dram_tensor("out", (B, N, F), F32, kind="ExternalOutput").ap()
    build(nc, g, out)
    r = _run(nc, [arrays], core_ids=[0])
    return r.results[0]["out"]
```
